# Optimizing a Trainium2 kernel written in Bass

```python
import numpy as np
import jax
import jax.numpy as jnp

def _softmax(x, axis=-1):
    return jax.nn.softmax(x, axis=axis)

def _gelu(x):
    return jax.nn.gelu(x, approximate=True)

def _silu(x):
    return jax.nn.silu(x)

def _sigmoid(x):
    return jax.nn.sigmoid(x)

def _layernorm(x, axis=-1, eps=1e-05):
    m = jnp.mean(x, axis=axis, keepdims=True)
    v = jnp.var(x, axis=axis, keepdims=True)
    return (x - m) / jnp.sqrt(v + eps)

def _scatter_add(tgt, idx, src, axis=0):
    return tgt.at[idx].add(src)

def _segment_sum(src, seg, n):
    return jax.ops.segment_sum(src, seg, n)
kernel_name = 'mk_flamingo_gated_d2_seqx_r4_1e42c0'

def setup_inputs(seed: int=0):
    np.random.seed(seed)
    _w = jnp.asarray

    def _rec_inputs():
        import jax
        import jax.numpy as jnp
        _rk = jax.random.key(seed)
        x = 6.313e-05 + 0.9998 * jax.random.normal(jax.random.fold_in(_rk, 1), (8, 256, 256), jnp.float32)
        _lenS = 256 - jax.random.randint(jax.random.fold_in(_rk, 7), (8,), 0, max(1, 256 // 4) + 1, jnp.int32)
        _lenS2 = 77 - jax.random.randint(jax.random.fold_in(_rk, 8), (8,), 0, max(1, 77 // 4) + 1, jnp.int32)
        _ctx_1024P = jax.random.normal(jax.random.fold_in(_rk, 11), (8, 16, 256), jnp.float32)
        _ctx_1024c = jax.random.dirichlet(jax.random.fold_in(_rk, 511), 0.3 * jnp.ones((16,), jnp.float32), (8, 77))
        _ctx_1024t = jnp.einsum('bsk,bkd->bsd', _ctx_1024c, _ctx_1024P)
        _ctx_1024t = _ctx_1024t * jax.lax.rsqrt(jnp.mean(jnp.square(_ctx_1024t)) + 1e-12) * 0.953939
        ctx_1024 = -0.000214406 + 1.00034 * (_ctx_1024t + 0.3 * jax.random.normal(jax.random.fold_in(_rk, 611), (8, 77, 256), jnp.float32))
        _g = jax.random.normal(jax.random.fold_in(_rk, 9001), (2, 2), jnp.float32)
        _g = jnp.sign(_g) * jnp.maximum(jnp.abs(_g), 1.0) + (_g == 0) * 1.0
        g_xattn = _g[0]
        g_ffn = _g[1]
        return (x, ctx_1024, g_xattn, g_ffn)
    x, ctx_1024, g_xattn, g_ffn = _rec_inputs()

    def _L0_xattn_setup():
        import jax, jax.numpy as jnp
        import numpy as np
        from jax import lax
        BIG = jnp.float32(1e+30)

        def _pairwise_euclidean(a, b):
            aa = jnp.sum(a * a, axis=-1)[:, None]
            bb = jnp.sum(b * b, axis=-1)[None, :]
            ab = a @ b.T
            return jnp.sqrt(jnp.maximum(aa + bb - 2.0 * ab, 0.0))

        def _dtw_cost(D):
            row0 = jnp.cumsum(D[0])

            def row_step(prev_row, d_row):
                first = d_row[0] + prev_row[0]

                def col_step(left, inp):
                    d_ij, up, diag = inp
                    r = d_ij + jnp.minimum(jnp.minimum(up, left), diag)
                    return (r, r)
                _, rest = lax.scan(col_step, first, (d_row[1:], prev_row[1:], prev_row[:-1]))
                row = jnp.concatenate([first[None], rest])
                return (row, row)
            _, rows = lax.scan(row_step, row0, D[1:])
            return jnp.concatenate([row0[None], rows], axis=0)

        def _backtrack(R, T1, T2):
            L = T1 + T2 - 1

            def step(carry, _):
                i, j, done = carry
                valid = jnp.logical_not(done)
                cd = jnp.where((i > 0) & (j > 0), R[jnp.maximum(i - 1, 0), jnp.maximum(j - 1, 0)], BIG)
                cu = jnp.where(i > 0, R[jnp.maximum(i - 1, 0), j], BIG)
                cl = jnp.where(j > 0, R[i, jnp.maximum(j - 1, 0)], BIG)
                choice = jnp.argmin(jnp.stack([cd, cu, cl]))
                ni = jnp.where(choice <= 1, i - 1, i)
                nj = jnp.where((choice == 0) | (choice == 2), j - 1, j)
                at_origin = (i == 0) & (j == 0)
                ni = jnp.where(at_origin, 0, ni)
                nj = jnp.where(at_origin, 0, nj)
                return ((ni, nj, done | at_origin), (i, j, valid))
            init = (jnp.int32(T1 - 1), jnp.int32(T2 - 1), jnp.bool_(False))
            _, (i_idx, j_idx, valid) = lax.scan(step, init, None, length=L)
            return (i_idx, j_idx, valid)

        def _align_one(small, large):
            T_small, d = small.shape
            T_large = large.shape[0]
            D = _pairwise_euclidean(small, large)
            R = _dtw_cost(D)
            i_idx, j_idx, valid = _backtrack(R, T_small, T_large)
            contrib = small[i_idx] * valid[:, None].astype(small.dtype)
            expanded = jnp.zeros((T_large, d), dtype=small.dtype).at[j_idx].add(contrib)
            return expanded
        key = jax.random.key(seed)
        k1, k2 = jax.random.split(key)
        teacher = jax.random.normal(k1, (16, 100, 256), dtype=jnp.float32)
        student = jax.random.normal(k2, (16, 150, 256), dtype=jnp.float32)
        return {'teacher_features': teacher, 'student_features': student}
    _L0_xattn_all = _L0_xattn_setup()
    _L0_xattn_in = {k: v for k, v in _L0_xattn_all.items() if k in ()}
    del _L0_xattn_all

    def _L0_ffn_setup():
        import jax, jax.numpy as jnp
        import numpy as np
        LN_EPS = 1e-05

        def layernorm(x, g, b):
            mu = jnp.mean(x, axis=-1, keepdims=True)
            var = jnp.mean((x - mu) ** 2, axis=-1, keepdims=True)
            return (x - mu) * jax.lax.rsqrt(var + LN_EPS) * g + b

        def act_quant_fake(x):
            scale = 127.0 / jnp.clip(jnp.max(jnp.abs(x), axis=-1, keepdims=True), 1e-05)
            return jnp.clip(jnp.round(x * scale), -128.0, 127.0) / scale

        def weight_quant_fake(w):
            scale = 1.0 / jnp.clip(jnp.mean(jnp.abs(w)), 1e-05)
            return jnp.clip(jnp.round(w * scale), -1.0, 1.0) / scale

        def bitlinear(x, w, b):
            dqx = act_quant_fake(x)
            dqw = weight_quant_fake(w)
            return jnp.einsum('btd,hd->bth', dqx, dqw) + b
        key = jax.random.key(seed)
        ks = jax.random.split(key, 5)
        B, T, D, H = (8, 1024, 256, 1024)
        return {'x': jax.random.normal(ks[0], (B, T, D), dtype=jnp.float32), 'ln1_g': jnp.ones((D,), jnp.float32), 'ln1_b': jnp.zeros((D,), jnp.float32), 'w1': jax.random.normal(ks[1], (H, D), dtype=jnp.float32) * (1.0 / np.sqrt(D)), 'b1': jax.random.normal(ks[2], (H,), dtype=jnp.float32) * 0.02, 'ln2_g': jnp.ones((H,), jnp.float32), 'ln2_b': jnp.zeros((H,), jnp.float32), 'w2': jax.random.normal(ks[3], (D, H), dtype=jnp.float32) * (1.0 / np.sqrt(H)), 'b2': jax.random.normal(ks[4], (D,), jnp.float32) * 0.02}
    _L0_ffn_all = _L0_ffn_setup()
    _L0_ffn_in = {k: v for k, v in _L0_ffn_all.items() if k in ('ln1_g', 'ln1_b', 'w1', 'b1', 'ln2_g', 'ln2_b', 'w2', 'b2')}
    del _L0_ffn_all

    def _L1_xattn_setup():
        import jax, jax.numpy as jnp
        import numpy as np
        EPS = 1e-05

        def layernorm(x, g, b):
            mu = jnp.mean(x, axis=-1, keepdims=True)
            var = jnp.var(x, axis=-1, keepdims=True)
            return (x - mu) * jax.lax.rsqrt(var + EPS) * g + b
        DIM = 256
        CTX = 256
        HEADS = 12
        DHEAD = 64
        INNER = HEADS * DHEAD
        B = 4
        F = 512
        J = 256
        key = jax.random.key(seed)
        ks = jax.random.split(key, 8)
        s = lambda d: 1.0 / np.sqrt(d)
        return {'x': jax.random.normal(ks[0], (B, F, DIM), jnp.float32), 'tab_x': jax.random.normal(ks[1], (B, J, CTX), jnp.float32), 'tab_g': jnp.ones((CTX,), jnp.float32), 'tab_b': jnp.zeros((CTX,), jnp.float32), 'vid_g': jnp.ones((DIM,), jnp.float32), 'vid_b': jnp.zeros((DIM,), jnp.float32), 'Wq': jax.random.normal(ks[2], (DIM, INNER), jnp.float32) * s(DIM), 'Wk': jax.random.normal(ks[3], (CTX, INNER), jnp.float32) * s(CTX), 'Wv': jax.random.normal(ks[4], (CTX, INNER), jnp.float32) * s(CTX), 'q_g': jnp.ones((INNER,), jnp.float32), 'q_b': jnp.zeros((INNER,), jnp.float32), 'k_g': jnp.ones((INNER,), jnp.float32), 'k_b': jnp.zeros((INNER,), jnp.float32), 'Wo': jax.random.normal(ks[5], (INNER, DIM), jnp.float32) * s(INNER), 'bo': jnp.zeros((DIM,), jnp.float32)}
    _L1_xattn_all = _L1_xattn_setup()
    _L1_xattn_in = {k: v for k, v in _L1_xattn_all.items() if k in ('tab_g', 'tab_b', 'vid_g', 'vid_b', 'Wq', 'Wk', 'Wv', 'q_g', 'q_b', 'k_g', 'k_b', 'Wo', 'bo')}
    del _L1_xattn_all

    def _L1_ffn_setup():
        import jax, jax.numpy as jnp
        import numpy as np
        N_EMBD = 256
        N_EXPERTS = 8
        TOP_K = 2
        B, T = (4, 512)
        key = jax.random.key(seed)
        ks = jax.random.split(key, 8)
        C, E, H = (N_EMBD, N_EXPERTS, 4 * N_EMBD)
        s_in = 1.0 / np.sqrt(C)
        s_hid = 1.0 / np.sqrt(H)
        x = jax.random.normal(ks[0], (B, T, C), dtype=jnp.float32)
        W1 = jax.random.uniform(ks[1], (E, C, H), minval=-s_in, maxval=s_in, dtype=jnp.float32)
        b1 = jax.random.uniform(ks[2], (E, H), minval=-s_in, maxval=s_in, dtype=jnp.float32)
        W2 = jax.random.uniform(ks[3], (E, H, C), minval=-s_hid, maxval=s_hid, dtype=jnp.float32)
        b2 = jax.random.uniform(ks[4], (E, C), minval=-s_hid, maxval=s_hid, dtype=jnp.float32)
        Wg = jax.random.uniform(ks[5], (C, E), minval=-s_in, maxval=s_in, dtype=jnp.float32)
        bg = jax.random.uniform(ks[6], (E,), minval=-s_in, maxval=s_in, dtype=jnp.float32)
        return {'x': x, 'W1': W1, 'b1': b1, 'W2': W2, 'b2': b2, 'Wg': Wg, 'bg': bg}
    _L1_ffn_all = _L1_ffn_setup()
    _L1_ffn_in = {k: v for k, v in _L1_ffn_all.items() if k in ('W1', 'b1', 'W2', 'b2', 'Wg', 'bg')}
    del _L1_ffn_all
    return {'x': x, 'ctx_1024': ctx_1024, 'g_xattn': g_xattn, 'g_ffn': g_ffn, 'L0_ffn_ln1_g': _L0_ffn_in['ln1_g'], 'L0_ffn_ln1_b': _L0_ffn_in['ln1_b'], 'L0_ffn_w1': _L0_ffn_in['w1'], 'L0_ffn_b1': _L0_ffn_in['b1'], 'L0_ffn_ln2_g': _L0_ffn_in['ln2_g'], 'L0_ffn_ln2_b': _L0_ffn_in['ln2_b'], 'L0_ffn_w2': _L0_ffn_in['w2'], 'L0_ffn_b2': _L0_ffn_in['b2'], 'L1_xattn_tab_g': _L1_xattn_in['tab_g'], 'L1_xattn_tab_b': _L1_xattn_in['tab_b'], 'L1_xattn_vid_g': _L1_xattn_in['vid_g'], 'L1_xattn_vid_b': _L1_xattn_in['vid_b'], 'L1_xattn_Wq': _L1_xattn_in['Wq'], 'L1_xattn_Wk': _L1_xattn_in['Wk'], 'L1_xattn_Wv': _L1_xattn_in['Wv'], 'L1_xattn_q_g': _L1_xattn_in['q_g'], 'L1_xattn_q_b': _L1_xattn_in['q_b'], 'L1_xattn_k_g': _L1_xattn_in['k_g'], 'L1_xattn_k_b': _L1_xattn_in['k_b'], 'L1_xattn_Wo': _L1_xattn_in['Wo'], 'L1_xattn_bo': _L1_xattn_in['bo'], 'L1_ffn_W1': _L1_ffn_in['W1'], 'L1_ffn_b1': _L1_ffn_in['b1'], 'L1_ffn_W2': _L1_ffn_in['W2'], 'L1_ffn_b2': _L1_ffn_in['b2'], 'L1_ffn_Wg': _L1_ffn_in['Wg'], 'L1_ffn_bg': _L1_ffn_in['bg']}

def reference(x, ctx_1024, g_xattn, g_ffn, L0_ffn_ln1_g, L0_ffn_ln1_b, L0_ffn_w1, L0_ffn_b1, L0_ffn_ln2_g, L0_ffn_ln2_b, L0_ffn_w2, L0_ffn_b2, L1_xattn_tab_g, L1_xattn_tab_b, L1_xattn_vid_g, L1_xattn_vid_b, L1_xattn_Wq, L1_xattn_Wk, L1_xattn_Wv, L1_xattn_q_g, L1_xattn_q_b, L1_xattn_k_g, L1_xattn_k_b, L1_xattn_Wo, L1_xattn_bo, L1_ffn_W1, L1_ffn_b1, L1_ffn_W2, L1_ffn_b2, L1_ffn_Wg, L1_ffn_bg):
    import jax
    import jax.numpy as jnp

    def _L0_xattn_ref(teacher_features, student_features):
        import jax, jax.numpy as jnp
        import numpy as np
        from jax import lax
        BIG = jnp.float32(1e+30)

        def _pairwise_euclidean(a, b):
            aa = jnp.sum(a * a, axis=-1)[:, None]
            bb = jnp.sum(b * b, axis=-1)[None, :]
            ab = a @ b.T
            return jnp.sqrt(jnp.maximum(aa + bb - 2.0 * ab, 0.0))

        def _dtw_cost(D):
            row0 = jnp.cumsum(D[0])

            def row_step(prev_row, d_row):
                first = d_row[0] + prev_row[0]

                def col_step(left, inp):
                    d_ij, up, diag = inp
                    r = d_ij + jnp.minimum(jnp.minimum(up, left), diag)
                    return (r, r)
                _, rest = lax.scan(col_step, first, (d_row[1:], prev_row[1:], prev_row[:-1]))
                row = jnp.concatenate([first[None], rest])
                return (row, row)
            _, rows = lax.scan(row_step, row0, D[1:])
            return jnp.concatenate([row0[None], rows], axis=0)

        def _backtrack(R, T1, T2):
            L = T1 + T2 - 1

            def step(carry, _):
                i, j, done = carry
                valid = jnp.logical_not(done)
                cd = jnp.where((i > 0) & (j > 0), R[jnp.maximum(i - 1, 0), jnp.maximum(j - 1, 0)], BIG)
                cu = jnp.where(i > 0, R[jnp.maximum(i - 1, 0), j], BIG)
                cl = jnp.where(j > 0, R[i, jnp.maximum(j - 1, 0)], BIG)
                choice = jnp.argmin(jnp.stack([cd, cu, cl]))
                ni = jnp.where(choice <= 1, i - 1, i)
                nj = jnp.where((choice == 0) | (choice == 2), j - 1, j)
                at_origin = (i == 0) & (j == 0)
                ni = jnp.where(at_origin, 0, ni)
                nj = jnp.where(at_origin, 0, nj)
                return ((ni, nj, done | at_origin), (i, j, valid))
            init = (jnp.int32(T1 - 1), jnp.int32(T2 - 1), jnp.bool_(False))
            _, (i_idx, j_idx, valid) = lax.scan(step, init, None, length=L)
            return (i_idx, j_idx, valid)

        def _align_one(small, large):
            T_small, d = small.shape
            T_large = large.shape[0]
            D = _pairwise_euclidean(small, large)
            R = _dtw_cost(D)
            i_idx, j_idx, valid = _backtrack(R, T_small, T_large)
            contrib = small[i_idx] * valid[:, None].astype(small.dtype)
            expanded = jnp.zeros((T_large, d), dtype=small.dtype).at[j_idx].add(contrib)
            return expanded
        return jax.vmap(_align_one)(teacher_features, student_features)

    def _L0_ffn_ref(x, ln1_g, ln1_b, w1, b1, ln2_g, ln2_b, w2, b2):
        import jax, jax.numpy as jnp
        import numpy as np
        LN_EPS = 1e-05

        def layernorm(x, g, b):
            mu = jnp.mean(x, axis=-1, keepdims=True)
            var = jnp.mean((x - mu) ** 2, axis=-1, keepdims=True)
            return (x - mu) * jax.lax.rsqrt(var + LN_EPS) * g + b

        def act_quant_fake(x):
            scale = 127.0 / jnp.clip(jnp.max(jnp.abs(x), axis=-1, keepdims=True), 1e-05)
            return jnp.clip(jnp.round(x * scale), -128.0, 127.0) / scale

        def weight_quant_fake(w):
            scale = 1.0 / jnp.clip(jnp.mean(jnp.abs(w)), 1e-05)
            return jnp.clip(jnp.round(w * scale), -1.0, 1.0) / scale

        def bitlinear(x, w, b):
            dqx = act_quant_fake(x)
            dqw = weight_quant_fake(w)
            return jnp.einsum('btd,hd->bth', dqx, dqw) + b
        h = layernorm(x, ln1_g, ln1_b)
        h = bitlinear(h, w1, b1)
        h = jax.nn.gelu(h, approximate=False)
        h = layernorm(h, ln2_g, ln2_b)
        h = bitlinear(h, w2, b2)
        return h

    def _L1_xattn_ref(x, tab_x, tab_g, tab_b, vid_g, vid_b, Wq, Wk, Wv, q_g, q_b, k_g, k_b, Wo, bo):
        import jax, jax.numpy as jnp
        import numpy as np
        EPS = 1e-05

        def layernorm(x, g, b):
            mu = jnp.mean(x, axis=-1, keepdims=True)
            var = jnp.var(x, axis=-1, keepdims=True)
            return (x - mu) * jax.lax.rsqrt(var + EPS) * g + b
        DIM = 256
        CTX = 256
        HEADS = 12
        DHEAD = 64
        INNER = HEADS * DHEAD
        B = 4
        F = 512
        J = 256
        scale = DHEAD ** (-0.5)
        kv_in = layernorm(tab_x, tab_g, tab_b)
        q = layernorm(layernorm(x, vid_g, vid_b) @ Wq, q_g, q_b)
        k = layernorm(kv_in @ Wk, k_g, k_b)
        v = kv_in @ Wv
        split = lambda t: t.reshape(t.shape[0], t.shape[1], HEADS, DHEAD).transpose(0, 2, 1, 3)
        q, k, v = (split(q) * scale, split(k), split(v))
        sim = jnp.einsum('bhid,bhjd->bhij', q, k)
        attn = jax.nn.softmax(sim, axis=-1)
        out = jnp.einsum('bhij,bhjd->bhid', attn, v)
        out = out.transpose(0, 2, 1, 3).reshape(x.shape[0], x.shape[1], INNER)
        return out @ Wo + bo

    def _L1_ffn_ref(x, W1, b1, W2, b2, Wg, bg):
        import jax, jax.numpy as jnp
        import numpy as np
        N_EMBD = 256
        N_EXPERTS = 8
        TOP_K = 2
        B, T = (4, 512)
        gate_scores = jax.nn.softmax(jnp.einsum('btc,ce->bte', x, Wg) + bg, axis=-1)
        h = jax.nn.relu(jnp.einsum('btc,ech->bteh', x, W1) + b1)
        expert_out = jnp.einsum('bteh,ehc->btec', h, W2) + b2
        topk_scores, topk_idx = jax.lax.top_k(gate_scores, TOP_K)
        top_probs = jax.nn.softmax(topk_scores, axis=-1)
        sel = jnp.take_along_axis(expert_out, topk_idx[..., None], axis=2)
        out = jnp.sum(sel * top_probs[..., None], axis=2)
        return out
    x = x + jnp.tanh(g_xattn[0]) * _L0_xattn_ref(ctx_1024, _layernorm(x, axis=-1))
    x = x + jnp.tanh(g_ffn[0]) * _L0_ffn_ref(_layernorm(x, axis=-1), L0_ffn_ln1_g, L0_ffn_ln1_b, L0_ffn_w1, L0_ffn_b1, L0_ffn_ln2_g, L0_ffn_ln2_b, L0_ffn_w2, L0_ffn_b2)
    x = x + jnp.tanh(g_xattn[1]) * _L1_xattn_ref(_layernorm(x, axis=-1), ctx_1024, L1_xattn_tab_g, L1_xattn_tab_b, L1_xattn_vid_g, L1_xattn_vid_b, L1_xattn_Wq, L1_xattn_Wk, L1_xattn_Wv, L1_xattn_q_g, L1_xattn_q_b, L1_xattn_k_g, L1_xattn_k_b, L1_xattn_Wo, L1_xattn_bo)
    x = x + jnp.tanh(g_ffn[1]) * _L1_ffn_ref(_layernorm(x, axis=-1), L1_ffn_W1, L1_ffn_b1, L1_ffn_W2, L1_ffn_b2, L1_ffn_Wg, L1_ffn_bg)
    return x

_drawn_inputs = setup_inputs


def setup_inputs(seed=0):
    import zlib

    import numpy as np

    out = dict(_drawn_inputs(seed))
    spreads = {'g_ffn': (-1.0, 0.6),
     'L0_ffn_ln1_g': (1.0, 0.2),
     'L0_ffn_ln1_b': (0.0, 0.1),
     'L0_ffn_ln2_g': (1.0, 0.2),
     'L0_ffn_ln2_b': (0.0, 0.1),
     'L1_xattn_tab_g': (1.0, 0.2),
     'L1_xattn_tab_b': (0.0, 0.1),
     'L1_xattn_vid_g': (1.0, 0.2),
     'L1_xattn_vid_b': (0.0, 0.361),
     'L1_xattn_q_g': (1.0, 0.2),
     'L1_xattn_q_b': (0.0, 0.407),
     'L1_xattn_k_g': (1.0, 0.2),
     'L1_xattn_k_b': (0.0, 0.8),
     'L1_xattn_bo': (0.0, 0.1)}
    factors = {'L0_ffn_b1': 3.162, 'L0_ffn_b2': 4.299, 'L1_ffn_b1': 8.0, 'L1_ffn_b2': 7.744}
    for name, (base, spread) in spreads.items():
        noise = np.random.default_rng([zlib.crc32(name.encode()), seed]).standard_normal(out[name].shape)
        drawn = base * np.exp(spread * noise) if base else spread * noise
        out[name] = jnp.asarray(drawn.astype(out[name].dtype))
    for name, factor in factors.items():
        out[name] = (out[name] * factor).astype(out[name].dtype)
    return out
```

```python
from contextlib import ExitStack

import concourse.bass as bass
from concourse import mybir

F32, F16, BF16 = mybir.dt.float32, mybir.dt.float16, mybir.dt.bfloat16
I32, U32 = mybir.dt.int32, mybir.dt.uint32
ALU = mybir.AluOpType
ACT = mybir.ActivationFunctionType
AX = mybir.AxisListType

P = 128
B, TQ, D = 8, 256, 256
S = 77
TILES = B * TQ // P
KD = D // P
HID = 1024
HT = HID // P
HEADS, DH = 12, 64
INNER = HEADS * DH
PAIRS = INNER // P
NE = 8
LN_EPS = 1e-5
BIG = 1e30
MAGIC = 12582912.0

CH, LAG = 4, 2
CW = TQ // CH
PADR = LAG * (CH - 1)
RING = 12
STEPS = -(-(S + PADR) // RING) * RING
DROWS = PADR + STEPS + (STEPS - S) % 2
GROUP = 4

SLOTS = (2 * B * TQ - NE) // P + NE


class Memory:
    pass


class Region:

    def __init__(self, tensor):
        self.tensor, self.at = tensor, 0

    def take(self, parts, cols, dtype=F32, at=None):
        if at is not None:
            self.at = at
        words = cols if dtype in (F32, I32, U32) else cols // 2
        view = self.tensor[0:parts, self.at:self.at + words]
        self.at += words
        assert self.at <= self.tensor.shape[1], self.at
        return view if dtype == F32 else view.bitcast(dtype)


def bcast(vector, parts):
    return vector.rearrange("(o n) -> o n", o=1).broadcast_to([parts, vector.shape[0]])


def allocate(nc, ctx, m):
    def region(name, cols):
        return Region(ctx.enter_context(nc.sbuf_tensor(name, [P, cols], F32)))

    psum = ctx.enter_context(nc.psum_tensor("banks", [P, 8, 512], F32))
    m.bank = lambda k, n=1: psum[:, k:k + n, :]
    keep = region("keep", 4096 + 2048 + 256 + 2048 + 128 + 256 + 128)
    m.x = keep.take(P, TILES * D).rearrange("p (t d) -> p t d", t=TILES)
    m.ctx = keep.take(S, B * D).rearrange("p (b d) -> p b d", b=B)
    m.w1T = keep.take(P, KD * HID, BF16).rearrange("p (k h) -> p k h", k=KD)
    m.w2T = keep.take(P, HT * D, BF16).rearrange("p (k d) -> p k d", k=HT)
    m.spare = Region(keep.tensor)
    m.spare.at = TILES * D
    m.ident = keep.take(P, P)
    m.identb = keep.take(P, P, BF16)
    m.iota = keep.take(P, TQ)
    m.tanh = keep.take(P, 4)
    m.wscale = keep.take(P, 4)
    m.power = keep.take(P, 32)
    m.power1 = keep.take(P, 2)
    m.vT = keep.take(S, 2 * B).rearrange("p (k b) -> p k b", k=2)
    m.early = region("early", NE * KD * HID)
    m.late = region("late", NE * HT * D)
    m.arena = region("arena", 11000)
    m.kT = m.late.take(P, PAIRS * B * S, at=0).rearrange("p (i b s) -> p i b s", i=PAIRS, b=B)
    m.v = m.late.take(S, B * HEADS * (DH + 1)).rearrange("p (b h e) -> p b h e", b=B, h=HEADS)
    m.wa = m.late.take(P, KD * INNER)
    m.wb = m.late.take(P, KD * INNER)
    m.qg = m.late.take(P, INNER)
    m.qb = m.late.take(P, INNER)
    m.vg = m.late.take(P, D)
    m.vb = m.late.take(P, D)
    m.bo = m.late.take(P, D)


def align(nc, ctx, m, a):
    def sem(name):
        return nc.alloc_semaphore(name)

    dist_dram = nc.dram_tensor("dist_dram", [B, DROWS, TQ], F32, kind="Internal").ap()
    cost_dram = nc.dram_tensor("cost_dram", [CH * B, STEPS, CW], F32, kind="Internal").ap()
    jump_dram = nc.dram_tensor("jump_dram", [B, S, TQ], F16, kind="Internal").ap()

    early, arena = m.early, m.arena
    dist = early.take(CH * B, STEPS * CW, at=0).rearrange("p (t w) -> p t w", t=STEPS)
    xn = early.take(P, TILES * D, at=5376).rearrange("p (t d) -> p t d", t=TILES)
    drow = early.take(S, B * TQ).rearrange("p (b j) -> p b j", b=B)
    xnT = early.take(P, 2 * KD * TQ).rearrange("p (u k j) -> p u k j", u=2, k=KD)
    xsq = early.take(P, 2 * KD * TQ).rearrange("p (u k j) -> p u k j", u=2, k=KD)
    sq = early.take(S, 3 * TQ).rearrange("p (n j) -> p n j", n=3)
    sqjunk = early.take(S, D)
    W1 = TQ + 1
    cost = early.take(S, B * W1, at=0).rearrange("p (b j) -> p b j", b=B)
    above = early.take(S, B * W1).rearrange("p (b j) -> p b j", b=B)
    best = early.take(S, B * TQ).rearrange("p (b j) -> p b j", b=B)
    stay = early.take(S, B * TQ).rearrange("p (b j) -> p b j", b=B)
    turn = early.take(S, B * TQ).rearrange("p (b j) -> p b j", b=B)
    jump = early.take(S, B * TQ).rearrange("p (b j) -> p b j", b=B)
    djump = early.take(S, B * TQ, F16).rearrange("p (b j) -> p b j", b=B)
    djump_b = early.take(B, S * TQ, F16, at=0).rearrange("p (i j) -> p i j", i=S)

    w1s = arena.take(P, HT * D, at=0).rearrange("p (k d) -> p k d", k=HT)
    w2s = arena.take(P, KD * HID).rearrange("p (k h) -> p k h", k=KD)
    wq = arena.take(P, HT * D, BF16)
    ones = arena.take(P, P)
    kvn = arena.take(S, B * D).rearrange("p (b d) -> p b d", b=B)
    kvT = arena.take(P, KD * S).rearrange("p (k s) -> p k s", k=KD)
    kraw = arena.take(S, INNER)
    kn = arena.take(S, INNER)
    ring = arena.take(CH * B, RING * (CW + 1)).rearrange("p (r w) -> p r w", r=RING)
    diag = arena.take(CH * B, CW)
    first = arena.take(CH * B, 1)
    floor = arena.take(CH * B, 1)
    shifted = arena.take(CH * B, 2)
    path = arena.take(B, S + 1)
    ctxT = arena.take(P, KD * S).rearrange("p (k s) -> p k s", k=KD)
    junk = arena.take(P, 4)
    stats = arena.take(P, TILES * 6).rearrange("p (t n) -> p t n", t=TILES)
    mv = arena.take(P, TILES * 2).rearrange("p (t n) -> p t n", t=TILES)
    rstd = arena.take(P, TILES)
    cstats = arena.take(S, B * 6).rearrange("p (t n) -> p t n", t=B)
    cmv = arena.take(S, B * 2).rearrange("p (t n) -> p t n", t=B)
    crstd = arena.take(S, B)
    norm2 = arena.take(S, B)
    ksum = arena.take(S, 5 * B).rearrange("p (n b) -> p n b", n=5)
    wsum = arena.take(P, 2)
    big = arena.take(B, 2 * TQ)

    wk = m.wa.rearrange("p (k n) -> p k n", k=KD)
    wv = m.wb.rearrange("p (k n) -> p k n", k=KD)

    hopjunk = early.take(B, TQ, at=14000)
    NPAD = PADR // 2 + -(-(DROWS - PADR - S) // 2)

    s_x = [sem(f"ld_x{q}") for q in range(4)]
    s_cost = [sem(f"st_cost{g}") for g in range(RING // GROUP)]
    s_ctx, s_gate, s_w12, s_kv, s_kvg = map(sem, "ld_ctx ld_gate ld_w12 ld_kvw ld_kvg".split())
    s_id0, s_const, s_init = map(sem, "ident0 const dtw_init".split())
    s_cst, s_cmv, s_cr, s_st, s_mv, s_r = map(sem, "cstats cmv crstd stats mv rstd".split())
    s_v1, s_v2 = map(sem, "var_eps cvar_eps".split())
    s_xn, s_kvn, s_xT, s_xTc, s_xsq, s_cT, s_cTc, s_aa = map(sem, "xn kvn xT xTcopy xsq cT cTcopy norm2".split())
    s_D, s_a, s_sq, s_rc, s_ar, s_dr = map(sem, "distp dist2 sqrt recip quot drow".split())
    s_pad, s_dst, s_dist = map(sem, "st_pad st_dist ld_dist".split())
    s_min, s_scan, s_shf, s_bnd = map(sem, "dtw_min dtw_scan dtw_shift dtw_left".split())
    s_cl, s_cm, s_F, s_djst, s_djld, s_hop, s_path, s_vT, s_vTc = map(
        sem, "ld_cost cost_big choose st_jump ld_jump hop path0 vT vTcopy".split())
    s_ab, s_tot, s_ws, s_wq, s_wqb, s_wT, s_wTc = map(sem, "wabs wtotal wscale wq wqb wT wTcopy".split())
    s_kg, s_kvb, s_kvTp, s_kvTc, s_k, s_ksum, s_knm, s_kssq, s_kvar, s_krs, s_kbias, s_kn, s_kga, s_kb, s_kTp, s_kTc = map(
        sem, "kvgain kvbias kvT kvTcopy k ksum kmean kssq kvar krstd kbias knorm kgain kaff kTp kTcopy".split())
    s_v, s_vc, s_one, s_th, s_pw = map(sem, "v vcopy vones tanh power".split())

    x_t = a["x"].rearrange("b (h p) d -> p (b h) d", p=P)

    with nc.Block() as block:
        @block.sync
        def _(sp):
            sp.dma_start(m.ctx, a["ctx_1024"].rearrange("b s d -> s b d")).then_inc(s_ctx, 16)
            for q in range(4):
                sp.dma_start(m.x[:, 4 * q:4 * q + 4, :], x_t[:, 4 * q:4 * q + 4, :]).then_inc(s_x[q], 16)
            sp.wait_ge(s_init, 1)
            for r in list(range(0, PADR, 2)):
                sp.dma_start(dist_dram[:, r:r + 2, :], big.rearrange("p (r j) -> p r j", r=2)).then_inc(s_pad, 16)
            for r in range(PADR + S, DROWS, 2):
                r = min(r, DROWS - 2)
                sp.dma_start(dist_dram[:, r:r + 2, :], big.rearrange("p (r j) -> p r j", r=2)).then_inc(s_pad, 16)
            for b in range(B):
                sp.wait_ge(s_dr, b + 1)
                sp.dma_start(dist_dram[b, PADR:PADR + S, :], drow[:, b, :]).then_inc(s_dst, 16)
            sp.wait_ge(s_pad, 16 * NPAD)
            sp.wait_ge(s_dst, 16 * B)
            sp.wait_ge(s_xn, TILES)
            for c in range(CH):
                r = PADR - LAG * c
                sp.dma_start(dist[c * B:(c + 1) * B, :, :],
                             dist_dram[:, r:r + STEPS, c * CW:(c + 1) * CW]).then_inc(s_dist, 16)
            with sp.Fori(0, STEPS // RING) as i:
                for g in range(RING // GROUP):
                    sp.wait_ge(s_scan, i * RING + (g + 1) * GROUP)
                    sp.dma_start(cost_dram[:, bass.ds(i * RING + g * GROUP, GROUP), :],
                                 ring[:, g * GROUP:(g + 1) * GROUP, 1:CW + 1]).then_inc(s_cost[g], 16)
            for g in range(RING // GROUP):
                sp.wait_ge(s_cost[g], 16 * STEPS // RING)
            cost_v = cost_dram.rearrange("(c b) t w -> c t b w", c=CH)
            for c in range(CH):
                lo = 1 + c * CW
                sp.dma_start(cost[:, :, lo:lo + CW], cost_v[c, LAG * c:LAG * c + S]).then_inc(s_cl, 16)
                sp.dma_start(above[1:S, :, lo:lo + CW], cost_v[c, LAG * c:LAG * c + S - 1]).then_inc(s_cl, 16)
            sp.wait_ge(s_F, 7)
            sp.dma_start(jump_dram.rearrange("b i j -> i b j"), djump).then_inc(s_djst, 16)
            sp.wait_ge(s_djst, 16)
            sp.dma_start(djump_b, jump_dram).then_inc(s_djld, 16)

        @block.gpsimd
        def _(pool):
            pool.memset(m.power, -0.5).then_inc(s_pw, 1)
            pool.memset(m.power1, -1.0).then_inc(s_pw, 1)
            pool.memset(m.ident, 0.0).then_inc(s_id0, 1)
            pool.memset(ones, 1.0).then_inc(s_const, 1)
            pool.wait_ge(s_id0, 1)
            pool.affine_select(out=m.ident, in_=m.ident, compare_op=ALU.not_equal, fill=1.0, base=0,
                               pattern=[[-1, P]], channel_multiplier=1).then_inc(s_const, 1)
            pool.iota(m.iota, [[1, TQ]], base=0, channel_multiplier=0,
                      allow_small_or_imprecise_dtypes=True).then_inc(s_const, 1)
            pool.wait_ge(s_const, 3)
            pool.tensor_copy(m.identb, m.ident).then_inc(s_const, 1)
            pool.memset(big, BIG).then_inc(s_init, 1)
            pool.wait_ge(s_pw, 2)
            pool.wait_ge(s_cmv, B)
            pool.tensor_scalar(crstd, cmv[:, :, 1], LN_EPS, None, ALU.add).then_inc(s_v2, 1)
            pool.wait_ge(s_v2, 1)
            pool.tensor_tensor(crstd, crstd, m.power[0:S, 0:B], ALU.pow).then_inc(s_cr, 1)
            for q in range(4):
                t = slice(4 * q, 4 * q + 4)
                pool.wait_ge(s_mv, 4 * q + 4)
                pool.tensor_scalar(rstd[:, t], mv[:, t, 1], LN_EPS, None, ALU.add).then_inc(s_v1, 1)
                pool.wait_ge(s_v1, q + 1)
                pool.tensor_tensor(rstd[:, t], rstd[:, t], m.power[:, 0:4], ALU.pow).then_inc(s_r, 1)
            pool.memset(ring, BIG).then_inc(s_init, 1)
            pool.memset(first, BIG).then_inc(s_init, 1)
            pool.memset(floor, 0.0).then_inc(s_init, 1)
            pool.wait_ge(s_init, 4)
            pool.memset(first[0:B], 0.0).then_inc(s_init, 1)
            pool.memset(floor[0:B], BIG).then_inc(s_init, 1)
            pool.memset(path, float(TQ - 1)).then_inc(s_path, 1)
            pool.wait_ge(s_path, 1)
            pool.memset(path[:, 0:1], 0.0).then_inc(s_hop, 1)
            pool.memset(m.v, 1.0).then_inc(s_one, 1)
            pool.wait_ge(s_kvn, B)
            pool.wait_ge(s_kvg, 64)
            for b in range(B):
                pool.tensor_tensor(kvn[:, b, :], kvn[:, b, :], m.vg[0:S, :], ALU.mult).then_inc(s_kg, 1)
                pool.wait_ge(s_kg, b + 1)
                pool.tensor_tensor(kvn[:, b, :], kvn[:, b, :], m.vb[0:S, :], ALU.add).then_inc(s_kvb, 1)
            pool.wait_ge(s_tot, 1)
            pool.tensor_scalar(m.wscale[:, 0:2], wsum, 1.0 / (HID * D), 1e-5, ALU.mult, ALU.max).then_inc(s_ws, 1)
            pool.wait_ge(s_ws, 1)
            pool.tensor_tensor(m.wscale[:, 2:4], m.wscale[:, 0:2], m.power1, ALU.pow).then_inc(s_ws, 1)
            pool.wait_ge(s_ws, 2)
            for n, w in enumerate((w1s.rearrange("p k d -> p (k d)"), w2s.rearrange("p k h -> p (k h)"))):
                pool.tensor_scalar(w, w, m.wscale[:, 2 + n:3 + n], MAGIC, ALU.mult, ALU.add).then_inc(s_wq, 1)
                pool.wait_ge(s_wq, 2 * n + 1)
                pool.tensor_scalar(w, w, MAGIC, 1.0, ALU.subtract, ALU.min).then_inc(s_wq, 1)
                pool.wait_ge(s_wq, 2 * n + 2)
                if n:
                    pool.wait_ge(s_wT, 3)
                pool.tensor_scalar(wq, w, -1.0, None, ALU.max).then_inc(s_wqb, 1)
            for b in range(B):
                tot, mean, ssq, rs, bias = (ksum[:, n, b:b + 1] for n in range(5))
                pool.wait_ge(s_ksum, b + 1)
                pool.tensor_scalar(mean, tot, -1.0 / INNER, None, ALU.mult).then_inc(s_knm, 1)
                pool.wait_ge(s_kssq, b + 1)
                pool.tensor_scalar(rs, ssq, 1.0 / INNER, LN_EPS, ALU.mult, ALU.add).then_inc(s_kvar, 1)
                pool.wait_ge(s_kvar, b + 1)
                pool.tensor_tensor(rs, rs, m.power[0:S, 0:1], ALU.pow).then_inc(s_krs, 1)
                pool.wait_ge(s_krs, b + 1)
                pool.tensor_tensor(bias, rs, mean, ALU.mult).then_inc(s_kbias, 1)
                pool.wait_ge(s_kn, b + 1)
                pool.tensor_tensor(kn, kn, m.qg[0:S, :], ALU.mult).then_inc(s_kga, 1)
                pool.wait_ge(s_kga, b + 1)
                pool.tensor_tensor(kn, kn, m.qb[0:S, :], ALU.add).then_inc(s_kb, 1)

        @block.scalar
        def _(act):
            act.dma_start(junk[:, 0:2], bcast(a["g_xattn"], P)).then_inc(s_gate, 16)
            act.dma_start(junk[:, 2:4], bcast(a["g_ffn"], P)).then_inc(s_gate, 16)
            act.dma_start(w1s, a["L0_ffn_w1"].rearrange("(k p) d -> p k d", p=P)).then_inc(s_w12, 16)
            act.dma_start(w2s, a["L0_ffn_w2"].rearrange("(k p) h -> p k h", p=P)).then_inc(s_w12, 16)
            act.dma_start(m.vg, bcast(a["L1_xattn_tab_g"], P)).then_inc(s_kvg, 16)
            act.dma_start(m.vb, bcast(a["L1_xattn_tab_b"], P)).then_inc(s_kvg, 16)
            act.dma_start(m.qg, bcast(a["L1_xattn_k_g"], P)).then_inc(s_kvg, 16)
            act.dma_start(m.qb, bcast(a["L1_xattn_k_b"], P)).then_inc(s_kvg, 16)
            act.dma_start(wk, a["L1_xattn_Wk"].rearrange("(k p) n -> p k n", p=P)).then_inc(s_kv, 16)
            act.dma_start(wv, a["L1_xattn_Wv"].rearrange("(k p) n -> p k n", p=P)).then_inc(s_kv, 16)
            act.wait_ge(s_gate, 32)
            act.activation(m.tanh, junk, ACT.Tanh).then_inc(s_th, 1)
            act.wait_ge(s_ctx, 16)
            for b in range(B):
                if b:
                    act.wait_ge(s_aa, b)
                act.activation(sqjunk, m.ctx[:, b, :], ACT.Square, accum_out=norm2[:, b:b + 1]).then_inc(s_aa, 1)
            def roots(b):
                act.wait_ge(s_a, b + 1)
                act.activation(sq[:, 1, :], sq[:, 0, :], ACT.Sqrt).then_inc(s_sq, 1)
            for b in range(B):
                act.wait_ge(s_xT, b + 1)
                if b >= 2:
                    act.wait_ge(s_D, b - 1)
                bank = m.bank(b % 2)[:, 0, :].rearrange("p (k j) -> p k j", k=KD)
                act.activation(xnT[:, b % 2], bank, ACT.Copy).then_inc(s_xTc, 1)
                act.activation(xsq[:, b % 2], bank, ACT.Square).then_inc(s_xsq, 1)
                if b:
                    roots(b - 1)
            roots(B - 1)
            act.wait_ge(s_w12, 32)
            act.activation(wq[:, 0:HT * D], w1s.rearrange("p k d -> p (k d)"), ACT.Abs,
                           accum_out=wsum[:, 0:1]).then_inc(s_ab, 1)
            act.wait_ge(s_ab, 1)
            act.activation(wq[:, 0:HT * D], w2s.rearrange("p k h -> p (k h)"), ACT.Abs,
                           accum_out=wsum[:, 1:2]).then_inc(s_ab, 1)
            act.wait_ge(s_wT, 1)
            act.activation(wsum, m.bank(7)[:, 0, 0:2], ACT.Copy).then_inc(s_tot, 1)
            for n in range(2):
                for half in range(2):
                    act.wait_ge(s_wT, 2 + 2 * n + half)
                    dst = (m.w1T[:, half, :] if n == 0 else
                           m.w2T[:, 4 * half:4 * half + 4, :].rearrange("p k d -> p (k d)"))
                    act.activation(dst, m.bank(6 + half)[:, 0, :].bitcast(BF16), ACT.Copy).then_inc(s_wTc, 1)
            for b in range(B):
                act.wait_ge(s_kvTp, b + 1)
                if b:
                    act.wait_ge(s_v, b)
                act.activation(kvT, m.bank(5)[:, 0, 0:KD * S].rearrange("p (k s) -> p k s", k=KD),
                               ACT.Copy).then_inc(s_kvTc, 1)
                act.wait_ge(s_k, b + 1)
                if b:
                    act.wait_ge(s_kn, b)
                kp = m.bank(0, 2)[0:S, :, 0:INNER // 2]
                kr = kraw.rearrange("p (n j) -> p n j", n=2)
                act.activation(kr, kp, ACT.Identity, accum_out=ksum[:, 0, b:b + 1]).then_inc(s_ksum, 1)
                act.wait_ge(s_v, b + 1)
                if b == 0:
                    act.wait_ge(s_one, 1)
                for n in range(2):
                    act.activation(m.v[:, b, 6 * n:6 * n + 6, 0:DH],
                                   m.bank(2 + n)[0:S, 0, 0:INNER // 2].rearrange("p (h e) -> p h e", e=DH),
                                   ACT.Copy).then_inc(s_vc, 1)
                act.wait_ge(s_knm, b + 1)
                act.wait_ge(s_ksum, b + 1)
                if b:
                    act.wait_ge(s_kTp, b)
                act.activation(kn, kraw, ACT.Square, bias=ksum[:, 1, b:b + 1],
                               accum_out=ksum[:, 2, b:b + 1]).then_inc(s_kssq, 1)
                act.wait_ge(s_kbias, b + 1)
                act.wait_ge(s_kssq, b + 1)
                act.activation(kn, kraw, ACT.Identity, bias=ksum[:, 4, b:b + 1],
                               scale=ksum[:, 3, b:b + 1]).then_inc(s_kn, 1)
                act.wait_ge(s_kTp, b + 1)
                act.activation(m.kT[:, :, b, :], m.bank(4)[:, 0, 0:PAIRS * S].rearrange("p (i s) -> p i s", i=PAIRS),
                               ACT.Copy).then_inc(s_kTc, 1)
            act.wait_ge(s_vT, 1)
            act.activation(m.vT, m.bank(7)[0:S, 0, 0:2 * B].rearrange("p (k b) -> p k b", k=2),
                           ACT.Copy).then_inc(s_vTc, 1)

        @block.tensor
        def _(pe):
            pe.wait_ge(s_const, 4)
            pe.wait_ge(s_ctx, 16)
            for b in range(B):
                if b >= 2:
                    pe.wait_ge(s_cTc, b - 1)
                for k in range(KD):
                    mm = pe.transpose(m.bank(2 + b % 2)[:, 0, k * S:(k + 1) * S],
                                      m.ctx[:, b, k * P:(k + 1) * P], m.ident[0:S, 0:S])
                mm.then_inc(s_cT, 1)
                pe.wait_ge(s_xn, 2 * b + 2)
                if b >= 2:
                    pe.wait_ge(s_xsq, b - 1)
                for h in range(2):
                    for k in range(KD):
                        mm = pe.transpose(m.bank(b % 2)[:, 0, k * TQ + h * P:k * TQ + (h + 1) * P],
                                          xn[:, 2 * b + h, k * P:(k + 1) * P], m.ident)
                mm.then_inc(s_xT, 1)
                pe.wait_ge(s_cTc, b + 1)
                pe.wait_ge(s_xTc, b + 1)
                if b >= 2:
                    pe.wait_ge(s_a, b - 1)
                out = m.bank(4 + b % 2)[0:S, 0, 0:TQ]
                for k in range(KD):
                    pe.matmul(out, ctxT[:, k, :], xnT[:, b % 2, k, :], start=(k == 0), stop=False)
                pe.wait_ge(s_xsq, b + 1)
                for k in range(KD):
                    mm = pe.matmul(out, ones[:, 0:S], xsq[:, b % 2, k, :], start=False, stop=(k == KD - 1))
                mm.then_inc(s_D, 1)
            pe.wait_ge(s_ab, 2)
            pe.matmul(m.bank(7)[:, 0, 0:2], ones, wsum, start=True, stop=True).then_inc(s_wT, 1)
            for n in range(2):
                pe.wait_ge(s_wqb, n + 1)
                src = wq.rearrange("p (k d) -> p k d", k=HT) if n == 0 else wq.rearrange("p (k h) -> p k h", k=KD)
                for half in range(2):
                    if n == 0 and half:
                        pe.wait_ge(s_tot, 1)
                    if n:
                        pe.wait_ge(s_wTc, half + 1)
                    bank = m.bank(6 + half)[:, 0, :].bitcast(BF16)
                    for k in range(8):
                        if n == 0:
                            out, in_ = bank[:, k * P:(k + 1) * P], src[:, k, half * P:(half + 1) * P]
                        else:
                            tile = 4 * half + k // 2
                            out = bank[:, k * P:(k + 1) * P]
                            in_ = src[:, k % 2, tile * P:(tile + 1) * P]
                        mm = pe.transpose(out, in_, m.identb)
                    mm.then_inc(s_wT, 1)
            pe.wait_ge(s_kv, 32)
            for b in range(B):
                pe.wait_ge(s_kvb, b + 1)
                if b:
                    pe.wait_ge(s_kvTc, b)
                for k in range(KD):
                    mm = pe.transpose(m.bank(5)[:, 0, k * S:(k + 1) * S], kvn[:, b, k * P:(k + 1) * P],
                                      m.ident[0:S, 0:S])
                mm.then_inc(s_kvTp, 1)
                pe.wait_ge(s_kvTc, b + 1)
                for w, bank, done, read in ((wk, 0, s_k, s_ksum), (wv, 2, s_v, s_vc)):
                    if b:
                        pe.wait_ge(read, b if read is s_ksum else 2 * b)
                    for n in range(2):
                        for k in range(KD):
                            mm = pe.matmul(m.bank(bank + n)[0:S, 0, 0:INNER // 2], kvT[:, k, :],
                                           w[:, k, n * INNER // 2:(n + 1) * INNER // 2],
                                           start=(k == 0), stop=(k == KD - 1))
                    mm.then_inc(done, 1)
                pe.wait_ge(s_kb, b + 1)
                if b:
                    pe.wait_ge(s_kTc, b)
                for i in range(PAIRS):
                    mm = pe.transpose(m.bank(4)[:, 0, i * S:(i + 1) * S], kn[:, i * P:(i + 1) * P],
                                      m.ident[0:S, 0:S])
                mm.then_inc(s_kTp, 1)
            pe.wait_ge(s_hop, S)
            pe.wait_ge(s_wTc, 4)
            for k in range(2):
                mm = pe.transpose(m.bank(7)[0:S, 0, k * B:(k + 1) * B], path[:, k:k + S], m.ident[0:B, 0:B])
            mm.then_inc(s_vT, 1)

        @block.vector
        def _(dve):
            dve.wait_ge(s_ctx, 16)
            for b in range(B):
                dve.bn_stats(cstats[:, b, :], m.ctx[:, b, :]).then_inc(s_cst, 1)
            for b in range(B):
                dve.wait_ge(s_cst, b + 1)
                dve.bn_aggr(cmv[:, b, :], cstats[:, b, :]).then_inc(s_cmv, 1)
            for q in range(4):
                dve.wait_ge(s_x[q], 16)
                for t in range(4 * q, 4 * q + 4):
                    dve.bn_stats(stats[:, t, :], m.x[:, t, :]).then_inc(s_st, 1)
                for t in range(4 * q, 4 * q + 4):
                    dve.wait_ge(s_st, t + 1)
                    dve.bn_aggr(mv[:, t, :], stats[:, t, :]).then_inc(s_mv, 1)
            dve.wait_ge(s_const, 4)
            def transposed_context(b):
                dve.wait_ge(s_cT, b + 1)
                if b:
                    dve.wait_ge(s_D, b)
                dve.tensor_scalar(ctxT, m.bank(2 + b % 2)[:, 0, 0:KD * S].rearrange("p (k s) -> p k s", k=KD),
                                  -2.0, None, ALU.mult).then_inc(s_cTc, 1)
            for q in range(4):
                dve.wait_ge(s_r, q + 1)
                for t in range(4 * q, 4 * q + 4):
                    dve.tensor_scalar(xn[:, t, :], m.x[:, t, :], mv[:, t, 0:1], rstd[:, t:t + 1],
                                      ALU.subtract, ALU.mult).then_inc(s_xn, 1)
            dve.wait_ge(s_cr, 1)
            for b in range(B):
                dve.tensor_scalar(kvn[:, b, :], m.ctx[:, b, :], cmv[:, b, 0:1], crstd[:, b:b + 1],
                                  ALU.subtract, ALU.mult).then_inc(s_kvn, 1)
            dve.wait_ge(s_aa, B)
            for b in range(B):
                transposed_context(b)
                dve.wait_ge(s_D, b + 1)
                if b:
                    dve.wait_ge(s_ar, b)
                dve.tensor_scalar(sq[:, 0, :], m.bank(4 + b % 2)[0:S, 0, 0:TQ], norm2[:, b:b + 1], 1e-30,
                                  ALU.add, ALU.max).then_inc(s_a, 1)
                dve.wait_ge(s_sq, b + 1)
                if b:
                    dve.wait_ge(s_dr, b)
                dve.reciprocal(sq[:, 2, :], sq[:, 1, :]).then_inc(s_rc, 1)
                dve.wait_ge(s_rc, b + 1)
                dve.wait_ge(s_a, b + 1)
                dve.tensor_tensor(sq[:, 0, :], sq[:, 0, :], sq[:, 2, :], ALU.mult).then_inc(s_ar, 1)
                dve.wait_ge(s_ar, b + 1)
                dve.tensor_tensor(drow[:, b, :], sq[:, 0, :], sq[:, 1, :], ALU.add).then_inc(s_dr, 1)

            dve.wait_ge(s_init, 6)
            dve.wait_ge(s_dist, 16 * CH)
            to_right = [(p - B) % (CH * B) for p in range(CH * B)]

            def step(base, u, turn_no=0):
                t = base + u
                start = isinstance(base, int) and u == 0
                prev, row = ring[:, (u - 1) % RING, :], ring[:, u, :]
                if not start:
                    dve.wait_ge(s_scan, t)
                    if not (isinstance(base, int) and u < 3):
                        dve.wait_ge(s_bnd, t - 2)
                dve.tensor_tensor(diag, prev[:, 1:CW + 1], prev[:, 0:CW], ALU.min).then_inc(s_min, 1)
                if not start:
                    dve.stream_shuffle(shifted[:, u % 2:u % 2 + 1], prev[:, CW:CW + 1], to_right).then_inc(s_shf, 1)
                dve.wait_ge(s_min, t + 1)
                if not (isinstance(base, int) and u < 2):
                    dve.wait_ge(s_bnd, t - 1)
                if u % GROUP == 0 and not isinstance(base, int):
                    dve.wait_ge(s_cost[u // GROUP], 16 * turn_no)
                dve.tensor_tensor_scan(row[:, 1:CW + 1], diag, dist[:, bass.ds(t, 1), :].rearrange("p t w -> p (t w)"),
                                       first if start else row[:, 0:1], ALU.min, ALU.add).then_inc(s_scan, 1)
                if not start:
                    dve.wait_ge(s_shf, t)
                    dve.tensor_tensor(ring[:, (u + 1) % RING, 0:1], shifted[:, u % 2:u % 2 + 1], floor, ALU.max).then_inc(s_bnd, 1)

            for u in range(RING):
                step(0, u)
            with dve.Fori(1, STEPS // RING) as turn_no:
                for u in range(RING):
                    step(turn_no * RING, u, turn_no)

            for g in range(RING // GROUP):
                dve.wait_ge(s_cost[g], 16 * STEPS // RING)
            for buf in (cost, above):
                dve.memset(buf[:, :, 0:1], BIG).then_inc(s_cm, 1)
            dve.memset(above[0:1, :, 1:W1], BIG).then_inc(s_cm, 1)
            dve.wait_ge(s_cm, 3)
            dve.wait_ge(s_cl, 32 * CH)
            up, corner, left = above[:, :, 1:W1], above[:, :, 0:TQ], cost[:, :, 0:TQ]
            iota_b = m.iota[0:S, :].unsqueeze(1).to_broadcast([S, B, TQ])
            dve.tensor_tensor(best, up, corner, ALU.min).then_inc(s_F, 1)
            dve.tensor_tensor(turn, corner, up, ALU.is_le).then_inc(s_F, 1)
            dve.wait_ge(s_F, 1)
            dve.tensor_tensor(stay, left, best, ALU.is_ge).then_inc(s_F, 1)
            dve.wait_ge(s_F, 2)
            dve.scalar_tensor_tensor(turn, turn, -0.75, iota_b, ALU.mult, ALU.add).then_inc(s_F, 1)
            dve.wait_ge(s_F, 4)
            dve.tensor_tensor(turn, turn, stay, ALU.mult).then_inc(s_F, 1)
            dve.wait_ge(s_F, 5)
            for b in range(B):
                scan = dve.tensor_tensor_scan(jump[:, b, :], turn[:, b, :], turn[:, b, :], 0.0, ALU.max, ALU.max)
            scan.then_inc(s_F, 1)
            dve.wait_ge(s_F, 6)
            dve.tensor_copy(djump[:, :, 0:1], jump[:, :, 0:1]).then_inc(s_cm, 1)
            dve.tensor_tensor(djump[:, :, 1:TQ], jump[:, :, 1:TQ], jump[:, :, 0:TQ - 1], ALU.subtract)\
               .then_inc(s_F, 1)
            dve.wait_ge(s_djld, 16)
            with dve.Fori(1, S) as n:
                here, below = n * -1 + S, n * -1 + (S + 1)
                dve.wait_ge(s_hop, n)
                dve.scalar_tensor_tensor(hopjunk, m.iota[0:B, :], path[:, bass.ds(below, 1)],
                                         djump_b[:, bass.ds(here, 1), :].rearrange("p i j -> p (i j)"),
                                         ALU.is_le, ALU.mult,
                                         accum_out=path[:, bass.ds(here, 1)]).then_inc(s_hop, 1)


def pipeline(eng, stages, count, head):
    assert head % 2 == 0
    depth = max(lag for _, lag in stages)

    def turn(k):
        for stage, lag in stages:
            if 0 <= k - lag < count:
                stage(k - lag, (k - lag) % 2)

    for k in range(head):
        turn(k)
    tail = max(head, (count - 2) // 2 * 2)
    if head < tail:
        with eng.Fori(head // 2, tail // 2) as i:
            for u in range(2):
                for stage, lag in stages:
                    stage(i * 2 + (u - lag), (u - lag) % 2)
    for k in range(tail, count + depth):
        turn(k)


class Waits:

    def __init__(self, eng, tick):
        self.eng, self.tick = eng, tick

    def __call__(self, sem, n, alone=False):
        if isinstance(n, int):
            if n > 0:
                self.eng.wait_ge(sem, n)
        else:
            self.eng.wait_ge(sem, n)
            if alone:
                self.eng.sem_inc(self.tick, 1)


def ffn(nc, ctx, m, a):
    def sem(name):
        return nc.alloc_semaphore("f_" + name)

    arena = m.arena
    b1 = arena.take(P, HID, at=0)
    g2, c2 = arena.take(P, HID), arena.take(P, HID)
    g1, c1, b2 = (arena.take(P, D) for _ in range(3))
    def pair(cols, dtype=F32, parts=P):
        return [arena.take(parts, cols, dtype) for _ in range(2)]
    h, hq, hqT = pair(D), pair(D, BF16), pair(D, BF16)
    z, zq, zqT = pair(HID), pair(HID, BF16), pair(HID, BF16)
    out1 = arena.take(P, D)
    mask = arena.take(S, TQ)
    half_mask = arena.take(S, TQ)
    st1, mv1, r1, am1, inv1, sc1, f1 = pair(6), pair(2), pair(1), pair(1), pair(1), pair(1), pair(1)
    st2, mv2, r2, am2, inv2, sc2, f2 = pair(12), pair(2), pair(1), pair(1), pair(1), pair(1), pair(1)
    magic, unmagic = arena.take(P, 1), arena.take(P, 1)

    names = ("ld start go mhalf mask E x1 st1 mv1 v1 r1 t1 h am1 inv1 sc1 f1 hr hq T1 hqT Z z g st2 mv2 v2 r2 "
             "t2 h2 am2 inv2 sc2 f2 zr zq T2 zqT Y y x2").split()
    q = {n: sem(n) for n in names}

    def work(t):
        return m.x[:, bass.ds(t, 1), :].rearrange("p t d -> p (t d)")

    with nc.Block() as block:
        @block.sync
        def _(sp):
            for dst, src in ((b1, a["L0_ffn_b1"]), (g2, a["L0_ffn_ln2_g"]), (c2, a["L0_ffn_ln2_b"]), (g1, a["L0_ffn_ln1_g"]),
                             (c1, a["L0_ffn_ln1_b"]), (b2, a["L0_ffn_b2"])):
                sp.dma_start(dst, bcast(src, P)).then_inc(q["ld"], 16)
            sp.dma_start(m.wa.rearrange("p (k n) -> p k n", k=KD),
                         a["L1_xattn_Wq"].rearrange("(k p) n -> p k n", p=P)).then_inc(m.ld_attn, 16)
            sp.dma_start(m.wb.rearrange("p (k n) -> p k n", k=PAIRS),
                         a["L1_xattn_Wo"].rearrange("(k p) n -> p k n", p=P)).then_inc(m.ld_attn, 16)
            for dst, src in ((m.qg, a["L1_xattn_q_g"]), (m.qb, a["L1_xattn_q_b"]), (m.vg, a["L1_xattn_vid_g"]),
                             (m.vb, a["L1_xattn_vid_b"]), (m.bo, a["L1_xattn_bo"])):
                sp.dma_start(dst, bcast(src, P)).then_inc(m.ld_attn, 16)
            sp.dma_start(m.early.tensor[:, :].rearrange("p (e k h) -> p e k h", e=NE, k=KD),
                         a["L1_ffn_W1"].rearrange("e (k p) h -> p e k h", p=P)).then_inc(m.ld_w1, 16)

        @block.gpsimd
        def _(pool):
            wait = Waits(pool, sem("tick_pool"))
            pool.memset(magic, MAGIC).then_inc(q["start"], 1)
            pool.memset(unmagic, -MAGIC).then_inc(q["start"], 1)

            def rstd1(t, p):
                wait(q["mv1"], t + 1, alone=True)
                wait(q["h"], t - 1, alone=True)
                pool.tensor_scalar(r1[p], mv1[p][:, 1:2], 1.0 + LN_EPS, LN_EPS * LN_EPS, ALU.mult,
                                   ALU.add).then_inc(q["v1"], 1)
                wait(q["v1"], t + 1)
                pool.tensor_tensor(r1[p], r1[p], m.power[:, 0:1], ALU.pow).then_inc(q["r1"], 1)

            def rstd2(t, p):
                wait(q["mv2"], t + 1, alone=True)
                wait(q["h2"], t - 1, alone=True)
                pool.tensor_scalar(r2[p], mv2[p][:, 1:2], LN_EPS, None, ALU.add).then_inc(q["v2"], 1)
                wait(q["v2"], t + 1)
                pool.tensor_tensor(r2[p], r2[p], m.power[:, 0:1], ALU.pow).then_inc(q["r2"], 1)

            pipeline(pool, [(rstd2, 3), (rstd1, 0)], TILES, 6)

        @block.scalar
        def _(act):
            wait = Waits(act, sem("tick_act"))

            act.wait_ge(q["start"], 2)

            def scale1(t, p):
                wait(q["sc1"], t + 1)
                act.activation(h[p], h[p], ACT.Identity, bias=magic, scale=sc1[p]).then_inc(q["hr"], 1)

            def round1(t, p):
                wait(q["hr"], t + 1)
                wait(q["T1"], t - 1)
                act.activation(hq[p], h[p], ACT.Identity, bias=unmagic).then_inc(q["hq"], 1)

            def copy1(t, p):
                wait(q["T1"], t + 1)
                wait(q["Z"], t - 1)
                act.activation(hqT[p], m.bank(1)[:, 0, 0:P].bitcast(BF16), ACT.Copy)\
                   .then_inc(q["hqT"], 1)

            def gelu(t, p):
                wait(q["z"], t + 1)
                act.activation(z[p], z[p], ACT.Gelu).then_inc(q["g"], 1)

            def scale2(t, p):
                wait(q["sc2"], t + 1)
                act.activation(z[p], z[p], ACT.Identity, bias=magic, scale=sc2[p]).then_inc(q["zr"], 1)

            def round2(t, p):
                wait(q["zr"], t + 1)
                wait(q["T2"], t - 1)
                act.activation(zq[p], z[p], ACT.Identity, bias=unmagic).then_inc(q["zq"], 1)

            def copy2(t, p):
                wait(q["T2"], t + 1)
                wait(q["Y"], t - 1)
                act.activation(zqT[p], m.bank(6)[:, 0, :].bitcast(BF16), ACT.Copy).then_inc(q["zqT"], 1)

            pipeline(act, [(copy2, 4), (scale1, 1), (round1, 1), (gelu, 2), (copy1, 1), (scale2, 3), (round2, 3)],
                     TILES, 6)

        @block.tensor
        def _(pe):
            wait = Waits(pe, sem("tick_pe"))

            def aligned(t, p):
                b = t // 2 if isinstance(t, int) else (t - p) // 2
                wait(q["mask"], (t // 2 if isinstance(t, int) else b) + 1)
                wait(q["x1"], t)
                pe.matmul(m.bank(0)[:, 0, 0:D], mask[:, p * P:(p + 1) * P],
                          m.ctx[:, bass.ds(b, 1), :].rearrange("s b d -> s (b d)"), start=True, stop=True)\
                  .then_inc(q["E"], 1)

            def turn1(t, p):
                wait(q["hq"], t + 1)
                wait(q["hqT"], t)
                for k in range(KD):
                    mm = pe.transpose(m.bank(1)[:, 0, k * 64:(k + 1) * 64].bitcast(BF16),
                                      hq[p][:, k * P:(k + 1) * P], m.identb)
                mm.then_inc(q["T1"], 1)

            def up(t, p):
                wait(q["hqT"], t + 1)
                wait(q["z"], t - 1)
                for n in range(2):
                    for k in range(KD):
                        mm = pe.matmul(m.bank(2 + 2 * p + n)[:, 0, :], hqT[p][:, k * P:(k + 1) * P],
                                       m.w1T[:, k, n * 512:(n + 1) * 512], start=(k == 0), stop=(k == KD - 1))
                mm.then_inc(q["Z"], 1)

            def turn2(t, p):
                wait(q["zq"], t + 1)
                wait(q["zqT"], t)
                for k in range(HT):
                    mm = pe.transpose(m.bank(6)[:, 0, k * 64:(k + 1) * 64].bitcast(BF16),
                                      zq[p][:, k * P:(k + 1) * P], m.identb)
                mm.then_inc(q["T2"], 1)

            def down(t, p):
                wait(q["zqT"], t + 1)
                wait(q["y"], t)
                for k in range(HT):
                    mm = pe.matmul(m.bank(7)[:, 0, 0:D], zqT[p][:, k * P:(k + 1) * P],
                                   m.w2T[:, k, :], start=(k == 0), stop=(k == HT - 1))
                mm.then_inc(q["Y"], 1)

            pipeline(pe, [(turn2, 4), (down, 4), (aligned, 0), (turn1, 1), (up, 1)], TILES, 6)

        @block.vector
        def _(dve):
            wait = Waits(dve, sem("tick_dve"))
            dve.wait_ge(q["ld"], 96)

            def path_mask(b):
                v0, v1 = (m.vT[:, k, bass.ds(b, 1)] for k in range(2))
                wait(q["mask"], b)
                dve.tensor_scalar(half_mask, m.iota[0:S, :], v0, None, ALU.is_ge).then_inc(q["mhalf"], 1)
                wait(q["mhalf"], b + 1)
                dve.scalar_tensor_tensor(mask, m.iota[0:S, :], v1, half_mask, ALU.is_le, ALU.mult)\
                   .then_inc(q["mask"], 1)

            def next_mask(t, p):
                if p and not (isinstance(t, int) and t == TILES - 1):
                    wait(q["E"], t + 1)
                    path_mask((t + 1) // 2)

            def add_aligned(t, p):
                wait(q["E"], t + 1)
                dve.scalar_tensor_tensor(work(t), m.bank(0)[:, 0, 0:D], m.tanh[:, 0:1], work(t),
                                         ALU.mult, ALU.add).then_inc(q["x1"], 1)
                wait(q["x1"], t + 1, alone=True)
                dve.bn_stats(st1[p], work(t)).then_inc(q["st1"], 1)
                wait(q["st1"], t + 1, alone=True)
                wait(q["r1"], t - 1, alone=True)
                dve.bn_aggr(mv1[p], st1[p]).then_inc(q["mv1"], 1)

            def quant(t, p, k, am, inv, sc, f, src, wscale):
                dve.tensor_reduce(am[p], src, AX.X, ALU.max, apply_absolute_value=True).then_inc(q["am" + k], 1)
                wait(q["am" + k], t + 1)
                dve.tensor_scalar(inv[p], am[p], 1e-5, 1.0 / 127.0, ALU.max, ALU.mult).then_inc(q["inv" + k], 1)
                wait(q["inv" + k], t + 1)
                dve.reciprocal(sc[p], inv[p]).then_inc(q["sc" + k], 1)
                dve.tensor_tensor(f[p], inv[p], wscale, ALU.mult).then_inc(q["f" + k], 1)

            def norm1(t, p):
                wait(q["r1"], t + 1)
                wait(q["hq"], t - 1)
                dve.scalar_tensor_tensor(h[p], work(t), mv1[p][:, 0:1], g1, ALU.subtract, ALU.mult)\
                   .then_inc(q["t1"], 1)
                wait(q["t1"], t + 1)
                dve.scalar_tensor_tensor(h[p], h[p], r1[p], c1, ALU.mult, ALU.add).then_inc(q["h"], 1)
                wait(q["h"], t + 1)
                quant(t, p, "1", am1, inv1, sc1, f1, h[p], m.wscale[:, 0:1])

            def hidden(t, p):
                wait(q["Z"], t + 1)
                wait(q["f1"], t + 1)
                wait(q["zq"], t - 1)
                dve.scalar_tensor_tensor(z[p], m.bank(2 + 2 * p, 2).rearrange("p n j -> p (n j)"), f1[p], b1,
                                         ALU.mult, ALU.add).then_inc(q["z"], 1)

            def stats2(t, p):
                wait(q["g"], t + 1)
                for n in range(2):
                    dve.bn_stats(st2[p][:, 6 * n:6 * n + 6], z[p][:, n * 512:(n + 1) * 512]).then_inc(q["st2"], 1)
                wait(q["st2"], t * 2 + 2, alone=True)
                wait(q["r2"], t - 1, alone=True)
                dve.bn_aggr(mv2[p], st2[p]).then_inc(q["mv2"], 1)

            def norm2(t, p):
                wait(q["r2"], t + 1)
                dve.scalar_tensor_tensor(z[p], z[p], mv2[p][:, 0:1], g2, ALU.subtract, ALU.mult)\
                   .then_inc(q["t2"], 1)
                wait(q["t2"], t + 1)
                dve.scalar_tensor_tensor(z[p], z[p], r2[p], c2, ALU.mult, ALU.add).then_inc(q["h2"], 1)
                wait(q["h2"], t + 1)
                quant(t, p, "2", am2, inv2, sc2, f2, z[p], m.wscale[:, 1:2])

            def add_out(t, p):
                wait(q["Y"], t + 1)
                wait(q["f2"], t + 1)
                wait(q["x2"], t)
                dve.scalar_tensor_tensor(out1, m.bank(7)[:, 0, 0:D], f2[p], b2,
                                         ALU.mult, ALU.add).then_inc(q["y"], 1)
                wait(q["y"], t + 1)
                dve.scalar_tensor_tensor(work(t), out1, m.tanh[:, 2:3], work(t), ALU.mult, ALU.add)\
                   .then_inc(q["x2"], 1)

            path_mask(0)
            pipeline(dve, [(stats2, 3), (norm1, 1), (hidden, 2), (add_aligned, 0), (next_mask, 0), (norm2, 3),
                           (add_out, 4)], TILES, 6)


def cap(n):
    return min(n, TILES) if isinstance(n, int) else n


def attention(nc, ctx, m, a):
    def sem(name):
        return ctx.enter_context(nc.semaphore("a_" + name))

    arena = m.arena
    arena.at = 0
    def pair(cols):
        return [arena.take(P, cols) for _ in range(2)]
    h, hT = arena.take(P, D), arena.take(P, D)
    qn, qT, prob, o, oT = pair(INNER), pair(INNER), pair(HEADS * S), pair(INNER), pair(INNER)
    pT = arena.take(S, HEADS * P).rearrange("s (h j) -> s h j", h=HEADS)
    kb = arena.take(P, PAIRS * S).rearrange("p (i s) -> p i s", i=PAIRS)
    out1 = arena.take(P, D)
    st, mv, r = pair(6), pair(2), pair(1)
    stq, mvq, rq, top, rden = pair(12), pair(2), pair(1), arena.take(P, HEADS), arena.take(P, HEADS)
    wq = m.wa.rearrange("p (k n) -> p k n", k=KD)
    wo = m.wb.rearrange("p (i n) -> p i n", i=PAIRS)
    HALF = INNER // 2

    names = ("st mv v r t1 h xT hT q stq mvq vq rq qg qn qT qTc kb S top sub exp PT PTc PV rden o oT oTc out o1 x3 "
             "qscale").split()
    q = {n: sem(n) for n in names}

    s_ps = m.bank(0, 2)[:, :, 0:HEADS // 2 * S]
    q_ps = m.bank(2, 2)[:, :, 0:HALF]
    t_ps = m.bank(4, 2)[:, :, 0:HALF]
    p_ps = m.bank(6, 2)[:, :, 0:HALF]
    PVW = DH + 1
    pv_ps = [m.bank(3)[:, 0, 0:6 * PVW].rearrange("p (h e) -> p h e", h=6),
             m.bank(2)[:, 0, 0:6 * PVW].rearrange("p (h e) -> p h e", h=6)]

    def work(t):
        return m.x[:, bass.ds(t, 1), :].rearrange("p t d -> p (t d)")

    def halves(x):
        return x.rearrange("p (n c) -> p n c", n=2)

    with nc.Block() as block:
        @block.gpsimd
        def _(pool):
            wait = Waits(pool, sem("tick_pool"))

            def keys(b):
                pool.tensor_copy(kb, m.kT[:, :, bass.ds(b, 1), :].rearrange("p i b s -> p i (b s)"))\
                    .then_inc(q["kb"], 1)

            def rstd(t, p):
                wait(q["mv"], t + 1, alone=True)
                wait(q["h"], t - 1, alone=True)
                pool.tensor_scalar(r[p], mv[p][:, 1:2], 1.0 + LN_EPS, LN_EPS * LN_EPS, ALU.mult, ALU.add)\
                    .then_inc(q["v"], 1)
                wait(q["v"], t + 1)
                pool.tensor_tensor(r[p], r[p], m.power[:, 0:1], ALU.pow).then_inc(q["r"], 1)

            def rstd_q(t, p):
                wait(q["mvq"], t + 1, alone=True)
                wait(q["qn"], t - 1, alone=True)
                pool.tensor_scalar(rq[p], mvq[p][:, 1:2], LN_EPS, None, ALU.add).then_inc(q["vq"], 1)
                wait(q["vq"], t + 1)
                pool.tensor_tensor(rq[p], rq[p], m.power[:, 0:1], ALU.pow).then_inc(q["rq"], 1)

            def next_keys(t, p):
                if p and not (isinstance(t, int) and t == TILES - 1):
                    wait(q["S"], t + 1, alone=True)
                    keys((t + 1) // 2)

            keys(0)
            pipeline(pool, [(rstd, 0), (rstd_q, 1), (next_keys, 2)], TILES, 6)

        @block.scalar
        def _(act):
            wait = Waits(act, sem("tick_act"))

            def copy_x(t, p):
                wait(q["xT"], t + 1)
                wait(q["q"], t)
                act.activation(hT, m.bank(4)[:, 0, 0:D], ACT.Copy).then_inc(q["hT"], 1)

            def copy_q(t, p):
                wait(q["qT"], t + 1)
                wait(q["S"], t - 1)
                act.activation(halves(qT[p]), t_ps, ACT.Copy).then_inc(q["qTc"], 1)

            def exponent(t, p):
                wait(q["sub"], t + 1)
                act.activation(prob[p], prob[p], ACT.Exp).then_inc(q["exp"], 1)

            def copy_p(n):
                def stage(t, p):
                    wait(q["PT"], t * 2 + n + 1)
                    wait(q["PV"], t * 2 - 1 + n)
                    act.activation(halves(pT[:, 6 * n:6 * n + 6, :].rearrange("s h j -> s (h j)")), p_ps[0:S],
                                   ACT.Copy).then_inc(q["PTc"], 1)
                return stage

            def copy_o(t, p):
                wait(q["oT"], t + 1)
                wait(q["out"], t - 1)
                act.activation(halves(oT[p]), t_ps, ACT.Copy).then_inc(q["oTc"], 1)

            pipeline(act, [(copy_x, 1), (copy_q, 2), (copy_p(0), 3), (copy_o, 4), (copy_p(1), 3), (exponent, 2)],
                     TILES, 6)

        @block.tensor
        def _(pe):
            wait = Waits(pe, sem("tick_pe"))
            pe.wait_ge(m.ld_attn, 112)

            def turn_x(t, p):
                wait(q["h"], t + 1)
                if isinstance(t, int):
                    wait(q["qTc"], t - 1)
                wait(q["oTc"], t - 3)
                for k in range(KD):
                    mm = pe.transpose(m.bank(4)[:, 0, k * P:(k + 1) * P], h[:, k * P:(k + 1) * P], m.ident)
                mm.then_inc(q["xT"], 1)

            def query(t, p):
                wait(q["hT"], t + 1)
                if isinstance(t, int):
                    wait(q["qg"], t)
                wait(q["o"], t * 2 - 4)
                for n in range(2):
                    for k in range(KD):
                        mm = pe.matmul(q_ps[:, n, :], hT[:, k * P:(k + 1) * P], wq[:, k, n * HALF:(n + 1) * HALF],
                                       start=(k == 0), stop=(k == KD - 1))
                mm.then_inc(q["q"], 1)

            def turn_q(t, p):
                wait(q["qn"], t + 1)
                wait(q["hT"], cap(t + 2))
                for i in range(PAIRS):
                    mm = pe.transpose(t_ps[:, i // 3, i % 3 * P:(i % 3 + 1) * P], qn[p][:, i * P:(i + 1) * P],
                                      m.ident)
                mm.then_inc(q["qT"], 1)

            def scores(t, p):
                b = (t - p) // 2
                wait(q["qTc"], t + 1)
                wait(q["kb"], b + 1)
                wait(q["sub"], t)
                for i in range(HEADS):
                    rows = slice(i % 2 * DH, (i % 2 + 1) * DH)
                    mm = pe.matmul(s_ps[:, i % 2, i // 2 * S:(i // 2 + 1) * S],
                                   qT[p][rows, i // 2 * P:(i // 2 + 1) * P], kb[rows, i // 2, :],
                                   start=True, stop=True)
                mm.then_inc(q["S"], 1)

            def turn_p(n):
                def stage(t, p):
                    wait(q["exp"], t + 1)
                    wait(q["PTc"], t * 2 + n)
                    for i in range(6):
                        j = 6 * n + i
                        mm = pe.transpose(p_ps[0:S, i // 3, i % 3 * P:(i % 3 + 1) * P],
                                          prob[p][:, j * S:(j + 1) * S], m.ident)
                    mm.then_inc(q["PT"], 1)
                return stage

            def turn_o(t, p):
                wait(q["o"], t * 2 + 2)
                wait(q["qTc"], cap(t + 3))
                for i in range(PAIRS):
                    mm = pe.transpose(t_ps[:, i // 3, i % 3 * P:(i % 3 + 1) * P], o[p][:, i * P:(i + 1) * P],
                                      m.ident)
                mm.then_inc(q["oT"], 1)

            def output(t, p):
                wait(q["oTc"], t + 1)
                wait(q["qg"], cap(t + 4))
                for i in range(PAIRS):
                    mm = pe.matmul(m.bank(2)[:, 0, 0:D], oT[p][:, i * P:(i + 1) * P], wo[:, i, :],
                                   start=(i == 0), stop=(i == PAIRS - 1))
                mm.then_inc(q["out"], 1)

            def values(n):
                def stage(t, p):
                    b = (t - p) // 2
                    wait(q["PTc"], t * 2 + n + 1)
                    wait(q["qg"], cap(t + 3))
                    if n:
                        wait(q["o1"], t)
                    for i in range(6):
                        mm = pe.matmul(pv_ps[n][:, i, :], pT[:, 6 * n + i, :],
                                       m.v[:, bass.ds(b, 1), 2 * i + n, :].rearrange("s b e -> s (b e)"),
                                       start=True, stop=True)
                    mm.then_inc(q["PV"], 1)
                return stage

            pipeline(pe, [(turn_x, 1), (turn_q, 2), (query, 1), (scores, 2), (turn_p(0), 3), (turn_o, 4),
                          (turn_p(1), 3), (output, 4), (values(0), 3), (values(1), 3)], TILES, 6)

        @block.vector
        def _(dve):
            wait = Waits(dve, sem("tick_dve"))
            dve.wait_ge(m.ld_attn, 112)
            dve.tensor_scalar(m.qg, m.qg, DH ** -0.5, None, ALU.mult).then_inc(q["qscale"], 1)
            dve.tensor_scalar(m.qb, m.qb, DH ** -0.5, None, ALU.mult).then_inc(q["qscale"], 1)
            dve.wait_ge(q["qscale"], 2)

            def stats(t, p):
                wait(q["mv"], t - 1, alone=True)
                dve.bn_stats(st[p], work(t)).then_inc(q["st"], 1)
                wait(q["st"], t + 1, alone=True)
                wait(q["r"], t - 1, alone=True)
                dve.bn_aggr(mv[p], st[p]).then_inc(q["mv"], 1)

            def norm(t, p):
                wait(q["r"], t + 1)
                wait(q["xT"], t)
                dve.scalar_tensor_tensor(h, work(t), mv[p][:, 0:1], m.vg, ALU.subtract, ALU.mult)\
                   .then_inc(q["t1"], 1)
                wait(q["t1"], t + 1)
                dve.scalar_tensor_tensor(h, h, r[p], m.vb, ALU.mult, ALU.add).then_inc(q["h"], 1)

            def query_stats(t, p):
                wait(q["q"], t + 1)
                wait(q["mvq"], t - 1)
                for n in range(2):
                    dve.bn_stats(stq[p][:, 6 * n:6 * n + 6], q_ps[:, n, :]).then_inc(q["stq"], 1)
                wait(q["stq"], t * 2 + 2, alone=True)
                wait(q["rq"], t - 1, alone=True)
                dve.bn_aggr(mvq[p], stq[p]).then_inc(q["mvq"], 1)
                wait(q["mvq"], t + 1)
                wait(q["qT"], t - 1)
                dve.scalar_tensor_tensor(halves(qn[p]), q_ps, mvq[p][:, 0:1], halves(m.qg), ALU.subtract,
                                         ALU.mult).then_inc(q["qg"], 1)

            def query_norm(t, p):
                wait(q["rq"], t + 1)
                wait(q["qg"], t + 1)
                dve.scalar_tensor_tensor(qn[p], qn[p], rq[p], m.qb, ALU.mult, ALU.add).then_inc(q["qn"], 1)

            def shift(t, p):
                s4 = s_ps.rearrange("p n (h s) -> p n h s", s=S)
                wait(q["S"], t + 1)
                wait(q["sub"], t)
                dve.tensor_reduce(top.rearrange("p (n h) -> p n h", n=2), s4, AX.X, ALU.max).then_inc(q["top"], 1)
                wait(q["top"], t + 1)
                wait(q["PT"], t * 2 - 2)
                dve.tensor_tensor(prob[p].rearrange("p (n h s) -> p n h s", n=2, s=S), s4,
                                  top.rearrange("p (n h) -> p n h", n=2).unsqueeze(3)
                                  .to_broadcast([P, 2, 6, S]), ALU.subtract).then_inc(q["sub"], 1)

            def average(t, p):
                for n in range(2):
                    wait(q["PV"], t * 2 + n + 1)
                    wait(q["o"], t * 2 + n - 1)
                    dve.reciprocal(rden[:, 6 * n:6 * n + 6], pv_ps[n][:, :, DH]).then_inc(q["rden"], 1)
                    wait(q["rden"], t * 2 + n + 1)
                    wait(q["oT"], t - 1)
                    dve.tensor_tensor(o[p].rearrange("p (h n e) -> p n h e", n=2, e=DH)[:, n],
                                      pv_ps[n][:, :, 0:DH],
                                      rden[:, 6 * n:6 * n + 6].unsqueeze(2).to_broadcast([P, 6, DH]),
                                      ALU.mult).then_inc(q["o"], 1)

            def add_out(t, p):
                wait(q["out"], t + 1)
                wait(q["x3"], t)
                dve.tensor_tensor(out1, m.bank(2)[:, 0, 0:D], m.bo, ALU.add).then_inc(q["o1"], 1)
                wait(q["o1"], t + 1)
                dve.scalar_tensor_tensor(work(t), out1, m.tanh[:, 1:2], work(t), ALU.mult, ALU.add)\
                   .then_inc(q["x3"], 1)

            pipeline(dve, [(norm, 1), (stats, 0), (query_stats, 1), (shift, 2), (query_norm, 1), (add_out, 4),
                           (average, 3)], TILES, 6)



def route(nc, ctx, m, a):
    def sem(name):
        return ctx.enter_context(nc.semaphore("r_" + name))

    TE, COPIES = TILES * NE, 2 * TILES
    arena = m.arena
    m.weight = arena.take(P, COPIES, at=0).rearrange("p (c t) -> p c t", c=2)
    m.place = arena.take(P, COPIES, U32).rearrange("p (t c) -> p t c", c=2)
    m.token = arena.take(P, SLOTS + 1, U32)
    m.expert = arena.take(P, SLOTS + 1, I32)
    m.b1T = arena.take(P, NE * HT).rearrange("p (e k) -> p e k", e=NE)
    m.b2 = arena.take(P, NE * D).rearrange("p (e d) -> p e d", e=NE)
    m.routed_end = arena.at

    y = [arena.take(P, D) for _ in range(2)]
    yT = [arena.take(P, D) for _ in range(2)]
    def te():
        return arena.take(P, TE).rearrange("p (t e) -> p t e", t=TILES)
    logit, prob, cand, both, place, picked = te(), te(), te(), te(), te(), te()
    hot = [te(), te()]
    def per_tile():
        return arena.take(P, TILES)
    top, total, inv, p1, i1, p2, i2, gap, den = (per_tile() for _ in range(9))
    wg = arena.take(P, KD * NE).rearrange("p (k e) -> p k e", k=KD)
    bg = arena.take(P, NE)
    b1 = arena.take(NE * HT, P)
    st, mv, r = ([arena.take(P, n) for _ in range(2)] for n in (6, 2, 1))
    ones, upper = arena.take(P, P), arena.take(P, P)
    used, slots, last, start = (arena.take(P, NE) for _ in range(4))
    tokens = arena.take(P, TILES)
    where, slot, lane = (arena.take(P, COPIES).rearrange("p (c t) -> p c t", c=2) for _ in range(3))
    onlane = m.spare.take(P, COPIES * P, F16).rearrange("p (n j) -> p n j", n=COPIES)
    inslot = m.spare.take(P, COPIES * 40, F16).rearrange("p (n s) -> p n s", n=COPIES)[:, :, 0:SLOTS]
    past = arena.take(P, SLOTS * (NE - 1)).rearrange("p (s e) -> p s e", s=SLOTS)
    expert = arena.take(P, SLOTS)

    q = {n: sem(n) for n in ("ld st mv v r y T yT G lg const b1T e pe soft route onehot idx").split()}
    st_y = [sem(f"st_y{p}") for p in range(2)]
    m.y_dram = nc.dram_tensor("y_dram", [TILES * P, D], F32, kind="Internal").ap()

    def tile(x, t):
        return x[:, bass.ds(t, 1), :].rearrange("p t d -> p (t d)")

    def over_e(x):
        return x.unsqueeze(2).to_broadcast([P, TILES, NE])

    iota_e = m.iota[:, 0:NE].unsqueeze(1).to_broadcast([P, TILES, NE])

    with nc.Block() as block:
        @block.sync
        def _(sp):
            for dst, src in ((wg, a["L1_ffn_Wg"].rearrange("(k p) e -> p k e", p=P)), (bg, bcast(a["L1_ffn_bg"], P)),
                             (b1, a["L1_ffn_b1"].rearrange("e (k p) -> (e k) p", p=P)),
                             (m.b2.rearrange("p e d -> p (e d)"), bcast(a["L1_ffn_b2"].rearrange("e d -> (e d)"), P))):
                sp.dma_start(dst, src).then_inc(q["ld"], 16)
            sp.dma_start(m.late.tensor[:, :].rearrange("p (e k d) -> p e k d", e=NE, k=HT),
                         a["L1_ffn_W2"].rearrange("e (k p) d -> p e k d", p=P)).then_inc(m.ld_w2, 16)
            wait = Waits(sp, sem("tick_sp"))

            def store(t, p):
                wait(q["y"], t + 1)
                sp.dma_start(m.y_dram[bass.ds(t * P, P), :], y[p]).then_inc(st_y[p], 16)

            pipeline(sp, [(store, 0)], TILES, 6)
            for p in range(2):
                sp.wait_ge(st_y[p], 16 * TILES // 2)

        @block.gpsimd
        def _(pool):
            wait = Waits(pool, sem("tick_pool"))
            pool.memset(ones, 1.0).then_inc(q["const"], 1)
            pool.wait_ge(q["const"], 1)
            pool.affine_select(out=upper, in_=ones, compare_op=ALU.is_ge, fill=0.0, base=-1,
                               pattern=[[1, P]], channel_multiplier=-1).then_inc(q["const"], 1)
            pool.iota(tokens, [[P, TILES]], base=0, channel_multiplier=1,
                      allow_small_or_imprecise_dtypes=True).then_inc(q["const"], 1)

            def rstd(t, p):
                wait(q["mv"], t + 1, alone=True)
                wait(q["y"], t - 1, alone=True)
                pool.tensor_scalar(r[p], mv[p][:, 1:2], LN_EPS, None, ALU.add).then_inc(q["v"], 1)
                wait(q["v"], t + 1)
                pool.tensor_tensor(r[p], r[p], m.power[:, 0:1], ALU.pow).then_inc(q["r"], 1)

            pipeline(pool, [(rstd, 0)], TILES, 6)

        @block.scalar
        def _(act):
            wait = Waits(act, sem("tick_act"))

            def copy_y(t, p):
                wait(q["T"], t + 1)
                wait(q["G"], t - 1)
                act.activation(yT[p], m.bank(p)[:, 0, 0:D], ACT.Copy).then_inc(q["yT"], 1)

            pipeline(act, [(copy_y, 2)], TILES, 6)
            act.wait_ge(q["b1T"], 1)
            act.activation(m.b1T.rearrange("p e k -> p (e k)"), m.bank(4)[:, 0, 0:NE * HT], ACT.Copy)\
               .then_inc(q["b1T"], 1)
            act.wait_ge(q["soft"], 2)
            act.activation(prob, prob, ACT.Exp).then_inc(q["e"], 1)
            act.wait_ge(q["soft"], 17)
            act.activation(gap, gap, ACT.Exp).then_inc(q["e"], 1)

        @block.tensor
        def _(pe):
            wait = Waits(pe, sem("tick_pe"))
            pe.wait_ge(q["ld"], 64)
            pe.transpose(m.bank(4)[:, 0, 0:NE * HT], b1, m.ident[0:NE * HT, 0:NE * HT]).then_inc(q["b1T"], 1)

            def turn_y(t, p):
                wait(q["y"], t + 1)
                wait(q["yT"], t - 1)
                for k in range(KD):
                    mm = pe.transpose(m.bank(p)[:, 0, k * P:(k + 1) * P],
                                      y[p][:, k * P:(k + 1) * P], m.ident)
                mm.then_inc(q["T"], 1)

            def logits(t, p):
                wait(q["yT"], t + 1)
                wait(q["lg"], t - 1)
                for k in range(KD):
                    mm = pe.matmul(m.bank(2 + p)[:, 0, 0:NE], yT[p][:, k * P:(k + 1) * P], wg[:, k, :],
                                   start=(k == 0), stop=(k == KD - 1))
                mm.then_inc(q["G"], 1)

            pipeline(pe, [(turn_y, 2), (logits, 3)], TILES, 6)
            pe.wait_ge(q["const"], 3)
            pe.wait_ge(q["route"], 2)
            pe.matmul(m.bank(5)[:, 0, 0:TE], upper, both.rearrange("p t e -> p (t e)"), start=True, stop=False)
            for t in range(TILES - 1):
                n = TILES - 1 - t
                mm = pe.matmul(m.bank(5)[:, 0, (t + 1) * NE:TE].rearrange("p (t e) -> p t e", e=NE), ones,
                               both[:, t:t + 1, :].to_broadcast([P, n, NE]), start=False, stop=(t == TILES - 2))
            mm.then_inc(q["pe"], 1)
            pe.matmul(m.bank(6)[:, 0, 0:NE], ones, used, start=True, stop=True).then_inc(q["pe"], 1)
            pe.wait_ge(q["onehot"], 3)
            for n in range(COPIES):
                mm = pe.matmul(m.bank(7)[:, 0, 0:SLOTS], onlane[:, n, :], inslot[:, n, :],
                               start=(n == 0), stop=(n == COPIES - 1))
            mm.then_inc(q["pe"], 1)

        @block.vector
        def _(dve):
            wait = Waits(dve, sem("tick_dve"))
            dve.wait_ge(q["ld"], 64)

            def stats(t, p):
                wait(q["mv"], t - 1, alone=True)
                dve.bn_stats(st[p], tile(m.x, t)).then_inc(q["st"], 1)
                wait(q["st"], t + 1, alone=True)
                wait(q["r"], t - 1, alone=True)
                dve.bn_aggr(mv[p], st[p]).then_inc(q["mv"], 1)

            def norm(t, p):
                wait(q["r"], t + 1)
                wait(q["T"], t - 1)
                wait(st_y[p], t * 8 - p * 8)
                dve.tensor_scalar(y[p], tile(m.x, t), mv[p][:, 0:1], r[p], ALU.subtract, ALU.mult)\
                   .then_inc(q["y"], 1)

            def keep_logits(t, p):
                wait(q["G"], t + 1)
                dve.tensor_tensor(tile(logit, t), m.bank(2 + p)[:, 0, 0:NE], bg, ALU.add).then_inc(q["lg"], 1)

            pipeline(dve, [(norm, 1), (stats, 0), (keep_logits, 3)], TILES, 6)

            dve.wait_ge(q["lg"], TILES)
            dve.tensor_reduce(top, logit, AX.X, ALU.max).then_inc(q["soft"], 1)
            dve.wait_ge(q["soft"], 1)
            dve.tensor_tensor(prob, logit, over_e(top), ALU.subtract).then_inc(q["soft"], 1)
            dve.wait_ge(q["e"], 1)
            dve.tensor_reduce(total, prob, AX.X, ALU.add).then_inc(q["soft"], 1)
            dve.wait_ge(q["soft"], 3)
            dve.reciprocal(inv, total).then_inc(q["soft"], 1)
            dve.wait_ge(q["soft"], 4)
            dve.tensor_tensor(prob, prob, over_e(inv), ALU.mult).then_inc(q["soft"], 1)
            dve.wait_ge(q["soft"], 5)
            dve.tensor_reduce(p1, prob, AX.X, ALU.max).then_inc(q["soft"], 1)
            dve.wait_ge(q["soft"], 6)
            dve.tensor_tensor(cand, prob, over_e(p1), ALU.is_lt).then_inc(q["soft"], 1)
            dve.wait_ge(q["soft"], 7)
            dve.scalar_tensor_tensor(cand, cand, 1000.0, iota_e, ALU.mult, ALU.add).then_inc(q["soft"], 1)
            dve.wait_ge(q["soft"], 8)
            dve.tensor_reduce(i1, cand, AX.X, ALU.min).then_inc(q["soft"], 1)
            dve.wait_ge(q["soft"], 9)
            dve.tensor_tensor(hot[0], iota_e, over_e(i1), ALU.is_equal).then_inc(q["soft"], 1)
            dve.wait_ge(q["soft"], 10)
            dve.scalar_tensor_tensor(prob, hot[0], -2.0, prob, ALU.mult, ALU.add).then_inc(q["soft"], 1)
            dve.wait_ge(q["soft"], 11)
            dve.tensor_reduce(p2, prob, AX.X, ALU.max).then_inc(q["soft"], 1)
            dve.wait_ge(q["soft"], 12)
            dve.tensor_tensor(cand, prob, over_e(p2), ALU.is_lt).then_inc(q["soft"], 1)
            dve.wait_ge(q["soft"], 13)
            dve.scalar_tensor_tensor(cand, cand, 1000.0, iota_e, ALU.mult, ALU.add).then_inc(q["soft"], 1)
            dve.wait_ge(q["soft"], 14)
            dve.tensor_reduce(i2, cand, AX.X, ALU.min).then_inc(q["soft"], 1)
            dve.wait_ge(q["soft"], 15)
            dve.tensor_tensor(hot[1], iota_e, over_e(i2), ALU.is_equal).then_inc(q["soft"], 1)
            dve.tensor_tensor(gap, p2, p1, ALU.subtract).then_inc(q["soft"], 1)
            dve.wait_ge(q["soft"], 16)
            dve.tensor_tensor(both, hot[0], hot[1], ALU.add).then_inc(q["route"], 1)
            dve.wait_ge(q["route"], 1)
            dve.tensor_reduce(used, both.rearrange("p t e -> p e t"), AX.X, ALU.add).then_inc(q["route"], 1)
            dve.wait_ge(q["e"], 2)
            dve.tensor_scalar(den, gap, 1.0, None, ALU.add).then_inc(q["soft"], 1)
            dve.wait_ge(q["soft"], 18)
            dve.reciprocal(m.weight[:, 0, :], den).then_inc(q["soft"], 1)
            dve.wait_ge(q["soft"], 19)
            dve.tensor_tensor(m.weight[:, 1, :], gap, m.weight[:, 0, :], ALU.mult).then_inc(q["soft"], 1)
            dve.wait_ge(q["soft"], 20)
            dve.tensor_scalar(m.weight, m.weight, m.tanh[:, 3:4], None, ALU.mult).then_inc(q["soft"], 1)
            dve.wait_ge(q["pe"], 2)
            dve.tensor_scalar(slots, m.bank(6)[:, 0, 0:NE], 1.0 / P, (P - 1.0) / P - 0.5 + 0.5 / P, ALU.mult,
                              ALU.add).then_inc(q["route"], 1)
            dve.wait_ge(q["route"], 3)
            dve.tensor_scalar(slots, slots, MAGIC, None, ALU.add).then_inc(q["route"], 1)
            dve.wait_ge(q["route"], 4)
            dve.tensor_scalar(slots, slots, MAGIC, None, ALU.subtract).then_inc(q["route"], 1)
            dve.wait_ge(q["route"], 5)
            dve.tensor_tensor_scan(last, ones[:, 0:NE], slots, 0.0, ALU.mult, ALU.add).then_inc(q["route"], 1)
            dve.wait_ge(q["route"], 6)
            dve.tensor_tensor(start, last, slots, ALU.subtract).then_inc(q["route"], 1)
            dve.wait_ge(q["route"], 7)
            dve.scalar_tensor_tensor(place, start.unsqueeze(1).to_broadcast([P, TILES, NE]), float(P),
                                     m.bank(5)[:, 0, 0:TE].rearrange("p (t e) -> p t e", t=TILES),
                                     ALU.mult, ALU.add).then_inc(q["route"], 1)
            dve.wait_ge(q["route"], 8)
            for c in range(2):
                dve.tensor_tensor(picked, place, hot[c], ALU.mult).then_inc(q["route"], 1)
                dve.wait_ge(q["route"], 9 + 2 * c)
                dve.tensor_reduce(where[:, c, :], picked, AX.X, ALU.add).then_inc(q["route"], 1)
                dve.wait_ge(q["route"], 10 + 2 * c)
            dve.tensor_copy(m.place.rearrange("p t c -> p c t"), where).then_inc(q["idx"], 1)
            dve.tensor_scalar(slot, where, 1.0 / P, -0.5 + 0.5 / P, ALU.mult, ALU.add).then_inc(q["route"], 1)
            dve.wait_ge(q["route"], 13)
            dve.tensor_scalar(slot, slot, MAGIC, None, ALU.add).then_inc(q["route"], 1)
            dve.wait_ge(q["route"], 14)
            dve.tensor_scalar(slot, slot, MAGIC, None, ALU.subtract).then_inc(q["route"], 1)
            dve.wait_ge(q["route"], 15)
            dve.scalar_tensor_tensor(lane, slot, -float(P), where, ALU.mult, ALU.add).then_inc(q["route"], 1)
            dve.wait_ge(q["route"], 16)
            flat = lambda x: x.rearrange("p c t -> p (c t)")
            dve.tensor_tensor(onlane, m.iota[:, 0:P].unsqueeze(1).to_broadcast([P, COPIES, P]),
                              flat(lane).unsqueeze(2).to_broadcast([P, COPIES, P]), ALU.is_equal)\
               .then_inc(q["onehot"], 1)
            dve.tensor_tensor(inslot, m.iota[:, 0:SLOTS].unsqueeze(1).to_broadcast([P, COPIES, SLOTS]),
                              flat(slot).unsqueeze(2).to_broadcast([P, COPIES, SLOTS]), ALU.is_equal)\
               .then_inc(q["onehot"], 1)
            dve.wait_ge(q["const"], 3)
            dve.wait_ge(q["onehot"], 2)
            two = inslot.rearrange("p (c t) s -> p c t s", c=2)
            dve.tensor_tensor(two, two, tokens.unsqueeze(1).unsqueeze(3).to_broadcast([P, 2, TILES, SLOTS]),
                              ALU.mult).then_inc(q["onehot"], 1)
            dve.tensor_tensor(past, m.iota[:, 0:SLOTS].unsqueeze(2).to_broadcast([P, SLOTS, NE - 1]),
                              last[:, 0:NE - 1].unsqueeze(1).to_broadcast([P, SLOTS, NE - 1]), ALU.is_ge)\
               .then_inc(q["route"], 1)
            dve.wait_ge(q["route"], 17)
            dve.tensor_reduce(expert, past, AX.X, ALU.add).then_inc(q["route"], 1)
            dve.wait_ge(q["route"], 18)
            dve.tensor_copy(m.expert[:, 0:SLOTS], expert).then_inc(q["idx"], 1)
            dve.wait_ge(q["pe"], 3)
            dve.tensor_copy(m.token[:, 0:SLOTS], m.bank(7)[:, 0, 0:SLOTS]).then_inc(q["idx"], 1)
            dve.wait_ge(q["idx"], 3)


def experts(nc, ctx, m, a):
    def sem(name):
        return ctx.enter_context(nc.semaphore("e_" + name))

    arena = m.arena
    arena.at = m.routed_end
    def pair(cols, dtype=F32):
        return [arena.take(P, cols, dtype) for _ in range(2)]
    col, xs, result = pair(1, U32), pair(D), pair(D)
    xT, h, hT = arena.take(P, D), arena.take(P, HID), arena.take(P, HT * P)
    cols, mine = pair(2, U32), [pair(D), pair(D)]
    w1 = m.early.tensor[:, :].rearrange("p (e k h) -> p e k h", e=NE, k=KD)
    w2 = m.late.tensor[:, :].rearrange("p (e k d) -> p e k d", e=NE, k=HT)
    out_dram = nc.dram_tensor("results_dram", [SLOTS * P, D], F32, kind="Internal").ap()

    q = {n: sem(n) for n in "col xT xTc H h T b hT Y res cols x1 x2".split()}
    ld = [sem(f"ld_rows{p}") for p in range(2)]
    stored = [sem(f"st_result{p}") for p in range(2)]
    fetched = [[sem(f"ld_mine{c}{p}") for p in range(2)] for c in range(2)]
    s_out = sem("st_out")

    h_ps = m.bank(1, 2)
    t_ps = m.bank(3, 2).rearrange("p n (k j) -> p (n k) j", j=P)

    def expert_of(eng, s):
        return eng.value_load(m.expert[0:1, bass.ds(s, 1)], min_val=0, max_val=NE - 1)

    with nc.Block() as block:
        @block.sync
        def _(sp):
            wait = Waits(sp, sem("tick_sp"))

            def store(s, p):
                wait(q["res"], s + 1)
                sp.dma_start(out_dram[bass.ds(s * P, P), :], result[p]).then_inc(stored[p], 16)

            pipeline(sp, [(store, 0)], SLOTS, 6)
            sp.wait_ge(stored[0], 16 * ((SLOTS + 1) // 2))
            sp.wait_ge(stored[1], 16 * (SLOTS // 2))

        @block.gpsimd
        def _(pool):
            wait = Waits(pool, sem("tick_pool"))

            def fetch(s, p):
                wait(q["xT"], s - 1, alone=True)
                pool.tensor_copy(col[p], m.token[:, bass.ds(s, 1)]).then_inc(q["col"], 1)
                wait(q["col"], s + 1, alone=True)
                pool.indirect_dma_start(xs[p], None, m.y_dram, bass.IndirectOffsetOnAxis(ap=col[p], axis=0))\
                    .then_inc(ld[p], 16)

            pipeline(pool, [(fetch, 0)], SLOTS, 6)

        @block.scalar
        def _(act):
            wait = Waits(act, sem("tick_act"))

            def copy_x(s, p):
                wait(q["xT"], s + 1)
                wait(q["H"], s)
                act.activation(xT, m.bank(0)[:, 0, 0:D], ACT.Copy).then_inc(q["xTc"], 1)

            def copy_h(s, p):
                wait(q["H"], s + 1)
                wait(q["T"], s)
                act.activation(h.rearrange("p (n j) -> p n j", n=2), h_ps, ACT.Copy).then_inc(q["h"], 1)

            pipeline(act, [(copy_h, 3), (copy_x, 2)], SLOTS, 6)

        @block.tensor
        def _(pe):
            wait = Waits(pe, sem("tick_pe"))
            pe.wait_ge(m.ld_w1, 16)
            pe.wait_ge(m.ld_w2, 16)
            of = {}

            def load(s, p):
                of[1] = expert_of(pe, s)

            def load2(s, p):
                of[2] = expert_of(pe, s)

            def turn_x(s, p):
                wait(ld[p], s * 8 - p * 8 + 16)
                wait(q["xTc"], s)
                for k in range(KD):
                    mm = pe.transpose(m.bank(0)[:, 0, k * P:(k + 1) * P], xs[p][:, k * P:(k + 1) * P], m.ident)
                mm.then_inc(q["xT"], 1)

            def turn_h(s, p):
                wait(q["h"], s + 1)
                wait(q["b"], s)
                for k in range(HT):
                    mm = pe.transpose(t_ps[:, k, :], h[:, k * P:(k + 1) * P], m.ident)
                mm.then_inc(q["T"], 1)

            def layer1(s, p):
                wait(q["xTc"], s + 1)
                wait(q["h"], s)
                for n in range(2):
                    for k in range(KD):
                        mm = pe.matmul(h_ps[:, n, :], xT[:, k * P:(k + 1) * P],
                                       w1[:, bass.ds(of[1], 1), k, n * 512:(n + 1) * 512]
                                       .rearrange("p e h -> p (e h)"), start=(k == 0), stop=(k == KD - 1))
                mm.then_inc(q["H"], 1)

            def layer2(s, p):
                wait(q["hT"], s + 1)
                wait(q["res"], s)
                for k in range(HT):
                    mm = pe.matmul(m.bank(5)[:, 0, 0:D], hT[:, k * P:(k + 1) * P],
                                   w2[:, bass.ds(of[2], 1), k, :].rearrange("p e d -> p (e d)"),
                                   start=(k == 0), stop=(k == HT - 1))
                mm.then_inc(q["Y"], 1)

            pipeline(pe, [(load, 2), (load2, 3), (turn_x, 2), (turn_h, 3), (layer1, 2), (layer2, 3)], SLOTS, 6)

        @block.vector
        def _(dve):
            wait = Waits(dve, sem("tick_dve"))
            of = {}

            def load(s, p):
                of[0] = expert_of(dve, s)

            def bias(s, p):
                wait(q["T"], s + 1)
                wait(q["Y"], s)
                b1 = m.b1T[:, bass.ds(of[0], 1), :].rearrange("p e k -> p (e k)").unsqueeze(2)
                dve.tensor_tensor(hT.rearrange("p (k j) -> p k j", k=HT), t_ps, b1.to_broadcast([P, HT, P]),
                                  ALU.add).then_inc(q["b"], 1)
                wait(q["b"], s + 1)
                dve.tensor_scalar(hT, hT, 0.0, None, ALU.max).then_inc(q["hT"], 1)

            def keep(s, p):
                wait(q["Y"], s + 1)
                wait(stored[p], s * 8 - p * 8)
                dve.tensor_tensor(result[p], m.bank(5)[:, 0, 0:D],
                                  m.b2[:, bass.ds(of[0], 1), :].rearrange("p e d -> p (e d)"), ALU.add)\
                   .then_inc(q["res"], 1)

            pipeline(dve, [(load, 3), (bias, 3), (keep, 3)], SLOTS, 6)

    out_t = a["out"].rearrange("b (h p) d -> p (b h) d", p=P)

    def work(t):
        return m.x[:, bass.ds(t, 1), :].rearrange("p t d -> p (t d)")

    with nc.Block() as block:
        @block.gpsimd
        def _(pool):
            wait = Waits(pool, sem("tick_pool2"))

            def fetch(t, p):
                wait(q["x2"], t - 1, alone=True)
                pool.tensor_copy(cols[p], m.place[:, bass.ds(t, 1), :].rearrange("p t c -> p (t c)"))\
                    .then_inc(q["cols"], 1)
                wait(q["cols"], t + 1, alone=True)
                for c in range(2):
                    pool.indirect_dma_start(mine[c][p], None, out_dram,
                                            bass.IndirectOffsetOnAxis(ap=cols[p][:, c:c + 1], axis=0))\
                        .then_inc(fetched[c][p], 16)

            pipeline(pool, [(fetch, 0)], TILES, 6)

        @block.vector
        def _(dve):
            wait = Waits(dve, sem("tick_dve2"))

            def add(t, p):
                wait(fetched[0][p], t * 8 - p * 8 + 16)
                dve.scalar_tensor_tensor(work(t), mine[0][p], m.weight[:, 0, bass.ds(t, 1)], work(t), ALU.mult,
                                         ALU.add).then_inc(q["x1"], 1)
                wait(q["x1"], t + 1)
                wait(fetched[1][p], t * 8 - p * 8 + 16)
                dve.scalar_tensor_tensor(work(t), mine[1][p], m.weight[:, 1, bass.ds(t, 1)], work(t), ALU.mult,
                                         ALU.add).then_inc(q["x2"], 1)

            pipeline(dve, [(add, 0)], TILES, 6)

        @block.sync
        def _(sp):
            for n in range(8):
                sp.wait_ge(q["x2"], 2 * n + 2)
                sp.dma_start(out_t[:, 2 * n:2 * n + 2, :], m.x[:, 2 * n:2 * n + 2, :]).then_inc(s_out, 16)
            sp.wait_ge(s_out, 16 * 8)


def build(nc, a):
    with ExitStack() as ctx:
        m = Memory()
        allocate(nc, ctx, m)
        m.ld_attn = ctx.enter_context(nc.semaphore("ld_attn"))
        m.ld_w1 = ctx.enter_context(nc.semaphore("ld_w1"))
        m.ld_w2 = ctx.enter_context(nc.semaphore("ld_w2"))
        before = nc.snapshot_sems()
        align(nc, ctx, m, a)
        ffn(nc, ctx, m, a)
        nc.clear_and_free_semaphores(nc.allocated_since(before))
        nc.all_engine_barrier()
        attention(nc, ctx, m, a)
        route(nc, ctx, m, a)
        experts(nc, ctx, m, a)


_INS = ["x", "ctx_1024", "g_xattn", "g_ffn", "L0_ffn_ln1_g", "L0_ffn_ln1_b", "L0_ffn_w1", "L0_ffn_b1",
        "L0_ffn_ln2_g", "L0_ffn_ln2_b", "L0_ffn_w2", "L0_ffn_b2", "L1_xattn_tab_g", "L1_xattn_tab_b",
        "L1_xattn_vid_g", "L1_xattn_vid_b", "L1_xattn_Wq", "L1_xattn_Wk", "L1_xattn_Wv", "L1_xattn_q_g",
        "L1_xattn_q_b", "L1_xattn_k_g", "L1_xattn_k_b", "L1_xattn_Wo", "L1_xattn_bo", "L1_ffn_W1", "L1_ffn_b1",
        "L1_ffn_W2", "L1_ffn_b2", "L1_ffn_Wg", "L1_ffn_bg"]


def kernel(**inputs):
    import numpy as np
    import concourse.bacc as bacc
    from concourse.bass_utils import run_bass_kernel_spmd

    nc = bacc.Bacc("TRN2", target_bir_lowering=False, num_devices=1)
    arrays, a = {}, {}
    for name in _INS:
        array = np.ascontiguousarray(inputs[name])
        arrays[f"in_{name}_dram"] = array
        a[name] = nc.dram_tensor(f"in_{name}_dram", array.shape, mybir.dt.from_np(array.dtype),
                                 kind="ExternalInput").ap()
    a["out"] = nc.dram_tensor("out_dram", [B, TQ, D], F32, kind="ExternalOutput").ap()
    build(nc, a)
    r = run_bass_kernel_spmd(nc, [arrays], core_ids=[0])
    return r.results[0]["out_dram"]
```

```python
from contextlib import ExitStack

import concourse.bass as bass
from concourse import mybir

F32, F16, BF16 = mybir.dt.float32, mybir.dt.float16, mybir.dt.bfloat16
I32, U32 = mybir.dt.int32, mybir.dt.uint32
ALU = mybir.AluOpType
ACT = mybir.ActivationFunctionType
AX = mybir.AxisListType

P = 128
B, TQ, D = 8, 256, 256
S = 77
TILES = B * TQ // P
KD = D // P
HID = 1024
HT = HID // P
HEADS, DH = 12, 64
INNER = HEADS * DH
PAIRS = INNER // P
NE = 8
LN_EPS = 1e-5
BIG = 1e30
MAGIC = 12582912.0

CH, LAG = 4, 2
CW = TQ // CH
PADR = LAG * (CH - 1)
RING = 12
STEPS = -(-(S + PADR) // RING) * RING
DROWS = PADR + STEPS + (STEPS - S) % 2
GROUP = 4

SLOTS = (2 * B * TQ - NE) // P + NE


class Memory:
    pass


class Region:

    def __init__(self, tensor):
        self.tensor, self.at = tensor, 0

    def take(self, parts, cols, dtype=F32, at=None):
        if at is not None:
            self.at = at
        words = cols if dtype in (F32, I32, U32) else cols // 2
        view = self.tensor[0:parts, self.at:self.at + words]
        self.at += words
        assert self.at <= self.tensor.shape[1], self.at
        return view if dtype == F32 else view.bitcast(dtype)


def bcast(vector, parts):
    return vector.rearrange("(o n) -> o n", o=1).broadcast_to([parts, vector.shape[0]])


def allocate(nc, ctx, m):
    def region(name, cols):
        return Region(ctx.enter_context(nc.sbuf_tensor(name, [P, cols], F32)))

    psum = ctx.enter_context(nc.psum_tensor("banks", [P, 8, 512], F32))
    m.bank = lambda k, n=1: psum[:, k:k + n, :]
    keep = region("keep", 4096 + 2048 + 256 + 2048 + 128 + 256 + 128)
    m.x = keep.take(P, TILES * D).rearrange("p (t d) -> p t d", t=TILES)
    m.ctx = keep.take(S, B * D).rearrange("p (b d) -> p b d", b=B)
    m.w1T = keep.take(P, KD * HID, BF16).rearrange("p (k h) -> p k h", k=KD)
    m.w2T = keep.take(P, HT * D, BF16).rearrange("p (k d) -> p k d", k=HT)
    m.spare = Region(keep.tensor)
    m.spare.at = TILES * D
    m.ident = keep.take(P, P)
    m.identb = keep.take(P, P, BF16)
    m.iota = keep.take(P, TQ)
    m.tanh = keep.take(P, 4)
    m.wscale = keep.take(P, 4)
    m.power = keep.take(P, 32)
    m.power1 = keep.take(P, 2)
    m.vT = keep.take(S, 2 * B).rearrange("p (k b) -> p k b", k=2)
    m.early = region("early", NE * KD * HID)
    m.late = region("late", NE * HT * D)
    m.arena = region("arena", 11200)
    m.kT = m.late.take(P, PAIRS * B * S, at=0).rearrange("p (i b s) -> p i b s", i=PAIRS, b=B)
    m.v = m.late.take(S, B * HEADS * (DH + 1)).rearrange("p (b h e) -> p b h e", b=B, h=HEADS)
    m.wa = m.late.take(P, KD * INNER)
    m.wb = m.late.take(P, KD * INNER)
    m.qg = m.late.take(P, INNER)
    m.qb = m.late.take(P, INNER)
    m.vg = m.late.take(P, D)
    m.vb = m.late.take(P, D)
    m.bo = m.late.take(P, D)


def align(nc, ctx, m, a):
    def sem(name):
        return nc.alloc_semaphore(name)

    dist_dram = nc.dram_tensor("dist_dram", [B, DROWS, TQ], F32, kind="Internal").ap()
    cost_dram = nc.dram_tensor("cost_dram", [CH * B, STEPS, CW], F32, kind="Internal").ap()
    jump_dram = nc.dram_tensor("jump_dram", [B, S, TQ], F16, kind="Internal").ap()

    early, arena = m.early, m.arena
    dist = early.take(CH * B, STEPS * CW, at=0).rearrange("p (t w) -> p t w", t=STEPS)
    xn = early.take(P, TILES * D, at=5376).rearrange("p (t d) -> p t d", t=TILES)
    drow = early.take(S, B * TQ).rearrange("p (b j) -> p b j", b=B)
    xnT = early.take(P, 2 * KD * TQ).rearrange("p (u k j) -> p u k j", u=2, k=KD)
    xsq = early.take(P, 2 * KD * TQ).rearrange("p (u k j) -> p u k j", u=2, k=KD)
    sq = early.take(S, 3 * TQ).rearrange("p (n j) -> p n j", n=3)
    sqjunk = early.take(S, D)
    W1 = TQ + 1
    cost = early.take(S, B * W1, at=0).rearrange("p (b j) -> p b j", b=B)
    above = early.take(S, B * W1).rearrange("p (b j) -> p b j", b=B)
    best = early.take(S, B * TQ).rearrange("p (b j) -> p b j", b=B)
    stay = early.take(S, B * TQ).rearrange("p (b j) -> p b j", b=B)
    turn = early.take(S, B * TQ).rearrange("p (b j) -> p b j", b=B)
    jump = early.take(S, B * TQ).rearrange("p (b j) -> p b j", b=B)
    djump = early.take(S, B * TQ, F16).rearrange("p (b j) -> p b j", b=B)
    djump_b = early.take(B, S * TQ, F16, at=0).rearrange("p (i j) -> p i j", i=S)

    w1s = arena.take(P, HT * D, at=0).rearrange("p (k d) -> p k d", k=HT)
    w2s = arena.take(P, KD * HID).rearrange("p (k h) -> p k h", k=KD)
    wq = arena.take(P, HT * D, BF16)
    ones = arena.take(P, P)
    kvn = arena.take(S, B * D).rearrange("p (b d) -> p b d", b=B)
    kvT = arena.take(P, KD * S).rearrange("p (k s) -> p k s", k=KD)
    kraw = [arena.take(S, INNER), arena.tensor[0:S, 0:INNER]]
    kn = [arena.take(S, INNER), arena.tensor[0:S, INNER:2 * INNER]]
    ring = arena.take(CH * B, RING * (CW + 1)).rearrange("p (r w) -> p r w", r=RING)
    diag = arena.take(CH * B, CW)
    first = arena.take(CH * B, 1)
    floor = arena.take(CH * B, 1)
    shifted = arena.take(CH * B, 2)
    path = arena.take(B, S + 1)
    ctxT = [arena.take(P, KD * S).rearrange("p (k s) -> p k s", k=KD) for _ in range(2)]
    junk = arena.take(P, 4)
    stats = arena.take(P, TILES * 6).rearrange("p (t n) -> p t n", t=TILES)
    mv = arena.take(P, TILES * 2).rearrange("p (t n) -> p t n", t=TILES)
    rstd = arena.take(P, TILES)
    cstats = arena.take(S, B * 6).rearrange("p (t n) -> p t n", t=B)
    cmv = arena.take(S, B * 2).rearrange("p (t n) -> p t n", t=B)
    crstd = arena.take(S, B)
    norm2 = arena.take(S, B)
    ksum = arena.take(S, 5 * B).rearrange("p (n b) -> p n b", n=5)
    wsum = arena.take(P, 2)
    big = arena.take(B, 2 * TQ)

    wk = m.wa.rearrange("p (k n) -> p k n", k=KD)
    wv = m.wb.rearrange("p (k n) -> p k n", k=KD)

    hopjunk = early.take(B, TQ, at=14000)
    NPAD = PADR // 2 + -(-(DROWS - PADR - S) // 2)

    s_x = [sem(f"ld_x{q}") for q in range(4)]
    s_cost = [sem(f"st_cost{g}") for g in range(RING // GROUP)]
    s_ctx, s_gate, s_w12, s_kv, s_kvg = map(sem, "ld_ctx ld_gate ld_w12 ld_kvw ld_kvg".split())
    s_id0, s_const, s_init = map(sem, "ident0 const dtw_init".split())
    s_cst, s_cmv, s_cr, s_st, s_mv, s_r = map(sem, "cstats cmv crstd stats mv rstd".split())
    s_v1, s_v2 = map(sem, "var_eps cvar_eps".split())
    s_xn, s_kvn, s_xT, s_xTc, s_xsq, s_cT, s_cTc, s_aa = map(sem, "xn kvn xT xTcopy xsq cT cTcopy norm2".split())
    s_D, s_a, s_sq, s_rc, s_ar, s_dr = map(sem, "distp dist2 sqrt recip quot drow".split())
    s_pad, s_dst, s_dist = map(sem, "st_pad st_dist ld_dist".split())
    s_min, s_scan, s_shf, s_bnd = map(sem, "dtw_min dtw_scan dtw_shift dtw_left".split())
    s_cl, s_cm, s_F, s_djst, s_djld, s_hop, s_path, s_vT, s_vTc = map(
        sem, "ld_cost cost_big choose st_jump ld_jump hop path0 vT vTcopy".split())
    s_ab, s_tot, s_ws, s_wq, s_wqb, s_wT, s_wTc = map(sem, "wabs wtotal wscale wq wqb wT wTcopy".split())
    s_kg, s_kvb, s_kvTp, s_kvTc, s_k, s_ksum, s_knm, s_kssq, s_kvar, s_krs, s_kbias, s_kn, s_kga, s_kb, s_kTp, s_kTc = map(
        sem, "kvgain kvbias kvT kvTcopy k ksum kmean kssq kvar krstd kbias knorm kgain kaff kTp kTcopy".split())
    s_v, s_vc, s_one, s_th, s_pw = map(sem, "v vcopy vones tanh power".split())

    x_t = a["x"].rearrange("b (h p) d -> p (b h) d", p=P)

    with nc.Block() as block:
        @block.sync
        def _(sp):
            sp.dma_start(m.ctx, a["ctx_1024"].rearrange("b s d -> s b d")).then_inc(s_ctx, 16)
            for q in range(4):
                sp.dma_start(m.x[:, 4 * q:4 * q + 4, :], x_t[:, 4 * q:4 * q + 4, :]).then_inc(s_x[q], 16)
            sp.wait_ge(s_init, 1)
            for r in list(range(0, PADR, 2)):
                sp.dma_start(dist_dram[:, r:r + 2, :], big.rearrange("p (r j) -> p r j", r=2)).then_inc(s_pad, 16)
            for r in range(PADR + S, DROWS, 2):
                r = min(r, DROWS - 2)
                sp.dma_start(dist_dram[:, r:r + 2, :], big.rearrange("p (r j) -> p r j", r=2)).then_inc(s_pad, 16)
            for b in range(B):
                sp.wait_ge(s_dr, b + 1)
                sp.dma_start(dist_dram[b, PADR:PADR + S, :], drow[:, b, :]).then_inc(s_dst, 16)
            sp.wait_ge(s_pad, 16 * NPAD)
            sp.wait_ge(s_dst, 16 * B)
            sp.wait_ge(s_xn, TILES)
            for c in range(CH):
                r = PADR - LAG * c
                sp.dma_start(dist[c * B:(c + 1) * B, :, :],
                             dist_dram[:, r:r + STEPS, c * CW:(c + 1) * CW]).then_inc(s_dist, 16)
            with sp.Fori(0, STEPS // RING) as i:
                for g in range(RING // GROUP):
                    sp.wait_ge(s_scan, i * RING + (g + 1) * GROUP)
                    sp.dma_start(cost_dram[:, bass.ds(i * RING + g * GROUP, GROUP), :],
                                 ring[:, g * GROUP:(g + 1) * GROUP, 1:CW + 1]).then_inc(s_cost[g], 16)
            for g in range(RING // GROUP):
                sp.wait_ge(s_cost[g], 16 * STEPS // RING)
            cost_v = cost_dram.rearrange("(c b) t w -> c t b w", c=CH)
            for c in range(CH):
                lo = 1 + c * CW
                sp.dma_start(cost[:, :, lo:lo + CW], cost_v[c, LAG * c:LAG * c + S]).then_inc(s_cl, 16)
                sp.dma_start(above[1:S, :, lo:lo + CW], cost_v[c, LAG * c:LAG * c + S - 1]).then_inc(s_cl, 16)
            sp.wait_ge(s_F, 7)
            sp.dma_start(jump_dram.rearrange("b i j -> i b j"), djump).then_inc(s_djst, 16)
            sp.wait_ge(s_djst, 16)
            sp.dma_start(djump_b, jump_dram).then_inc(s_djld, 16)

        @block.gpsimd
        def _(pool):
            pool.memset(m.power, -0.5).then_inc(s_pw, 1)
            pool.memset(m.power1, -1.0).then_inc(s_pw, 1)
            pool.memset(m.ident, 0.0).then_inc(s_id0, 1)
            pool.memset(ones, 1.0).then_inc(s_const, 1)
            pool.wait_ge(s_id0, 1)
            pool.affine_select(out=m.ident, in_=m.ident, compare_op=ALU.not_equal, fill=1.0, base=0,
                               pattern=[[-1, P]], channel_multiplier=1).then_inc(s_const, 1)
            pool.iota(m.iota, [[1, TQ]], base=0, channel_multiplier=0,
                      allow_small_or_imprecise_dtypes=True).then_inc(s_const, 1)
            pool.wait_ge(s_const, 3)
            pool.tensor_copy(m.identb, m.ident).then_inc(s_const, 1)
            pool.memset(big, BIG).then_inc(s_init, 1)
            pool.wait_ge(s_pw, 2)
            pool.wait_ge(s_cmv, B)
            pool.tensor_scalar(crstd, cmv[:, :, 1], LN_EPS, None, ALU.add).then_inc(s_v2, 1)
            pool.wait_ge(s_v2, 1)
            pool.tensor_tensor(crstd, crstd, m.power[0:S, 0:B], ALU.pow).then_inc(s_cr, 1)
            for q in range(4):
                t = slice(4 * q, 4 * q + 4)
                pool.wait_ge(s_mv, 4 * q + 4)
                pool.tensor_scalar(rstd[:, t], mv[:, t, 1], LN_EPS, None, ALU.add).then_inc(s_v1, 1)
                pool.wait_ge(s_v1, q + 1)
                pool.tensor_tensor(rstd[:, t], rstd[:, t], m.power[:, 0:4], ALU.pow).then_inc(s_r, 1)
            pool.memset(ring, BIG).then_inc(s_init, 1)
            pool.memset(first, BIG).then_inc(s_init, 1)
            pool.memset(floor, 0.0).then_inc(s_init, 1)
            pool.wait_ge(s_init, 4)
            pool.memset(first[0:B], 0.0).then_inc(s_init, 1)
            pool.memset(floor[0:B], BIG).then_inc(s_init, 1)
            pool.memset(path, float(TQ - 1)).then_inc(s_path, 1)
            pool.wait_ge(s_path, 1)
            pool.memset(path[:, 0:1], 0.0).then_inc(s_hop, 1)
            pool.memset(m.v, 1.0).then_inc(s_one, 1)
            pool.wait_ge(s_kvn, B)
            pool.wait_ge(s_kvg, 64)
            for b in range(B):
                pool.tensor_tensor(kvn[:, b, :], kvn[:, b, :], m.vg[0:S, :], ALU.mult).then_inc(s_kg, 1)
                pool.wait_ge(s_kg, b + 1)
                pool.tensor_tensor(kvn[:, b, :], kvn[:, b, :], m.vb[0:S, :], ALU.add).then_inc(s_kvb, 1)
            pool.wait_ge(s_tot, 1)
            pool.tensor_scalar(m.wscale[:, 0:2], wsum, 1.0 / (HID * D), 1e-5, ALU.mult, ALU.max).then_inc(s_ws, 1)
            pool.wait_ge(s_ws, 1)
            pool.tensor_tensor(m.wscale[:, 2:4], m.wscale[:, 0:2], m.power1, ALU.pow).then_inc(s_ws, 1)
            pool.wait_ge(s_ws, 2)
            for n, w in enumerate((w1s.rearrange("p k d -> p (k d)"), w2s.rearrange("p k h -> p (k h)"))):
                pool.tensor_scalar(w, w, m.wscale[:, 2 + n:3 + n], MAGIC, ALU.mult, ALU.add).then_inc(s_wq, 1)
                pool.wait_ge(s_wq, 2 * n + 1)
                pool.tensor_scalar(w, w, MAGIC, 1.0, ALU.subtract, ALU.min).then_inc(s_wq, 1)
                pool.wait_ge(s_wq, 2 * n + 2)
                if n:
                    pool.wait_ge(s_wT, 3)
                pool.tensor_scalar(wq, w, -1.0, None, ALU.max).then_inc(s_wqb, 1)
            for b in range(B):
                tot, mean, ssq, rs, bias = (ksum[:, n, b:b + 1] for n in range(5))
                pool.wait_ge(s_ksum, b + 1)
                pool.tensor_scalar(mean, tot, -1.0 / INNER, None, ALU.mult).then_inc(s_knm, 1)
                pool.wait_ge(s_kssq, b + 1)
                pool.tensor_scalar(rs, ssq, 1.0 / INNER, LN_EPS, ALU.mult, ALU.add).then_inc(s_kvar, 1)
                pool.wait_ge(s_kvar, b + 1)
                pool.tensor_tensor(rs, rs, m.power[0:S, 0:1], ALU.pow).then_inc(s_krs, 1)
                pool.wait_ge(s_krs, b + 1)
                pool.tensor_tensor(bias, rs, mean, ALU.mult).then_inc(s_kbias, 1)
                pool.wait_ge(s_kn, b + 1)
                k = kn[b % 2]
                pool.tensor_tensor(k, k, m.qg[0:S, :], ALU.mult).then_inc(s_kga, 1)
                pool.wait_ge(s_kga, b + 1)
                pool.tensor_tensor(k, k, m.qb[0:S, :], ALU.add).then_inc(s_kb, 1)

        @block.scalar
        def _(act):
            act.dma_start(junk[:, 0:2], bcast(a["g_xattn"], P)).then_inc(s_gate, 16)
            act.dma_start(junk[:, 2:4], bcast(a["g_ffn"], P)).then_inc(s_gate, 16)
            act.dma_start(w1s, a["L0_ffn_w1"].rearrange("(k p) d -> p k d", p=P)).then_inc(s_w12, 16)
            act.dma_start(w2s, a["L0_ffn_w2"].rearrange("(k p) h -> p k h", p=P)).then_inc(s_w12, 16)
            act.dma_start(m.vg, bcast(a["L1_xattn_tab_g"], P)).then_inc(s_kvg, 16)
            act.dma_start(m.vb, bcast(a["L1_xattn_tab_b"], P)).then_inc(s_kvg, 16)
            act.dma_start(m.qg, bcast(a["L1_xattn_k_g"], P)).then_inc(s_kvg, 16)
            act.dma_start(m.qb, bcast(a["L1_xattn_k_b"], P)).then_inc(s_kvg, 16)
            act.dma_start(wk, a["L1_xattn_Wk"].rearrange("(k p) n -> p k n", p=P)).then_inc(s_kv, 16)
            act.dma_start(wv, a["L1_xattn_Wv"].rearrange("(k p) n -> p k n", p=P)).then_inc(s_kv, 16)
            act.wait_ge(s_gate, 32)
            act.activation(m.tanh, junk, ACT.Tanh).then_inc(s_th, 1)
            act.wait_ge(s_ctx, 16)
            for b in range(B):
                if b:
                    act.wait_ge(s_aa, b)
                act.activation(sqjunk, m.ctx[:, b, :], ACT.Square, accum_out=norm2[:, b:b + 1]).then_inc(s_aa, 1)
            def roots(b):
                act.wait_ge(s_a, b + 1)
                if b:
                    act.wait_ge(s_dr, b)
                act.activation(sq[:, 1, :], sq[:, 0, :], ACT.Sqrt).then_inc(s_sq, 1)
            for b in range(B):
                act.wait_ge(s_xT, b + 1)
                if b >= 2:
                    act.wait_ge(s_D, b - 1)
                bank = m.bank(b % 2)[:, 0, :].rearrange("p (k j) -> p k j", k=KD)
                act.activation(xnT[:, b % 2], bank, ACT.Copy).then_inc(s_xTc, 1)
                act.activation(xsq[:, b % 2], bank, ACT.Square).then_inc(s_xsq, 1)
                if b:
                    roots(b - 1)
            roots(B - 1)
            act.wait_ge(s_w12, 32)
            act.activation(wq[:, 0:HT * D], w1s.rearrange("p k d -> p (k d)"), ACT.Abs,
                           accum_out=wsum[:, 0:1]).then_inc(s_ab, 1)
            act.wait_ge(s_ab, 1)
            act.activation(wq[:, 0:HT * D], w2s.rearrange("p k h -> p (k h)"), ACT.Abs,
                           accum_out=wsum[:, 1:2]).then_inc(s_ab, 1)
            act.wait_ge(s_wT, 1)
            act.activation(wsum, m.bank(7)[:, 0, 0:2], ACT.Copy).then_inc(s_tot, 1)
            for n in range(2):
                for half in range(2):
                    act.wait_ge(s_wT, 2 + 2 * n + half)
                    dst = (m.w1T[:, half, :] if n == 0 else
                           m.w2T[:, 4 * half:4 * half + 4, :].rearrange("p k d -> p (k d)"))
                    act.activation(dst, m.bank(6 + half)[:, 0, :].bitcast(BF16), ACT.Copy).then_inc(s_wTc, 1)
            def keep_keys(b):
                act.wait_ge(s_kTp, b + 1)
                act.activation(m.kT[:, :, b, :], m.bank(4)[:, 0, 0:PAIRS * S].rearrange("p (i s) -> p i s", i=PAIRS),
                               ACT.Copy).then_inc(s_kTc, 1)

            for b in range(B):
                act.wait_ge(s_kvTp, b + 1)
                if b:
                    act.wait_ge(s_v, b)
                act.activation(kvT, m.bank(5)[:, 0, 0:KD * S].rearrange("p (k s) -> p k s", k=KD),
                               ACT.Copy).then_inc(s_kvTc, 1)
                act.wait_ge(s_k, b + 1)
                if b >= 2:
                    act.wait_ge(s_kn, b - 1)
                kp = m.bank(0, 2)[0:S, :, 0:INNER // 2]
                kr = kraw[b % 2].rearrange("p (n j) -> p n j", n=2)
                act.activation(kr, kp, ACT.Identity, accum_out=ksum[:, 0, b:b + 1]).then_inc(s_ksum, 1)
                act.wait_ge(s_v, b + 1)
                if b == 0:
                    act.wait_ge(s_one, 1)
                for n in range(2):
                    act.activation(m.v[:, b, 6 * n:6 * n + 6, 0:DH],
                                   m.bank(2 + n)[0:S, 0, 0:INNER // 2].rearrange("p (h e) -> p h e", e=DH),
                                   ACT.Copy).then_inc(s_vc, 1)
                act.wait_ge(s_knm, b + 1)
                act.wait_ge(s_ksum, b + 1)
                if b >= 2:
                    act.wait_ge(s_kTp, b - 1)
                act.activation(kn[b % 2], kraw[b % 2], ACT.Square, bias=ksum[:, 1, b:b + 1],
                               accum_out=ksum[:, 2, b:b + 1]).then_inc(s_kssq, 1)
                act.wait_ge(s_kbias, b + 1)
                act.wait_ge(s_kssq, b + 1)
                act.activation(kn[b % 2], kraw[b % 2], ACT.Identity, bias=ksum[:, 4, b:b + 1],
                               scale=ksum[:, 3, b:b + 1]).then_inc(s_kn, 1)
                if b:
                    keep_keys(b - 1)
            keep_keys(B - 1)
            act.wait_ge(s_vT, 1)
            act.activation(m.vT, m.bank(7)[0:S, 0, 0:2 * B].rearrange("p (k b) -> p k b", k=2),
                           ACT.Copy).then_inc(s_vTc, 1)

        @block.tensor
        def _(pe):
            pe.wait_ge(s_const, 4)
            pe.wait_ge(s_ctx, 16)
            def turn_inputs(b):
                if b >= 2:
                    pe.wait_ge(s_cTc, b - 1)
                for k in range(KD):
                    mm = pe.transpose(m.bank(2 + b % 2)[:, 0, k * S:(k + 1) * S],
                                      m.ctx[:, b, k * P:(k + 1) * P], m.ident[0:S, 0:S])
                mm.then_inc(s_cT, 1)
                pe.wait_ge(s_xn, 2 * b + 2)
                if b >= 2:
                    pe.wait_ge(s_xsq, b - 1)
                for h in range(2):
                    for k in range(KD):
                        mm = pe.transpose(m.bank(b % 2)[:, 0, k * TQ + h * P:k * TQ + (h + 1) * P],
                                          xn[:, 2 * b + h, k * P:(k + 1) * P], m.ident)
                mm.then_inc(s_xT, 1)

            turn_inputs(0)
            for b in range(B):
                if b + 1 < B:
                    turn_inputs(b + 1)
                pe.wait_ge(s_cTc, b + 1)
                pe.wait_ge(s_xTc, b + 1)
                if b >= 2:
                    pe.wait_ge(s_a, b - 1)
                out = m.bank(4 + b % 2)[0:S, 0, 0:TQ]
                for k in range(KD):
                    pe.matmul(out, ctxT[b % 2][:, k, :], xnT[:, b % 2, k, :], start=(k == 0), stop=False)
                pe.wait_ge(s_xsq, b + 1)
                for k in range(KD):
                    mm = pe.matmul(out, ones[:, 0:S], xsq[:, b % 2, k, :], start=False, stop=(k == KD - 1))
                mm.then_inc(s_D, 1)
            pe.wait_ge(s_ab, 2)
            pe.matmul(m.bank(7)[:, 0, 0:2], ones, wsum, start=True, stop=True).then_inc(s_wT, 1)
            for n in range(2):
                pe.wait_ge(s_wqb, n + 1)
                src = wq.rearrange("p (k d) -> p k d", k=HT) if n == 0 else wq.rearrange("p (k h) -> p k h", k=KD)
                for half in range(2):
                    if n == 0 and half:
                        pe.wait_ge(s_tot, 1)
                    if n:
                        pe.wait_ge(s_wTc, half + 1)
                    bank = m.bank(6 + half)[:, 0, :].bitcast(BF16)
                    for k in range(8):
                        if n == 0:
                            out, in_ = bank[:, k * P:(k + 1) * P], src[:, k, half * P:(half + 1) * P]
                        else:
                            tile = 4 * half + k // 2
                            out = bank[:, k * P:(k + 1) * P]
                            in_ = src[:, k % 2, tile * P:(tile + 1) * P]
                        mm = pe.transpose(out, in_, m.identb)
                    mm.then_inc(s_wT, 1)
            def turn_keys(b):
                pe.wait_ge(s_kb, b + 1)
                if b:
                    pe.wait_ge(s_kTc, b)
                for i in range(PAIRS):
                    mm = pe.transpose(m.bank(4)[:, 0, i * S:(i + 1) * S], kn[b % 2][:, i * P:(i + 1) * P],
                                      m.ident[0:S, 0:S])
                mm.then_inc(s_kTp, 1)

            pe.wait_ge(s_kv, 32)
            for b in range(B):
                pe.wait_ge(s_kvb, b + 1)
                if b:
                    pe.wait_ge(s_kvTc, b)
                for k in range(KD):
                    mm = pe.transpose(m.bank(5)[:, 0, k * S:(k + 1) * S], kvn[:, b, k * P:(k + 1) * P],
                                      m.ident[0:S, 0:S])
                mm.then_inc(s_kvTp, 1)
                pe.wait_ge(s_kvTc, b + 1)
                for w, bank, done, read in ((wk, 0, s_k, s_ksum), (wv, 2, s_v, s_vc)):
                    if b:
                        pe.wait_ge(read, b if read is s_ksum else 2 * b)
                    for n in range(2):
                        for k in range(KD):
                            mm = pe.matmul(m.bank(bank + n)[0:S, 0, 0:INNER // 2], kvT[:, k, :],
                                           w[:, k, n * INNER // 2:(n + 1) * INNER // 2],
                                           start=(k == 0), stop=(k == KD - 1))
                    mm.then_inc(done, 1)
                if b:
                    turn_keys(b - 1)
            turn_keys(B - 1)
            pe.wait_ge(s_hop, S)
            pe.wait_ge(s_wTc, 4)
            for k in range(2):
                mm = pe.transpose(m.bank(7)[0:S, 0, k * B:(k + 1) * B], path[:, k:k + S], m.ident[0:B, 0:B])
            mm.then_inc(s_vT, 1)

        @block.vector
        def _(dve):
            dve.wait_ge(s_ctx, 16)
            for b in range(B):
                dve.bn_stats(cstats[:, b, :], m.ctx[:, b, :]).then_inc(s_cst, 1)
            for b in range(B):
                dve.wait_ge(s_cst, b + 1)
                dve.bn_aggr(cmv[:, b, :], cstats[:, b, :]).then_inc(s_cmv, 1)
            for q in range(4):
                dve.wait_ge(s_x[q], 16)
                for t in range(4 * q, 4 * q + 4):
                    dve.bn_stats(stats[:, t, :], m.x[:, t, :]).then_inc(s_st, 1)
                for t in range(4 * q, 4 * q + 4):
                    dve.wait_ge(s_st, t + 1)
                    dve.bn_aggr(mv[:, t, :], stats[:, t, :]).then_inc(s_mv, 1)
            dve.wait_ge(s_const, 4)
            def transposed_context(b):
                dve.wait_ge(s_cT, b + 1)
                if b >= 2:
                    dve.wait_ge(s_D, b - 1)
                dve.tensor_scalar(ctxT[b % 2], m.bank(2 + b % 2)[:, 0, 0:KD * S].rearrange("p (k s) -> p k s", k=KD),
                                  -2.0, None, ALU.mult).then_inc(s_cTc, 1)
            for q in range(4):
                dve.wait_ge(s_r, q + 1)
                for t in range(4 * q, 4 * q + 4):
                    dve.tensor_scalar(xn[:, t, :], m.x[:, t, :], mv[:, t, 0:1], rstd[:, t:t + 1],
                                      ALU.subtract, ALU.mult).then_inc(s_xn, 1)
            dve.wait_ge(s_cr, 1)
            for b in range(B):
                dve.tensor_scalar(kvn[:, b, :], m.ctx[:, b, :], cmv[:, b, 0:1], crstd[:, b:b + 1],
                                  ALU.subtract, ALU.mult).then_inc(s_kvn, 1)
            dve.wait_ge(s_aa, B)
            transposed_context(0)
            for b in range(B):
                if b + 1 < B:
                    transposed_context(b + 1)
                dve.wait_ge(s_D, b + 1)
                if b:
                    dve.wait_ge(s_dr, b)
                dve.tensor_scalar(sq[:, 0, :], m.bank(4 + b % 2)[0:S, 0, 0:TQ], norm2[:, b:b + 1], 1e-30,
                                  ALU.add, ALU.max).then_inc(s_a, 1)
                dve.wait_ge(s_sq, b + 1)
                dve.reciprocal(sq[:, 2, :], sq[:, 1, :]).then_inc(s_rc, 1)
                dve.wait_ge(s_rc, b + 1)
                dve.wait_ge(s_a, b + 1)
                dve.tensor_tensor(sq[:, 0, :], sq[:, 0, :], sq[:, 2, :], ALU.mult).then_inc(s_ar, 1)
                dve.wait_ge(s_ar, b + 1)
                dve.tensor_tensor(drow[:, b, :], sq[:, 0, :], sq[:, 1, :], ALU.add).then_inc(s_dr, 1)

            dve.wait_ge(s_init, 6)
            dve.wait_ge(s_dist, 16 * CH)
            to_right = [(p - B) % (CH * B) for p in range(CH * B)]

            def step(base, u, turn_no=0):
                t = base + u
                start = isinstance(base, int) and u == 0
                prev, row = ring[:, (u - 1) % RING, :], ring[:, u, :]
                if not start:
                    dve.wait_ge(s_scan, t)
                    if not (isinstance(base, int) and u < 3):
                        dve.wait_ge(s_bnd, t - 2)
                dve.tensor_tensor(diag, prev[:, 1:CW + 1], prev[:, 0:CW], ALU.min).then_inc(s_min, 1)
                if not start:
                    dve.stream_shuffle(shifted[:, u % 2:u % 2 + 1], prev[:, CW:CW + 1], to_right).then_inc(s_shf, 1)
                dve.wait_ge(s_min, t + 1)
                if not (isinstance(base, int) and u < 2):
                    dve.wait_ge(s_bnd, t - 1)
                if u % GROUP == 0 and not isinstance(base, int):
                    dve.wait_ge(s_cost[u // GROUP], 16 * turn_no)
                dve.tensor_tensor_scan(row[:, 1:CW + 1], diag, dist[:, bass.ds(t, 1), :].rearrange("p t w -> p (t w)"),
                                       first if start else row[:, 0:1], ALU.min, ALU.add).then_inc(s_scan, 1)
                if not start:
                    dve.wait_ge(s_shf, t)
                    dve.tensor_tensor(ring[:, (u + 1) % RING, 0:1], shifted[:, u % 2:u % 2 + 1], floor, ALU.max).then_inc(s_bnd, 1)

            for u in range(RING):
                step(0, u)
            with dve.Fori(1, STEPS // RING) as turn_no:
                for u in range(RING):
                    step(turn_no * RING, u, turn_no)

            for g in range(RING // GROUP):
                dve.wait_ge(s_cost[g], 16 * STEPS // RING)
            for buf in (cost, above):
                dve.memset(buf[:, :, 0:1], BIG).then_inc(s_cm, 1)
            dve.memset(above[0:1, :, 1:W1], BIG).then_inc(s_cm, 1)
            dve.wait_ge(s_cm, 3)
            dve.wait_ge(s_cl, 32 * CH)
            up, corner, left = above[:, :, 1:W1], above[:, :, 0:TQ], cost[:, :, 0:TQ]
            iota_b = m.iota[0:S, :].unsqueeze(1).to_broadcast([S, B, TQ])
            dve.tensor_tensor(best, up, corner, ALU.min).then_inc(s_F, 1)
            dve.tensor_tensor(turn, corner, up, ALU.is_le).then_inc(s_F, 1)
            dve.wait_ge(s_F, 1)
            dve.tensor_tensor(stay, left, best, ALU.is_ge).then_inc(s_F, 1)
            dve.wait_ge(s_F, 2)
            dve.scalar_tensor_tensor(turn, turn, -0.75, iota_b, ALU.mult, ALU.add).then_inc(s_F, 1)
            dve.wait_ge(s_F, 4)
            dve.tensor_tensor(turn, turn, stay, ALU.mult).then_inc(s_F, 1)
            dve.wait_ge(s_F, 5)
            for b in range(B):
                scan = dve.tensor_tensor_scan(jump[:, b, :], turn[:, b, :], turn[:, b, :], 0.0, ALU.max, ALU.max)
            scan.then_inc(s_F, 1)
            dve.wait_ge(s_F, 6)
            dve.tensor_copy(djump[:, :, 0:1], jump[:, :, 0:1]).then_inc(s_cm, 1)
            dve.tensor_tensor(djump[:, :, 1:TQ], jump[:, :, 1:TQ], jump[:, :, 0:TQ - 1], ALU.subtract)\
               .then_inc(s_F, 1)
            dve.wait_ge(s_djld, 16)
            HOPS = 4
            with dve.Fori(0, (S - 1) // HOPS) as n:
                for u in range(HOPS):
                    here = n * -HOPS + (S - 1 - u)
                    dve.wait_ge(s_hop, n * HOPS + (u + 1))
                    dve.scalar_tensor_tensor(hopjunk, m.iota[0:B, :], path[:, bass.ds(here + 1, 1)],
                                             djump_b[:, bass.ds(here, 1), :].rearrange("p i j -> p (i j)"),
                                             ALU.is_le, ALU.mult,
                                             accum_out=path[:, bass.ds(here, 1)]).then_inc(s_hop, 1)


def pipeline(eng, stages, count, head):
    assert head % 2 == 0
    depth = max(lag for _, lag in stages)

    def turn(k):
        for stage, lag in stages:
            if 0 <= k - lag < count:
                stage(k - lag, (k - lag) % 2)

    for k in range(head):
        turn(k)
    tail = max(head, (count - 2) // 2 * 2)
    if head < tail:
        with eng.Fori(head // 2, tail // 2) as i:
            for u in range(2):
                for stage, lag in stages:
                    stage(i * 2 + (u - lag), (u - lag) % 2)
    for k in range(tail, count + depth):
        turn(k)


class Waits:

    def __init__(self, eng, tick):
        self.eng, self.tick = eng, tick

    def __call__(self, sem, n, alone=False):
        if isinstance(n, int):
            if n > 0:
                self.eng.wait_ge(sem, n)
        else:
            self.eng.wait_ge(sem, n)
            if alone:
                self.eng.sem_inc(self.tick, 1)


def ffn(nc, ctx, m, a):
    def sem(name):
        return nc.alloc_semaphore("f_" + name)

    arena = m.arena
    b1 = arena.take(P, HID, at=0)
    g2, c2 = arena.take(P, HID), arena.take(P, HID)
    g1, c1, b2 = (arena.take(P, D) for _ in range(3))
    def pair(cols, dtype=F32, parts=P):
        return [arena.take(parts, cols, dtype) for _ in range(2)]
    h, hq, hqT = pair(D), pair(D, BF16), arena.take(P, D, BF16)
    z, w, zq, zqT = pair(HID), pair(HID), pair(HID, BF16), arena.take(P, HID, BF16)
    out1 = arena.take(P, D)
    mask = m.late.take(S, TQ)
    half_mask = m.late.take(S, TQ)
    junk = m.late.take(P, HID, BF16)
    st1, mv1, r1, am1, inv1, sc1, f1 = pair(6), pair(2), pair(1), pair(1), pair(1), pair(1), pair(1)
    sum2, neg2, sq2, r2, am2, inv2, sc2, f2 = (pair(1) for _ in range(8))
    magic, unmagic = arena.take(P, 1), arena.take(P, 1)

    HEAD = 8

    names = ("ld start go mhalf mask E x1 st1 mv1 v1 r1 t1 h am1 inv1 sc1 f1 hr hq T1 hqT Z z g neg2 sq2 v2 r2 "
             "t2 n2 h2 am2 inv2 sc2 f2 zr zq T2 zqT Y y x2").split()
    q = {n: sem(n) for n in names}

    def work(t):
        return m.x[:, bass.ds(t, 1), :].rearrange("p t d -> p (t d)")

    with nc.Block() as block:
        @block.sync
        def _(sp):
            for dst, src in ((b1, a["L0_ffn_b1"]), (g2, a["L0_ffn_ln2_g"]), (c2, a["L0_ffn_ln2_b"]), (g1, a["L0_ffn_ln1_g"]),
                             (c1, a["L0_ffn_ln1_b"]), (b2, a["L0_ffn_b2"])):
                sp.dma_start(dst, bcast(src, P)).then_inc(q["ld"], 16)
            sp.dma_start(m.wa.rearrange("p (k n) -> p k n", k=KD),
                         a["L1_xattn_Wq"].rearrange("(k p) n -> p k n", p=P)).then_inc(m.ld_attn, 16)
            sp.dma_start(m.wb.rearrange("p (k n) -> p k n", k=PAIRS),
                         a["L1_xattn_Wo"].rearrange("(k p) n -> p k n", p=P)).then_inc(m.ld_attn, 16)
            for dst, src in ((m.qg, a["L1_xattn_q_g"]), (m.qb, a["L1_xattn_q_b"]), (m.vg, a["L1_xattn_vid_g"]),
                             (m.vb, a["L1_xattn_vid_b"]), (m.bo, a["L1_xattn_bo"])):
                sp.dma_start(dst, bcast(src, P)).then_inc(m.ld_attn, 16)
            sp.dma_start(m.early.tensor[:, :].rearrange("p (e k h) -> p e k h", e=NE, k=KD),
                         a["L1_ffn_W1"].rearrange("e (k p) h -> p e k h", p=P)).then_inc(m.ld_w1, 16)

        @block.gpsimd
        def _(pool):
            wait = Waits(pool, sem("tick_pool"))
            pool.memset(magic, MAGIC).then_inc(q["start"], 1)
            pool.memset(unmagic, -MAGIC).then_inc(q["start"], 1)

            def rstd1(t, p):
                wait(q["mv1"], t + 1, alone=True)
                wait(q["h"], t - 1, alone=True)
                pool.tensor_scalar(r1[p], mv1[p][:, 1:2], 1.0 + LN_EPS, LN_EPS * LN_EPS, ALU.mult,
                                   ALU.add).then_inc(q["v1"], 1)
                wait(q["v1"], t + 1)
                pool.tensor_tensor(r1[p], r1[p], m.power[:, 0:1], ALU.pow).then_inc(q["r1"], 1)

            def mean2(t, p):
                wait(q["g"], t + 1, alone=True)
                wait(q["t2"], t - 1, alone=True)
                pool.tensor_scalar(neg2[p], sum2[p], -1.0 / HID, None, ALU.mult).then_inc(q["neg2"], 1)

            def rstd2(t, p):
                wait(q["sq2"], t + 1, alone=True)
                wait(q["t2"], t - 1, alone=True)
                pool.tensor_scalar(r2[p], sq2[p], 1.0 / HID, LN_EPS, ALU.mult, ALU.add).then_inc(q["v2"], 1)
                wait(q["v2"], t + 1)
                pool.tensor_tensor(r2[p], r2[p], m.power[:, 0:1], ALU.pow).then_inc(q["r2"], 1)

            def affine2(t, p):
                wait(q["t2"], t + 1)
                pool.tensor_tensor(w[p], w[p], g2, ALU.mult).then_inc(q["n2"], 1)
                wait(q["n2"], t + 1)
                pool.tensor_tensor(w[p], w[p], c2, ALU.add).then_inc(q["h2"], 1)

            pipeline(pool, [(mean2, 3), (rstd2, 3), (rstd1, 0), (affine2, 4)], TILES, HEAD)

        @block.scalar
        def _(act):
            wait = Waits(act, sem("tick_act"))

            act.wait_ge(q["start"], 2)

            def scale1(t, p):
                wait(q["sc1"], t + 1)
                act.activation(h[p], h[p], ACT.Identity, bias=magic, scale=sc1[p]).then_inc(q["hr"], 1)

            def round1(t, p):
                wait(q["hr"], t + 1)
                wait(q["T1"], t - 1)
                act.activation(hq[p], h[p], ACT.Identity, bias=unmagic).then_inc(q["hq"], 1)

            def copy1(t, p):
                wait(q["T1"], t + 1)
                wait(q["Z"], t)
                act.activation(hqT, m.bank(1)[:, 0, 0:P].bitcast(BF16), ACT.Copy)\
                   .then_inc(q["hqT"], 1)

            def gelu(t, p):
                wait(q["z"], t + 1)
                wait(q["neg2"], t - 1)
                act.activation(z[p], z[p], ACT.Gelu, accum_out=sum2[p]).then_inc(q["g"], 1)

            def square(t, p):
                wait(q["neg2"], t + 1)
                wait(q["v2"], t - 1)
                wait(q["sq2"], t)
                act.activation(junk, z[p], ACT.Square, bias=neg2[p], accum_out=sq2[p]).then_inc(q["sq2"], 1)

            def scale2(t, p):
                wait(q["sc2"], t + 1)
                act.activation(w[p], w[p], ACT.Identity, bias=magic, scale=sc2[p]).then_inc(q["zr"], 1)

            def round2(t, p):
                wait(q["zr"], t + 1)
                wait(q["T2"], t - 1)
                act.activation(zq[p], w[p], ACT.Identity, bias=unmagic).then_inc(q["zq"], 1)

            def copy2(t, p):
                wait(q["T2"], t + 1)
                wait(q["Y"], t)
                act.activation(zqT, m.bank(6)[:, 0, :].bitcast(BF16), ACT.Copy).then_inc(q["zqT"], 1)

            pipeline(act, [(copy1, 2), (copy2, 6), (gelu, 3), (scale1, 1), (round1, 1), (square, 3), (scale2, 5),
                           (round2, 5)], TILES, HEAD)

        @block.tensor
        def _(pe):
            wait = Waits(pe, sem("tick_pe"))

            def aligned(t, p):
                b = t // 2 if isinstance(t, int) else (t - p) // 2
                wait(q["mask"], (t // 2 if isinstance(t, int) else b) + 1)
                wait(q["x1"], t)
                pe.matmul(m.bank(0)[:, 0, 0:D], mask[:, p * P:(p + 1) * P],
                          m.ctx[:, bass.ds(b, 1), :].rearrange("s b d -> s (b d)"), start=True, stop=True)\
                  .then_inc(q["E"], 1)

            def turn1(t, p):
                wait(q["hq"], t + 1)
                wait(q["hqT"], t)
                for k in range(KD):
                    mm = pe.transpose(m.bank(1)[:, 0, k * 64:(k + 1) * 64].bitcast(BF16),
                                      hq[p][:, k * P:(k + 1) * P], m.identb)
                mm.then_inc(q["T1"], 1)

            def up(t, p):
                wait(q["hqT"], t + 1)
                wait(q["z"], t - 1)
                for n in range(2):
                    for k in range(KD):
                        mm = pe.matmul(m.bank(2 + 2 * p + n)[:, 0, :], hqT[:, k * P:(k + 1) * P],
                                       m.w1T[:, k, n * 512:(n + 1) * 512], start=(k == 0), stop=(k == KD - 1))
                mm.then_inc(q["Z"], 1)

            def turn2(t, p):
                wait(q["zq"], t + 1)
                wait(q["zqT"], t)
                for k in range(HT):
                    mm = pe.transpose(m.bank(6)[:, 0, k * 64:(k + 1) * 64].bitcast(BF16),
                                      zq[p][:, k * P:(k + 1) * P], m.identb)
                mm.then_inc(q["T2"], 1)

            def down(t, p):
                wait(q["zqT"], t + 1)
                wait(q["y"], t)
                for k in range(HT):
                    mm = pe.matmul(m.bank(7)[:, 0, 0:D], zqT[:, k * P:(k + 1) * P],
                                   m.w2T[:, k, :], start=(k == 0), stop=(k == HT - 1))
                mm.then_inc(q["Y"], 1)

            pipeline(pe, [(aligned, 0), (turn1, 2), (turn2, 6), (up, 2), (down, 6)], TILES, HEAD)

        @block.vector
        def _(dve):
            wait = Waits(dve, sem("tick_dve"))
            dve.wait_ge(q["ld"], 96)

            def path_mask(b):
                v0, v1 = (m.vT[:, k, bass.ds(b, 1)] for k in range(2))
                wait(q["mask"], b)
                dve.tensor_scalar(half_mask, m.iota[0:S, :], v0, None, ALU.is_ge).then_inc(q["mhalf"], 1)
                wait(q["mhalf"], b + 1)
                dve.scalar_tensor_tensor(mask, m.iota[0:S, :], v1, half_mask, ALU.is_le, ALU.mult)\
                   .then_inc(q["mask"], 1)

            def next_mask(t, p):
                if p and not (isinstance(t, int) and t == TILES - 1):
                    wait(q["E"], t + 1)
                    path_mask((t + 1) // 2)

            def add_aligned(t, p):
                wait(q["E"], t + 1)
                dve.scalar_tensor_tensor(work(t), m.bank(0)[:, 0, 0:D], m.tanh[:, 0:1], work(t),
                                         ALU.mult, ALU.add).then_inc(q["x1"], 1)
                wait(q["x1"], t + 1, alone=True)
                dve.bn_stats(st1[p], work(t)).then_inc(q["st1"], 1)
                wait(q["st1"], t + 1, alone=True)
                wait(q["r1"], t - 1, alone=True)
                dve.bn_aggr(mv1[p], st1[p]).then_inc(q["mv1"], 1)

            def quant(t, p, k, am, inv, sc, f, src, wscale):
                dve.tensor_reduce(am[p], src, AX.X, ALU.max, apply_absolute_value=True).then_inc(q["am" + k], 1)
                wait(q["am" + k], t + 1)
                dve.tensor_scalar(inv[p], am[p], 1e-5, 1.0 / 127.0, ALU.max, ALU.mult).then_inc(q["inv" + k], 1)
                wait(q["inv" + k], t + 1)
                dve.reciprocal(sc[p], inv[p]).then_inc(q["sc" + k], 1)
                dve.tensor_tensor(f[p], inv[p], wscale, ALU.mult).then_inc(q["f" + k], 1)

            def norm1(t, p):
                wait(q["r1"], t + 1)
                wait(q["hq"], t - 1)
                wait(q["z"], t - 1)
                dve.scalar_tensor_tensor(h[p], work(t), mv1[p][:, 0:1], g1, ALU.subtract, ALU.mult)\
                   .then_inc(q["t1"], 1)
                wait(q["t1"], t + 1)
                dve.scalar_tensor_tensor(h[p], h[p], r1[p], c1, ALU.mult, ALU.add).then_inc(q["h"], 1)
                wait(q["h"], t + 1)
                quant(t, p, "1", am1, inv1, sc1, f1, h[p], m.wscale[:, 0:1])

            def hidden(t, p):
                wait(q["Z"], t + 1)
                wait(q["f1"], t + 1)
                wait(q["t2"], t - 1)
                dve.scalar_tensor_tensor(z[p], m.bank(2 + 2 * p, 2).rearrange("p n j -> p (n j)"), f1[p], b1,
                                         ALU.mult, ALU.add).then_inc(q["z"], 1)

            def center2(t, p):
                wait(q["neg2"], t + 1)
                wait(q["sq2"], t + 1)
                wait(q["zq"], t - 1)
                wait(q["r2"], t + 1)
                dve.tensor_scalar(w[p], z[p], neg2[p], r2[p], ALU.add, ALU.mult).then_inc(q["t2"], 1)

            def range2(t, p):
                wait(q["h2"], t + 1)
                wait(q["f2"], t - 1)
                quant(t, p, "2", am2, inv2, sc2, f2, w[p], m.wscale[:, 1:2])

            def add_out(t, p):
                wait(q["Y"], t + 1)
                wait(q["f2"], t + 1)
                wait(q["x2"], t)
                dve.scalar_tensor_tensor(out1, m.bank(7)[:, 0, 0:D], f2[p], b2,
                                         ALU.mult, ALU.add).then_inc(q["y"], 1)
                wait(q["y"], t + 1)
                dve.scalar_tensor_tensor(work(t), out1, m.tanh[:, 2:3], work(t), ALU.mult, ALU.add)\
                   .then_inc(q["x2"], 1)

            path_mask(0)
            pipeline(dve, [(hidden, 3), (norm1, 1), (center2, 4), (add_aligned, 0), (next_mask, 0), (range2, 5),
                           (add_out, 6)], TILES, HEAD)


def cap(n):
    return min(n, TILES) if isinstance(n, int) else n


def attention(nc, ctx, m, a):
    def sem(name):
        return ctx.enter_context(nc.semaphore("a_" + name))

    arena = m.arena
    arena.at = 0
    def pair(cols):
        return [arena.take(P, cols) for _ in range(2)]
    h, hT = arena.take(P, D), arena.take(P, D)
    qn, qT, prob, o, oT = pair(INNER), pair(INNER), pair(HEADS * S), pair(INNER), pair(INNER)
    pT = arena.take(S, HEADS * P).rearrange("s (h j) -> s h j", h=HEADS)
    kb = arena.take(P, PAIRS * S).rearrange("p (i s) -> p i s", i=PAIRS)
    out1 = arena.take(P, D)
    st, mv, r = pair(6), pair(2), pair(1)
    spare = m.spare
    m.b2 = spare.take(P, NE * D).rearrange("p (e d) -> p e d", e=NE)
    m.logit = spare.take(P, TILES * NE).rearrange("p (t e) -> p t e", t=TILES)
    m.b1 = spare.take(NE * HT, P)
    wg = spare.take(P, KD * NE).rearrange("p (k e) -> p k e", k=KD)
    bg = spare.take(P, NE)
    y, yT = ([spare.take(P, D) for _ in range(2)] for _ in range(2))
    sty, mvy, ry = ([spare.take(P, n) for _ in range(2)] for n in (6, 2, 1))
    m.y_dram = nc.dram_tensor("y_dram", [TILES * P, D], F32, kind="Internal").ap()
    stq, mvq, rq, top, rden = pair(12), pair(2), pair(1), arena.take(P, HEADS), arena.take(P, HEADS)
    wq = m.wa.rearrange("p (k n) -> p k n", k=KD)
    wo = m.wb.rearrange("p (i n) -> p i n", i=PAIRS)
    HALF = INNER // 2
    HEAD = 10

    names = ("st mv v r t1 h xT hT q stq mvq vq rq qg qn qT qTc kb S top sub exp PT PTc PV rden o oT oTc out o1 x3 "
             "qscale ldg sty mvy vy ry y yp yT G lg").split()
    q = {n: sem(n) for n in names}
    st_y = [sem(f"st_y{p}") for p in range(2)]

    s_ps = m.bank(0, 2)[:, :, 0:HEADS // 2 * S]
    q_ps = m.bank(2, 2)[:, :, 0:HALF]
    t_ps = m.bank(4, 2)[:, :, 0:HALF]
    p_ps = m.bank(6, 2)[:, :, 0:HALF]
    PVW = DH + 1
    pv_ps = [m.bank(3)[:, 0, 0:6 * PVW].rearrange("p (h e) -> p h e", h=6),
             m.bank(2)[:, 0, 0:6 * PVW].rearrange("p (h e) -> p h e", h=6)]

    def work(t):
        return m.x[:, bass.ds(t, 1), :].rearrange("p t d -> p (t d)")

    def halves(x):
        return x.rearrange("p (n c) -> p n c", n=2)

    def tile(x, t):
        return x[:, bass.ds(t, 1), :].rearrange("p t d -> p (t d)")

    with nc.Block() as block:
        @block.sync
        def _(sp):
            wait = Waits(sp, sem("tick_sp"))
            for dst, src in ((wg, a["L1_ffn_Wg"].rearrange("(k p) e -> p k e", p=P)), (bg, bcast(a["L1_ffn_bg"], P)),
                             (m.b1, a["L1_ffn_b1"].rearrange("e (k p) -> (e k) p", p=P)),
                             (m.b2.rearrange("p e d -> p (e d)"), bcast(a["L1_ffn_b2"].rearrange("e d -> (e d)"), P))):
                sp.dma_start(dst, src).then_inc(q["ldg"], 16)

            def store(t, p):
                wait(q["y"], t + 1)
                sp.dma_start(m.y_dram[bass.ds(t * P, P), :], y[p]).then_inc(st_y[p], 16)

            pipeline(sp, [(store, 0)], TILES, 6)
            for p in range(2):
                sp.wait_ge(st_y[p], 16 * TILES // 2)

        @block.gpsimd
        def _(pool):
            wait = Waits(pool, sem("tick_pool"))

            def keys(b):
                pool.tensor_copy(kb, m.kT[:, :, bass.ds(b, 1), :].rearrange("p i b s -> p i (b s)"))\
                    .then_inc(q["kb"], 1)

            def rstd(t, p):
                wait(q["mv"], t + 1, alone=True)
                wait(q["h"], t - 1, alone=True)
                pool.tensor_scalar(r[p], mv[p][:, 1:2], 1.0 + LN_EPS, LN_EPS * LN_EPS, ALU.mult, ALU.add)\
                    .then_inc(q["v"], 1)
                wait(q["v"], t + 1)
                pool.tensor_tensor(r[p], r[p], m.power[:, 0:1], ALU.pow).then_inc(q["r"], 1)

            def rstd_q(t, p):
                wait(q["mvq"], t + 1, alone=True)
                wait(q["qn"], t - 1, alone=True)
                pool.tensor_scalar(rq[p], mvq[p][:, 1:2], LN_EPS, None, ALU.add).then_inc(q["vq"], 1)
                wait(q["vq"], t + 1)
                pool.tensor_tensor(rq[p], rq[p], m.power[:, 0:1], ALU.pow).then_inc(q["rq"], 1)

            def next_keys(t, p):
                if p and not (isinstance(t, int) and t == TILES - 1):
                    wait(q["S"], t + 1, alone=True)
                    keys((t + 1) // 2)

            def rstd_y(t, p):
                wait(q["mvy"], t + 1, alone=True)
                wait(q["y"], t - 1, alone=True)
                pool.tensor_scalar(ry[p], mvy[p][:, 1:2], LN_EPS, None, ALU.add).then_inc(q["vy"], 1)
                wait(q["vy"], t + 1)
                pool.tensor_tensor(ry[p], ry[p], m.power[:, 0:1], ALU.pow).then_inc(q["ry"], 1)

            keys(0)
            pipeline(pool, [(rstd, 0), (rstd_q, 2), (next_keys, 3), (rstd_y, 5)], TILES, HEAD)

        @block.scalar
        def _(act):
            wait = Waits(act, sem("tick_act"))

            def copy_x(t, p):
                wait(q["xT"], t + 1)
                wait(q["q"], t)
                act.activation(hT, m.bank(6)[:, 0, 0:D], ACT.Copy).then_inc(q["hT"], 1)

            def copy_q(t, p):
                wait(q["qT"], t + 1)
                wait(q["S"], t - 1)
                act.activation(halves(qT[p]), t_ps, ACT.Copy).then_inc(q["qTc"], 1)

            def exponent(t, p):
                wait(q["sub"], t + 1)
                act.activation(prob[p], prob[p], ACT.Exp).then_inc(q["exp"], 1)

            def copy_p(n):
                def stage(t, p):
                    wait(q["PT"], t * 2 + n + 1)
                    wait(q["PV"], t * 2 - 1 + n)
                    act.activation(halves(pT[:, 6 * n:6 * n + 6, :].rearrange("s h j -> s (h j)")), p_ps[0:S],
                                   ACT.Copy).then_inc(q["PTc"], 1)
                return stage

            def copy_o(t, p):
                wait(q["oT"], t + 1)
                wait(q["out"], t - 1)
                act.activation(halves(oT[p]), t_ps, ACT.Copy).then_inc(q["oTc"], 1)

            def copy_y(t, p):
                wait(q["yp"], t + 1)
                wait(q["xT"], cap(t + 6))
                wait(q["G"], t - 1)
                act.activation(yT[p], m.bank(6)[:, 0, D:2 * D], ACT.Copy).then_inc(q["yT"], 1)

            pipeline(act, [(copy_x, 2), (copy_y, 7), (copy_q, 3), (copy_p(0), 4), (copy_o, 5), (copy_p(1), 4),
                           (exponent, 3)], TILES, HEAD)

        @block.tensor
        def _(pe):
            wait = Waits(pe, sem("tick_pe"))
            pe.wait_ge(m.ld_attn, 112)

            def turn_x(t, p):
                wait(q["h"], t + 1)
                if isinstance(t, int):
                    wait(q["hT"], t)
                wait(q["PTc"], t * 2 - 4)
                for k in range(KD):
                    mm = pe.transpose(m.bank(6)[:, 0, k * P:(k + 1) * P], h[:, k * P:(k + 1) * P], m.ident)
                mm.then_inc(q["xT"], 1)

            def turn_y(t, p):
                wait(q["y"], t + 1)
                wait(q["yT"], t)
                wait(q["PTc"], cap(t + 3) * 2)
                for k in range(KD):
                    mm = pe.transpose(m.bank(6)[:, 0, D + k * P:D + (k + 1) * P], y[p][:, k * P:(k + 1) * P],
                                      m.ident)
                mm.then_inc(q["yp"], 1)

            def logits(t, p):
                if isinstance(t, int) and t == 0:
                    wait(q["ldg"], 64)
                wait(q["yT"], t + 1)
                wait(q["qg"], cap(t + 6))
                wait(q["o"], cap(t + 3) * 2)
                wait(q["lg"], t)
                for k in range(KD):
                    mm = pe.matmul(m.bank(2)[:, 0, D:D + NE], yT[p][:, k * P:(k + 1) * P], wg[:, k, :],
                                   start=(k == 0), stop=(k == KD - 1))
                mm.then_inc(q["G"], 1)

            def query(t, p):
                wait(q["hT"], t + 1)
                if isinstance(t, int):
                    wait(q["qg"], t)
                wait(q["o"], t * 2 - 4)
                for n in range(2):
                    for k in range(KD):
                        mm = pe.matmul(q_ps[:, n, :], hT[:, k * P:(k + 1) * P], wq[:, k, n * HALF:(n + 1) * HALF],
                                       start=(k == 0), stop=(k == KD - 1))
                mm.then_inc(q["q"], 1)

            def turn_q(t, p):
                wait(q["qn"], t + 1)
                if isinstance(t, int):
                    wait(q["qTc"], t)
                wait(q["oTc"], t - 2)
                for i in range(PAIRS):
                    mm = pe.transpose(t_ps[:, i // 3, i % 3 * P:(i % 3 + 1) * P], qn[p][:, i * P:(i + 1) * P],
                                      m.ident)
                mm.then_inc(q["qT"], 1)

            def scores(t, p):
                b = (t - p) // 2
                wait(q["qTc"], t + 1)
                wait(q["kb"], b + 1)
                wait(q["sub"], t)
                for i in range(HEADS):
                    rows = slice(i % 2 * DH, (i % 2 + 1) * DH)
                    mm = pe.matmul(s_ps[:, i % 2, i // 2 * S:(i // 2 + 1) * S],
                                   qT[p][rows, i // 2 * P:(i // 2 + 1) * P], kb[rows, i // 2, :],
                                   start=True, stop=True)
                mm.then_inc(q["S"], 1)

            def turn_p(n):
                def stage(t, p):
                    wait(q["exp"], t + 1)
                    if not n:
                        wait(q["hT"], cap(t + 3))
                        wait(q["yT"], t - 2)
                    wait(q["PTc"], t * 2 + n)
                    for i in range(6):
                        j = 6 * n + i
                        mm = pe.transpose(p_ps[0:S, i // 3, i % 3 * P:(i % 3 + 1) * P],
                                          prob[p][:, j * S:(j + 1) * S], m.ident)
                    mm.then_inc(q["PT"], 1)
                return stage

            def turn_o(t, p):
                wait(q["o"], t * 2 + 2)
                wait(q["qTc"], cap(t + 3))
                for i in range(PAIRS):
                    mm = pe.transpose(t_ps[:, i // 3, i % 3 * P:(i % 3 + 1) * P], o[p][:, i * P:(i + 1) * P],
                                      m.ident)
                mm.then_inc(q["oT"], 1)

            def output(t, p):
                wait(q["oTc"], t + 1)
                wait(q["qg"], cap(t + 4))
                for i in range(PAIRS):
                    mm = pe.matmul(m.bank(2)[:, 0, 0:D], oT[p][:, i * P:(i + 1) * P], wo[:, i, :],
                                   start=(i == 0), stop=(i == PAIRS - 1))
                mm.then_inc(q["out"], 1)

            def values(n):
                def stage(t, p):
                    b = (t - p) // 2
                    wait(q["PTc"], t * 2 + n + 1)
                    wait(q["qg"], cap(t + 3))
                    if n:
                        wait(q["o1"], t)
                        wait(q["lg"], t - 2)
                    for i in range(6):
                        mm = pe.matmul(pv_ps[n][:, i, :], pT[:, 6 * n + i, :],
                                       m.v[:, bass.ds(b, 1), 2 * i + n, :].rearrange("s b e -> s (b e)"),
                                       start=True, stop=True)
                    mm.then_inc(q["PV"], 1)
                return stage

            pipeline(pe, [(turn_y, 7), (turn_x, 2), (turn_q, 3), (turn_p(0), 4), (query, 2), (turn_o, 5), (scores, 3),
                          (turn_p(1), 4), (logits, 7), (output, 5), (values(0), 4), (values(1), 4)],
                     TILES, HEAD)

        @block.vector
        def _(dve):
            wait = Waits(dve, sem("tick_dve"))
            dve.wait_ge(m.ld_attn, 112)
            dve.tensor_scalar(m.qg, m.qg, DH ** -0.5, None, ALU.mult).then_inc(q["qscale"], 1)
            dve.tensor_scalar(m.qb, m.qb, DH ** -0.5, None, ALU.mult).then_inc(q["qscale"], 1)
            dve.wait_ge(q["qscale"], 2)

            def stats(t, p):
                wait(q["mv"], t - 1, alone=True)
                dve.bn_stats(st[p], work(t)).then_inc(q["st"], 1)
                wait(q["st"], t + 1, alone=True)
                wait(q["r"], t - 1, alone=True)
                dve.bn_aggr(mv[p], st[p]).then_inc(q["mv"], 1)

            def norm(t, p):
                wait(q["r"], t + 1)
                wait(q["xT"], t)
                dve.scalar_tensor_tensor(h, work(t), mv[p][:, 0:1], m.vg, ALU.subtract, ALU.mult)\
                   .then_inc(q["t1"], 1)
                wait(q["t1"], t + 1)
                dve.scalar_tensor_tensor(h, h, r[p], m.vb, ALU.mult, ALU.add).then_inc(q["h"], 1)

            def query_stats(t, p):
                wait(q["q"], t + 1)
                wait(q["mvq"], t - 1)
                for n in range(2):
                    dve.bn_stats(stq[p][:, 6 * n:6 * n + 6], q_ps[:, n, :]).then_inc(q["stq"], 1)
                wait(q["stq"], t * 2 + 2, alone=True)
                wait(q["rq"], t - 1, alone=True)
                dve.bn_aggr(mvq[p], stq[p]).then_inc(q["mvq"], 1)
                wait(q["mvq"], t + 1)
                wait(q["qT"], t - 1)
                dve.scalar_tensor_tensor(halves(qn[p]), q_ps, mvq[p][:, 0:1], halves(m.qg), ALU.subtract,
                                         ALU.mult).then_inc(q["qg"], 1)

            def query_norm(t, p):
                wait(q["rq"], t + 1)
                wait(q["qg"], t + 1)
                dve.scalar_tensor_tensor(qn[p], qn[p], rq[p], m.qb, ALU.mult, ALU.add).then_inc(q["qn"], 1)

            def shift(t, p):
                s4 = s_ps.rearrange("p n (h s) -> p n h s", s=S)
                wait(q["S"], t + 1)
                wait(q["sub"], t)
                dve.tensor_reduce(top.rearrange("p (n h) -> p n h", n=2), s4, AX.X, ALU.max).then_inc(q["top"], 1)
                wait(q["top"], t + 1)
                wait(q["PT"], t * 2 - 2)
                dve.tensor_tensor(prob[p].rearrange("p (n h s) -> p n h s", n=2, s=S), s4,
                                  top.rearrange("p (n h) -> p n h", n=2).unsqueeze(3)
                                  .to_broadcast([P, 2, 6, S]), ALU.subtract).then_inc(q["sub"], 1)

            def average(t, p):
                for n in range(2):
                    wait(q["PV"], t * 2 + n + 1)
                    wait(q["o"], t * 2 + n - 1)
                    dve.reciprocal(rden[:, 6 * n:6 * n + 6], pv_ps[n][:, :, DH]).then_inc(q["rden"], 1)
                    wait(q["rden"], t * 2 + n + 1)
                    wait(q["oT"], t - 1)
                    dve.tensor_tensor(o[p].rearrange("p (h n e) -> p n h e", n=2, e=DH)[:, n],
                                      pv_ps[n][:, :, 0:DH],
                                      rden[:, 6 * n:6 * n + 6].unsqueeze(2).to_broadcast([P, 6, DH]),
                                      ALU.mult).then_inc(q["o"], 1)

            def add_out(t, p):
                wait(q["out"], t + 1)
                wait(q["x3"], t)
                dve.tensor_tensor(out1, m.bank(2)[:, 0, 0:D], m.bo, ALU.add).then_inc(q["o1"], 1)
                wait(q["o1"], t + 1)
                dve.scalar_tensor_tensor(work(t), out1, m.tanh[:, 1:2], work(t), ALU.mult, ALU.add)\
                   .then_inc(q["x3"], 1)

            def stats_y(t, p):
                wait(q["x3"], t + 1, alone=True)
                wait(q["mvy"], t - 1, alone=True)
                dve.bn_stats(sty[p], work(t)).then_inc(q["sty"], 1)
                wait(q["sty"], t + 1, alone=True)
                wait(q["ry"], t - 1, alone=True)
                dve.bn_aggr(mvy[p], sty[p]).then_inc(q["mvy"], 1)

            def norm_y(t, p):
                wait(q["ry"], t + 1)
                wait(q["yp"], t - 1)
                wait(st_y[p], t * 8 - p * 8)
                dve.tensor_scalar(y[p], work(t), mvy[p][:, 0:1], ry[p], ALU.subtract, ALU.mult)\
                   .then_inc(q["y"], 1)

            def keep_logits(t, p):
                if isinstance(t, int) and t == 0:
                    wait(q["ldg"], 64)
                wait(q["G"], t + 1)
                wait(q["out"], cap(t + 3))
                dve.tensor_tensor(tile(m.logit, t), m.bank(2)[:, 0, D:D + NE], bg, ALU.add).then_inc(q["lg"], 1)

            pipeline(dve, [(stats, 0), (query_stats, 2), (norm, 1), (query_norm, 2), (norm_y, 6), (shift, 3),
                           (add_out, 5), (keep_logits, 7), (average, 4), (stats_y, 5)], TILES, HEAD)



def route(nc, ctx, m, a):
    def sem(name):
        return ctx.enter_context(nc.semaphore("r_" + name))

    TE, COPIES = TILES * NE, 2 * TILES
    arena = m.arena
    m.weight = arena.take(P, COPIES, at=0).rearrange("p (c t) -> p c t", c=2)
    m.place = arena.take(P, COPIES, U32).rearrange("p (t c) -> p t c", c=2)
    m.token = arena.take(P, SLOTS + 1, U32)
    m.expert = arena.take(P, SLOTS + 1, I32)
    m.b1T = arena.take(P, NE * HT).rearrange("p (e k) -> p e k", e=NE)
    m.routed_end = arena.at

    def te():
        return arena.take(P, TE).rearrange("p (t e) -> p t e", t=TILES)
    logit, prob, cand, place, picked = m.logit, te(), te(), te(), te()
    both = arena.take(P, TE, BF16).rearrange("p (t e) -> p t e", t=TILES)
    hot = [te(), te()]
    def per_tile():
        return arena.take(P, TILES)
    top, total, inv, p1, i1, p2, i2, gap, den = (per_tile() for _ in range(9))
    ones, upper, one = arena.take(P, P, BF16), arena.take(P, P, BF16), arena.take(P, P)
    used, slots, last, start = (arena.take(P, NE) for _ in range(4))
    tokens = arena.take(P, TILES)
    where, slot, lane = (arena.take(P, COPIES).rearrange("p (c t) -> p c t", c=2) for _ in range(3))
    onlane = arena.take(P, COPIES * P, F16).rearrange("p (n j) -> p n j", n=COPIES)
    inslot = arena.take(P, COPIES * 40, F16).rearrange("p (n s) -> p n s", n=COPIES)[:, :, 0:SLOTS]
    past = arena.take(P, SLOTS * (NE - 1)).rearrange("p (s e) -> p s e", s=SLOTS)
    expert = arena.take(P, SLOTS)

    q = {n: sem(n) for n in ("const b1T e pe soft route onehot idx").split()}

    def over_e(x):
        return x.unsqueeze(2).to_broadcast([P, TILES, NE])

    iota_e = m.iota[:, 0:NE].unsqueeze(1).to_broadcast([P, TILES, NE])

    with nc.Block() as block:
        @block.sync
        def _(sp):
            for e in range(NE):
                sp.dma_start(m.late.tensor[:, e * HT * D:(e + 1) * HT * D].rearrange("p (k d) -> p k d", k=HT),
                             a["L1_ffn_W2"][e].rearrange("(k p) d -> p k d", p=P)).then_inc(m.ld_w2[e], 16)

        @block.gpsimd
        def _(pool):
            pool.memset(ones, 1.0).then_inc(q["const"], 1)
            pool.memset(one, 1.0).then_inc(q["const"], 1)
            pool.wait_ge(q["const"], 2)
            pool.affine_select(out=upper, in_=ones, compare_op=ALU.is_ge, fill=0.0, base=-1,
                               pattern=[[1, P]], channel_multiplier=-1).then_inc(q["const"], 1)
            pool.iota(tokens, [[P, TILES]], base=0, channel_multiplier=1,
                      allow_small_or_imprecise_dtypes=True).then_inc(q["const"], 1)

        @block.scalar
        def _(act):
            act.wait_ge(q["b1T"], 1)
            act.activation(m.b1T.rearrange("p e k -> p (e k)"), m.bank(4)[:, 0, 0:NE * HT], ACT.Copy)\
               .then_inc(q["b1T"], 1)
            act.wait_ge(q["soft"], 2)
            act.activation(prob, prob, ACT.Exp).then_inc(q["e"], 1)
            act.wait_ge(q["soft"], 17)
            act.activation(gap, gap, ACT.Exp).then_inc(q["e"], 1)

        @block.tensor
        def _(pe):
            pe.transpose(m.bank(4)[:, 0, 0:NE * HT], m.b1, m.ident[0:NE * HT, 0:NE * HT]).then_inc(q["b1T"], 1)

            pe.wait_ge(q["const"], 4)
            pe.wait_ge(q["route"], 2)
            pe.matmul(m.bank(5)[:, 0, 0:TE], upper, both.rearrange("p t e -> p (t e)"), start=True, stop=False)
            for t in range(TILES - 1):
                n = TILES - 1 - t
                mm = pe.matmul(m.bank(5)[:, 0, (t + 1) * NE:TE].rearrange("p (t e) -> p t e", e=NE), ones,
                               both[:, t:t + 1, :].to_broadcast([P, n, NE]), start=False, stop=(t == TILES - 2))
            mm.then_inc(q["pe"], 1)
            pe.matmul(m.bank(6)[:, 0, 0:NE], one, used, start=True, stop=True).then_inc(q["pe"], 1)
            pe.wait_ge(q["onehot"], 3)
            for n in range(COPIES):
                mm = pe.matmul(m.bank(7)[:, 0, 0:SLOTS], onlane[:, n, :], inslot[:, n, :],
                               start=(n == 0), stop=(n == COPIES - 1))
            mm.then_inc(q["pe"], 1)

        @block.vector
        def _(dve):
            dve.tensor_reduce(top, logit, AX.X, ALU.max).then_inc(q["soft"], 1)
            dve.wait_ge(q["soft"], 1)
            dve.tensor_tensor(prob, logit, over_e(top), ALU.subtract).then_inc(q["soft"], 1)
            dve.wait_ge(q["e"], 1)
            dve.tensor_reduce(total, prob, AX.X, ALU.add).then_inc(q["soft"], 1)
            dve.wait_ge(q["soft"], 3)
            dve.reciprocal(inv, total).then_inc(q["soft"], 1)
            dve.wait_ge(q["soft"], 4)
            dve.tensor_tensor(prob, prob, over_e(inv), ALU.mult).then_inc(q["soft"], 1)
            dve.wait_ge(q["soft"], 5)
            dve.tensor_reduce(p1, prob, AX.X, ALU.max).then_inc(q["soft"], 1)
            dve.wait_ge(q["soft"], 6)
            dve.tensor_tensor(cand, prob, over_e(p1), ALU.is_lt).then_inc(q["soft"], 1)
            dve.wait_ge(q["soft"], 7)
            dve.scalar_tensor_tensor(cand, cand, 1000.0, iota_e, ALU.mult, ALU.add).then_inc(q["soft"], 1)
            dve.wait_ge(q["soft"], 8)
            dve.tensor_reduce(i1, cand, AX.X, ALU.min).then_inc(q["soft"], 1)
            dve.wait_ge(q["soft"], 9)
            dve.tensor_tensor(hot[0], iota_e, over_e(i1), ALU.is_equal).then_inc(q["soft"], 1)
            dve.wait_ge(q["soft"], 10)
            dve.scalar_tensor_tensor(prob, hot[0], -2.0, prob, ALU.mult, ALU.add).then_inc(q["soft"], 1)
            dve.wait_ge(q["soft"], 11)
            dve.tensor_reduce(p2, prob, AX.X, ALU.max).then_inc(q["soft"], 1)
            dve.wait_ge(q["soft"], 12)
            dve.tensor_tensor(cand, prob, over_e(p2), ALU.is_lt).then_inc(q["soft"], 1)
            dve.wait_ge(q["soft"], 13)
            dve.scalar_tensor_tensor(cand, cand, 1000.0, iota_e, ALU.mult, ALU.add).then_inc(q["soft"], 1)
            dve.wait_ge(q["soft"], 14)
            dve.tensor_reduce(i2, cand, AX.X, ALU.min).then_inc(q["soft"], 1)
            dve.wait_ge(q["soft"], 15)
            dve.tensor_tensor(hot[1], iota_e, over_e(i2), ALU.is_equal).then_inc(q["soft"], 1)
            dve.tensor_tensor(gap, p2, p1, ALU.subtract).then_inc(q["soft"], 1)
            dve.wait_ge(q["soft"], 16)
            dve.tensor_tensor(both, hot[0], hot[1], ALU.add).then_inc(q["route"], 1)
            dve.wait_ge(q["route"], 1)
            dve.tensor_reduce(used, both.rearrange("p t e -> p e t"), AX.X, ALU.add).then_inc(q["route"], 1)
            dve.wait_ge(q["e"], 2)
            dve.tensor_scalar(den, gap, 1.0, None, ALU.add).then_inc(q["soft"], 1)
            dve.wait_ge(q["soft"], 18)
            dve.reciprocal(m.weight[:, 0, :], den).then_inc(q["soft"], 1)
            dve.wait_ge(q["soft"], 19)
            dve.tensor_tensor(m.weight[:, 1, :], gap, m.weight[:, 0, :], ALU.mult).then_inc(q["soft"], 1)
            dve.wait_ge(q["soft"], 20)
            dve.tensor_scalar(m.weight, m.weight, m.tanh[:, 3:4], None, ALU.mult).then_inc(q["soft"], 1)
            dve.wait_ge(q["pe"], 2)
            dve.tensor_scalar(slots, m.bank(6)[:, 0, 0:NE], 1.0 / P, (P - 1.0) / P - 0.5 + 0.5 / P, ALU.mult,
                              ALU.add).then_inc(q["route"], 1)
            dve.wait_ge(q["route"], 3)
            dve.tensor_scalar(slots, slots, MAGIC, None, ALU.add).then_inc(q["route"], 1)
            dve.wait_ge(q["route"], 4)
            dve.tensor_scalar(slots, slots, MAGIC, 1.0, ALU.subtract, ALU.max).then_inc(q["route"], 1)
            dve.wait_ge(q["route"], 5)
            dve.wait_ge(q["const"], 2)
            dve.tensor_tensor_scan(last, one[:, 0:NE], slots, 0.0, ALU.mult, ALU.add).then_inc(q["route"], 1)
            dve.wait_ge(q["route"], 6)
            dve.tensor_tensor(start, last, slots, ALU.subtract).then_inc(q["route"], 1)
            dve.wait_ge(q["route"], 7)
            dve.scalar_tensor_tensor(place, start.unsqueeze(1).to_broadcast([P, TILES, NE]), float(P),
                                     m.bank(5)[:, 0, 0:TE].rearrange("p (t e) -> p t e", t=TILES),
                                     ALU.mult, ALU.add).then_inc(q["route"], 1)
            dve.wait_ge(q["route"], 8)
            for c in range(2):
                dve.tensor_tensor(picked, place, hot[c], ALU.mult).then_inc(q["route"], 1)
                dve.wait_ge(q["route"], 9 + 2 * c)
                dve.tensor_reduce(where[:, c, :], picked, AX.X, ALU.add).then_inc(q["route"], 1)
                dve.wait_ge(q["route"], 10 + 2 * c)
            dve.tensor_copy(m.place.rearrange("p t c -> p c t"), where).then_inc(q["idx"], 1)
            dve.tensor_scalar(slot, where, 1.0 / P, -0.5 + 0.5 / P, ALU.mult, ALU.add).then_inc(q["route"], 1)
            dve.wait_ge(q["route"], 13)
            dve.tensor_scalar(slot, slot, MAGIC, None, ALU.add).then_inc(q["route"], 1)
            dve.wait_ge(q["route"], 14)
            dve.tensor_scalar(slot, slot, MAGIC, None, ALU.subtract).then_inc(q["route"], 1)
            dve.wait_ge(q["route"], 15)
            dve.scalar_tensor_tensor(lane, slot, -float(P), where, ALU.mult, ALU.add).then_inc(q["route"], 1)
            dve.wait_ge(q["route"], 16)
            flat = lambda x: x.rearrange("p c t -> p (c t)")
            dve.tensor_tensor(onlane, m.iota[:, 0:P].unsqueeze(1).to_broadcast([P, COPIES, P]),
                              flat(lane).unsqueeze(2).to_broadcast([P, COPIES, P]), ALU.is_equal)\
               .then_inc(q["onehot"], 1)
            dve.tensor_tensor(inslot, m.iota[:, 0:SLOTS].unsqueeze(1).to_broadcast([P, COPIES, SLOTS]),
                              flat(slot).unsqueeze(2).to_broadcast([P, COPIES, SLOTS]), ALU.is_equal)\
               .then_inc(q["onehot"], 1)
            dve.wait_ge(q["const"], 4)
            dve.wait_ge(q["onehot"], 2)
            two = inslot.rearrange("p (c t) s -> p c t s", c=2)
            dve.tensor_tensor(two, two, tokens.unsqueeze(1).unsqueeze(3).to_broadcast([P, 2, TILES, SLOTS]),
                              ALU.mult).then_inc(q["onehot"], 1)
            dve.tensor_tensor(past, m.iota[:, 0:SLOTS].unsqueeze(2).to_broadcast([P, SLOTS, NE - 1]),
                              last[:, 0:NE - 1].unsqueeze(1).to_broadcast([P, SLOTS, NE - 1]), ALU.is_ge)\
               .then_inc(q["route"], 1)
            dve.wait_ge(q["route"], 17)
            dve.tensor_reduce(expert, past, AX.X, ALU.add).then_inc(q["route"], 1)
            dve.wait_ge(q["route"], 18)
            dve.tensor_copy(m.expert[:, 0:SLOTS], expert).then_inc(q["idx"], 1)
            dve.wait_ge(q["pe"], 3)
            dve.tensor_copy(m.token[:, 0:SLOTS], m.bank(7)[:, 0, 0:SLOTS]).then_inc(q["idx"], 1)
            dve.wait_ge(q["idx"], 3)


def experts(nc, ctx, m, a):
    def sem(name):
        return ctx.enter_context(nc.semaphore("e_" + name))

    arena = m.arena
    arena.at = m.routed_end
    def pair(cols, dtype=F32):
        return [arena.take(P, cols, dtype) for _ in range(2)]
    col, xs, result = pair(1, U32), pair(D), pair(D)
    xT, h, hT = arena.take(P, D), arena.take(P, HID), arena.take(P, HT * P)
    cols, mine = pair(2, U32), [pair(D), pair(D)]
    w1 = m.early.tensor[:, :].rearrange("p (e k h) -> p e k h", e=NE, k=KD)
    w2 = m.late.tensor[:, :].rearrange("p (e k d) -> p e k d", e=NE, k=HT)
    out_dram = nc.dram_tensor("results_dram", [SLOTS * P, D], F32, kind="Internal").ap()

    q = {n: sem(n) for n in "col xT xTc H h T b hT Y res cols x1 x2".split()}
    ld = [sem(f"ld_rows{p}") for p in range(2)]
    stored = [sem(f"st_result{p}") for p in range(2)]
    fetched = [[sem(f"ld_mine{c}{p}") for p in range(2)] for c in range(2)]
    s_out = sem("st_out")

    h_ps = m.bank(1, 2)
    t_ps = m.bank(3, 2).rearrange("p n (k j) -> p (n k) j", j=P)

    def expert_of(eng, s):
        return eng.value_load(m.expert[0:1, bass.ds(s, 1)], min_val=0, max_val=NE - 1)

    with nc.Block() as block:
        @block.sync
        def _(sp):
            wait = Waits(sp, sem("tick_sp"))

            def store(s, p):
                wait(q["res"], s + 1)
                sp.dma_start(out_dram[bass.ds(s * P, P), :], result[p]).then_inc(stored[p], 16)

            pipeline(sp, [(store, 0)], SLOTS, 6)
            sp.wait_ge(stored[0], 16 * ((SLOTS + 1) // 2))
            sp.wait_ge(stored[1], 16 * (SLOTS // 2))

        @block.gpsimd
        def _(pool):
            wait = Waits(pool, sem("tick_pool"))

            def fetch(s, p):
                wait(q["xT"], s - 1, alone=True)
                pool.tensor_copy(col[p], m.token[:, bass.ds(s, 1)]).then_inc(q["col"], 1)
                wait(q["col"], s + 1, alone=True)
                pool.indirect_dma_start(xs[p], None, m.y_dram, bass.IndirectOffsetOnAxis(ap=col[p], axis=0))\
                    .then_inc(ld[p], 16)

            pipeline(pool, [(fetch, 0)], SLOTS, 6)

        @block.scalar
        def _(act):
            wait = Waits(act, sem("tick_act"))

            def copy_x(s, p):
                wait(q["xT"], s + 1)
                wait(q["H"], s)
                act.activation(xT, m.bank(0)[:, 0, 0:D], ACT.Copy).then_inc(q["xTc"], 1)

            def copy_h(s, p):
                wait(q["H"], s + 1)
                wait(q["T"], s)
                act.activation(h.rearrange("p (n j) -> p n j", n=2), h_ps, ACT.Copy).then_inc(q["h"], 1)

            pipeline(act, [(copy_h, 3), (copy_x, 2)], SLOTS, 6)

        @block.tensor
        def _(pe):
            wait = Waits(pe, sem("tick_pe"))
            pe.wait_ge(m.ld_w1, 16)
            of = {}

            def load(s, p):
                of[1] = expert_of(pe, s)

            def load2(s, p):
                of[2] = expert_of(pe, s)

            def turn_x(s, p):
                wait(ld[p], s * 8 - p * 8 + 16)
                wait(q["xTc"], s)
                for k in range(KD):
                    mm = pe.transpose(m.bank(0)[:, 0, k * P:(k + 1) * P], xs[p][:, k * P:(k + 1) * P], m.ident)
                mm.then_inc(q["xT"], 1)

            def turn_h(s, p):
                wait(q["h"], s + 1)
                wait(q["b"], s)
                for k in range(HT):
                    mm = pe.transpose(t_ps[:, k, :], h[:, k * P:(k + 1) * P], m.ident)
                mm.then_inc(q["T"], 1)

            def layer1(s, p):
                wait(q["xTc"], s + 1)
                wait(q["h"], s)
                for n in range(2):
                    for k in range(KD):
                        mm = pe.matmul(h_ps[:, n, :], xT[:, k * P:(k + 1) * P],
                                       w1[:, bass.ds(of[1], 1), k, n * 512:(n + 1) * 512]
                                       .rearrange("p e h -> p (e h)"), start=(k == 0), stop=(k == KD - 1))
                mm.then_inc(q["H"], 1)

            def layer2(s, p):
                if isinstance(s, int) and s < NE:
                    wait(m.ld_w2[s], 16)
                wait(q["hT"], s + 1)
                wait(q["res"], s)
                for k in range(HT):
                    mm = pe.matmul(m.bank(5)[:, 0, 0:D], hT[:, k * P:(k + 1) * P],
                                   w2[:, bass.ds(of[2], 1), k, :].rearrange("p e d -> p (e d)"),
                                   start=(k == 0), stop=(k == HT - 1))
                mm.then_inc(q["Y"], 1)

            pipeline(pe, [(load, 2), (load2, 3), (turn_x, 2), (turn_h, 3), (layer1, 2), (layer2, 3)],
                     SLOTS, NE + 4)

        @block.vector
        def _(dve):
            wait = Waits(dve, sem("tick_dve"))
            of = {}

            def load(s, p):
                of[0] = expert_of(dve, s)

            def bias(s, p):
                wait(q["T"], s + 1)
                wait(q["Y"], s)
                b1 = m.b1T[:, bass.ds(of[0], 1), :].rearrange("p e k -> p (e k)").unsqueeze(2)
                dve.tensor_tensor(hT.rearrange("p (k j) -> p k j", k=HT), t_ps, b1.to_broadcast([P, HT, P]),
                                  ALU.add).then_inc(q["b"], 1)
                wait(q["b"], s + 1)
                dve.tensor_scalar(hT, hT, 0.0, None, ALU.max).then_inc(q["hT"], 1)

            def keep(s, p):
                wait(q["Y"], s + 1)
                wait(stored[p], s * 8 - p * 8)
                dve.tensor_tensor(result[p], m.bank(5)[:, 0, 0:D],
                                  m.b2[:, bass.ds(of[0], 1), :].rearrange("p e d -> p (e d)"), ALU.add)\
                   .then_inc(q["res"], 1)

            pipeline(dve, [(load, 3), (bias, 3), (keep, 3)], SLOTS, 6)

    out_t = a["out"].rearrange("b (h p) d -> p (b h) d", p=P)

    def work(t):
        return m.x[:, bass.ds(t, 1), :].rearrange("p t d -> p (t d)")

    with nc.Block() as block:
        @block.gpsimd
        def _(pool):
            wait = Waits(pool, sem("tick_pool2"))

            def fetch(t, p):
                wait(q["x2"], t - 1, alone=True)
                pool.tensor_copy(cols[p], m.place[:, bass.ds(t, 1), :].rearrange("p t c -> p (t c)"))\
                    .then_inc(q["cols"], 1)
                wait(q["cols"], t + 1, alone=True)
                for c in range(2):
                    pool.indirect_dma_start(mine[c][p], None, out_dram,
                                            bass.IndirectOffsetOnAxis(ap=cols[p][:, c:c + 1], axis=0))\
                        .then_inc(fetched[c][p], 16)

            pipeline(pool, [(fetch, 0)], TILES, 6)

        @block.vector
        def _(dve):
            wait = Waits(dve, sem("tick_dve2"))

            def add(t, p):
                wait(fetched[0][p], t * 8 - p * 8 + 16)
                dve.scalar_tensor_tensor(work(t), mine[0][p], m.weight[:, 0, bass.ds(t, 1)], work(t), ALU.mult,
                                         ALU.add).then_inc(q["x1"], 1)
                wait(q["x1"], t + 1)
                wait(fetched[1][p], t * 8 - p * 8 + 16)
                dve.scalar_tensor_tensor(work(t), mine[1][p], m.weight[:, 1, bass.ds(t, 1)], work(t), ALU.mult,
                                         ALU.add).then_inc(q["x2"], 1)

            pipeline(dve, [(add, 0)], TILES, 6)

        @block.sync
        def _(sp):
            for n in range(8):
                sp.wait_ge(q["x2"], 2 * n + 2)
                sp.dma_start(out_t[:, 2 * n:2 * n + 2, :], m.x[:, 2 * n:2 * n + 2, :]).then_inc(s_out, 16)
            sp.wait_ge(s_out, 16 * 8)


def build(nc, a):
    with ExitStack() as ctx:
        m = Memory()
        allocate(nc, ctx, m)
        m.ld_attn = ctx.enter_context(nc.semaphore("ld_attn"))
        m.ld_w1 = ctx.enter_context(nc.semaphore("ld_w1"))
        m.ld_w2 = [ctx.enter_context(nc.semaphore(f"ld_w2_{e}")) for e in range(NE)]
        before = nc.snapshot_sems()
        align(nc, ctx, m, a)
        ffn(nc, ctx, m, a)
        nc.clear_and_free_semaphores(nc.allocated_since(before))
        nc.all_engine_barrier()
        attention(nc, ctx, m, a)
        route(nc, ctx, m, a)
        experts(nc, ctx, m, a)


_INS = ["x", "ctx_1024", "g_xattn", "g_ffn", "L0_ffn_ln1_g", "L0_ffn_ln1_b", "L0_ffn_w1", "L0_ffn_b1",
        "L0_ffn_ln2_g", "L0_ffn_ln2_b", "L0_ffn_w2", "L0_ffn_b2", "L1_xattn_tab_g", "L1_xattn_tab_b",
        "L1_xattn_vid_g", "L1_xattn_vid_b", "L1_xattn_Wq", "L1_xattn_Wk", "L1_xattn_Wv", "L1_xattn_q_g",
        "L1_xattn_q_b", "L1_xattn_k_g", "L1_xattn_k_b", "L1_xattn_Wo", "L1_xattn_bo", "L1_ffn_W1", "L1_ffn_b1",
        "L1_ffn_W2", "L1_ffn_b2", "L1_ffn_Wg", "L1_ffn_bg"]


def kernel(**inputs):
    import numpy as np
    import concourse.bacc as bacc
    from concourse.bass_utils import run_bass_kernel_spmd

    nc = bacc.Bacc("TRN2", target_bir_lowering=False, num_devices=1)
    arrays, a = {}, {}
    for name in _INS:
        array = np.ascontiguousarray(inputs[name])
        arrays[f"in_{name}_dram"] = array
        a[name] = nc.dram_tensor(f"in_{name}_dram", array.shape, mybir.dt.from_np(array.dtype),
                                 kind="ExternalInput").ap()
    a["out"] = nc.dram_tensor("out_dram", [B, TQ, D], F32, kind="ExternalOutput").ap()
    build(nc, a)
    r = run_bass_kernel_spmd(nc, [arrays], core_ids=[0])
    return r.results[0]["out_dram"]
```

```python
from contextlib import ExitStack

import concourse.bass as bass
from concourse import mybir

F32, F16, BF16 = mybir.dt.float32, mybir.dt.float16, mybir.dt.bfloat16
I32, U32 = mybir.dt.int32, mybir.dt.uint32
ALU = mybir.AluOpType
ACT = mybir.ActivationFunctionType
AX = mybir.AxisListType

P = 128
B, TQ, D = 8, 256, 256
S = 77
TILES = B * TQ // P
KD = D // P
HID = 1024
HT = HID // P
HEADS, DH = 12, 64
INNER = HEADS * DH
PAIRS = INNER // P
NE = 8
LN_EPS = 1e-5
BIG = 1e30
MAGIC = 12582912.0

CH, LAG = 4, 2
CW = TQ // CH
PADR = LAG * (CH - 1)
RING = 12
STEPS = -(-(S + PADR) // RING) * RING
DROWS = PADR + STEPS + (STEPS - S) % 2
GROUP = 4

SLOTS = (2 * B * TQ - NE) // P + NE


class Memory:
    pass


class Region:

    def __init__(self, tensor):
        self.tensor, self.at = tensor, 0

    def take(self, parts, cols, dtype=F32, at=None):
        if at is not None:
            self.at = at
        words = cols if dtype in (F32, I32, U32) else cols // 2
        view = self.tensor[0:parts, self.at:self.at + words]
        self.at += words
        assert self.at <= self.tensor.shape[1], self.at
        return view if dtype == F32 else view.bitcast(dtype)


def bcast(vector, parts):
    return vector.rearrange("(o n) -> o n", o=1).broadcast_to([parts, vector.shape[0]])


def allocate(nc, ctx, m):
    def region(name, cols):
        return Region(ctx.enter_context(nc.sbuf_tensor(name, [P, cols], F32)))

    psum = ctx.enter_context(nc.psum_tensor("banks", [P, 8, 512], F32))
    m.bank = lambda k, n=1: psum[:, k:k + n, :]
    keep = region("keep", 4096 + 2048 + 256 + 2048 + 128 + 256 + 128)
    m.x = keep.take(P, TILES * D).rearrange("p (t d) -> p t d", t=TILES)
    m.ctx = keep.take(S, B * D).rearrange("p (b d) -> p b d", b=B)
    m.w1T = keep.take(P, KD * HID, BF16).rearrange("p (k h) -> p k h", k=KD)
    m.w2T = keep.take(P, HT * D, BF16).rearrange("p (k d) -> p k d", k=HT)
    m.spare = Region(keep.tensor)
    m.spare.at = TILES * D
    m.ident = keep.take(P, P)
    m.identb = keep.take(P, P, BF16)
    m.iota = keep.take(P, TQ)
    m.tanh = keep.take(P, 4)
    m.wscale = keep.take(P, 4)
    m.power = keep.take(P, 32)
    m.power1 = keep.take(P, 2)
    m.vT = keep.take(S, 2 * B).rearrange("p (k b) -> p k b", k=2)
    m.early = region("early", NE * KD * HID)
    m.late = region("late", NE * HT * D)
    m.arena = region("arena", 11200)
    m.kT = m.late.take(P, PAIRS * B * S, at=0).rearrange("p (i b s) -> p i b s", i=PAIRS, b=B)
    m.v = m.late.take(S, B * HEADS * (DH + 1)).rearrange("p (b h e) -> p b h e", b=B, h=HEADS)
    m.wa = m.late.take(P, KD * INNER)
    m.wb = m.late.take(P, KD * INNER)
    m.qg = m.late.take(P, INNER)
    m.qb = m.late.take(P, INNER)
    m.vg = m.late.take(P, D)
    m.vb = m.late.take(P, D)
    m.bo = m.late.take(P, D)


def ffn_vectors(m):
    m.arena.at = 0
    return [m.arena.take(P, HID) for _ in range(3)] + [m.arena.take(P, D) for _ in range(3)]


def align(nc, ctx, m, a):
    def sem(name):
        return nc.alloc_semaphore(name)

    dist_dram = nc.dram_tensor("dist_dram", [B, DROWS, TQ], F32, kind="Internal").ap()
    cost_dram = nc.dram_tensor("cost_dram", [CH * B, STEPS, CW], F32, kind="Internal").ap()
    jump_dram = nc.dram_tensor("jump_dram", [B, S, TQ], F16, kind="Internal").ap()

    early, arena = m.early, m.arena
    dist = early.take(CH * B, STEPS * CW, at=0).rearrange("p (t w) -> p t w", t=STEPS)
    xn = early.take(P, TILES * D, at=5376).rearrange("p (t d) -> p t d", t=TILES)
    drow = early.take(S, B * TQ).rearrange("p (b j) -> p b j", b=B)
    xnT = early.take(P, 2 * KD * TQ).rearrange("p (u k j) -> p u k j", u=2, k=KD)
    xsq = early.take(P, 2 * KD * TQ).rearrange("p (u k j) -> p u k j", u=2, k=KD)
    sq = early.take(S, 3 * TQ).rearrange("p (n j) -> p n j", n=3)
    sqjunk = early.take(S, D)
    W1 = TQ + 1
    best = early.take(S, B * TQ, at=0).rearrange("p (b j) -> p b j", b=B)
    stay = early.take(S, B * TQ).rearrange("p (b j) -> p b j", b=B)
    djump = early.take(S, B * TQ, F16).rearrange("p (b j) -> p b j", b=B)
    cost = early.take(S, B * W1, at=5376).rearrange("p (b j) -> p b j", b=B)
    above = early.take(S, B * W1).rearrange("p (b j) -> p b j", b=B)
    turn = early.take(S, B * TQ).rearrange("p (b j) -> p b j", b=B)
    jump = early.take(S, B * TQ).rearrange("p (b j) -> p b j", b=B)
    djump_b = early.take(B, S * TQ, F16, at=0).rearrange("p (i j) -> p i j", i=S)

    w1s = arena.take(P, HT * D, at=0).rearrange("p (k d) -> p k d", k=HT)
    w2s = arena.take(P, KD * HID).rearrange("p (k h) -> p k h", k=KD)
    wq = arena.take(P, HT * D, BF16)
    ones = arena.take(P, P)
    kvn = arena.take(S, B * D).rearrange("p (b d) -> p b d", b=B)
    kvT = arena.take(P, KD * S).rearrange("p (k s) -> p k s", k=KD)
    kraw = [arena.take(S, INNER), early.take(S, INNER, at=14592)]
    kn = [arena.take(S, INNER), early.take(S, INNER)]
    ring = arena.take(CH * B, RING * (CW + 1)).rearrange("p (r w) -> p r w", r=RING)
    diag = arena.take(CH * B, CW)
    first = arena.take(CH * B, 1)
    floor = arena.take(CH * B, 1)
    shifted = arena.take(CH * B, 2)
    path = arena.take(B, S + 1)
    HOPS = 19
    near_path = arena.take(B, HOPS + 1)
    ctxT = [arena.take(P, KD * S).rearrange("p (k s) -> p k s", k=KD) for _ in range(2)]
    junk = arena.take(P, 4)
    stats = arena.take(P, TILES * 6).rearrange("p (t n) -> p t n", t=TILES)
    mv = arena.take(P, TILES * 2).rearrange("p (t n) -> p t n", t=TILES)
    rstd = arena.take(P, TILES)
    cstats = arena.take(S, B * 6).rearrange("p (t n) -> p t n", t=B)
    cmv = arena.take(S, B * 2).rearrange("p (t n) -> p t n", t=B)
    crstd = arena.take(S, B)
    norm2 = arena.take(S, B)
    ksum = arena.take(S, 5 * B).rearrange("p (n b) -> p n b", n=5)
    wsum = arena.take(P, 2)
    big = arena.take(B, 2 * TQ)

    wk = m.wa.rearrange("p (k n) -> p k n", k=KD)
    wv = m.wb.rearrange("p (k n) -> p k n", k=KD)

    hopjunk = early.take(B, TQ, at=14000)
    NPAD = PADR // 2 + -(-(DROWS - PADR - S) // 2)

    m.ld_ffn = sem("ld_ffn")
    EARLY = 64
    assert EARLY <= STEPS - RING - PADR
    s_cl0 = sem("ld_cost0")
    s_x = [sem(f"ld_x{q}") for q in range(4)]
    s_cost = [sem(f"st_cost{g}") for g in range(RING // GROUP)]
    s_ctx, s_gate, s_w12, s_kv, s_kvg = map(sem, "ld_ctx ld_gate ld_w12 ld_kvw ld_kvg".split())
    s_id0, s_const, s_init = map(sem, "ident0 const dtw_init".split())
    s_cst, s_cmv, s_cr, s_st, s_mv, s_r = map(sem, "cstats cmv crstd stats mv rstd".split())
    s_v1, s_v2 = map(sem, "var_eps cvar_eps".split())
    s_xn, s_kvn, s_xT, s_xTc, s_xsq, s_cT, s_cTc, s_aa = map(sem, "xn kvn xT xTcopy xsq cT cTcopy norm2".split())
    s_D, s_a, s_sq, s_rc, s_ar, s_dr = map(sem, "distp dist2 sqrt recip quot drow".split())
    s_pad, s_dst, s_dist = map(sem, "st_pad st_dist ld_dist".split())
    s_min, s_scan, s_shf, s_bnd = map(sem, "dtw_min dtw_scan dtw_shift dtw_left".split())
    s_cl, s_cm, s_F, s_djst, s_djld, s_hop, s_path, s_vT, s_vTc = map(
        sem, "ld_cost cost_big choose st_jump ld_jump hop path0 vT vTcopy".split())
    s_ab, s_tot, s_ws, s_wq, s_wqb, s_wT, s_wTc = map(sem, "wabs wtotal wscale wq wqb wT wTcopy".split())
    s_kg, s_kvb, s_kvTp, s_kvTc, s_k, s_ksum, s_knm, s_kssq = map(
        sem, "kvgain kvbias kvT kvTcopy k ksum kmean kssq".split())
    s_kvar, s_krs, s_kbias, s_kn, s_kga, s_kb, s_kTp, s_kTc = map(
        sem, "kvar krstd kbias knorm kgain kaff kTp kTcopy".split())
    s_v, s_vc, s_one, s_th, s_pw = map(sem, "v vcopy vones tanh power".split())

    x_t = a["x"].rearrange("b (h p) d -> p (b h) d", p=P)

    with nc.Block() as block:
        @block.sync
        def _(sp):
            sp.dma_start(m.ctx, a["ctx_1024"].rearrange("b s d -> s b d")).then_inc(s_ctx, 16)
            for q in range(4):
                sp.dma_start(m.x[:, 4 * q:4 * q + 4, :], x_t[:, 4 * q:4 * q + 4, :]).then_inc(s_x[q], 16)
            sp.wait_ge(s_init, 1)
            for r in list(range(0, PADR, 2)):
                sp.dma_start(dist_dram[:, r:r + 2, :], big.rearrange("p (r j) -> p r j", r=2)).then_inc(s_pad, 16)
            for r in range(PADR + S, DROWS, 2):
                r = min(r, DROWS - 2)
                sp.dma_start(dist_dram[:, r:r + 2, :], big.rearrange("p (r j) -> p r j", r=2)).then_inc(s_pad, 16)
            for b in range(B):
                sp.wait_ge(s_dr, b + 1)
                sp.dma_start(dist_dram[b, PADR:PADR + S, :], drow[:, b, :]).then_inc(s_dst, 16)
            sp.wait_ge(s_pad, 16 * NPAD)
            sp.wait_ge(s_dst, 16 * B)
            sp.wait_ge(s_xn, TILES)
            for c in range(CH):
                r = PADR - LAG * c
                sp.dma_start(dist[c * B:(c + 1) * B, :, :],
                             dist_dram[:, r:r + STEPS, c * CW:(c + 1) * CW]).then_inc(s_dist, 16)
            def store(i):
                for g in range(RING // GROUP):
                    sp.wait_ge(s_scan, i * RING + (g + 1) * GROUP)
                    sp.dma_start(cost_dram[:, bass.ds(i * RING + g * GROUP, GROUP), :],
                                 ring[:, g * GROUP:(g + 1) * GROUP, 1:CW + 1]).then_inc(s_cost[g], 16)

            cost_v = cost_dram.rearrange("(c b) t w -> c t b w", c=CH)
            def load(r0, r1, done):
                for c in range(CH):
                    lo, t0 = 1 + c * CW, LAG * c
                    sp.dma_start(cost[r0:r1, :, lo:lo + CW], cost_v[c, t0 + r0:t0 + r1]).then_inc(done, 16)
                    a0 = max(r0, 1)
                    sp.dma_start(above[a0:r1, :, lo:lo + CW], cost_v[c, t0 + a0 - 1:t0 + r1 - 1]).then_inc(done, 16)

            TURNS = STEPS // RING
            with sp.Fori(0, TURNS - 1) as i:
                store(i)
            for g in range(RING // GROUP):
                sp.wait_ge(s_cost[g], 16 * (TURNS - 1))
            load(0, EARLY, s_cl0)
            store(TURNS - 1)
            for g in range(RING // GROUP):
                sp.wait_ge(s_cost[g], 16 * TURNS)
            load(EARLY, S, s_cl)
            sp.wait_ge(s_F, 7)
            sp.dma_start(jump_dram.rearrange("b i j -> i b j"), djump).then_inc(s_djst, 16)
            sp.wait_ge(s_djst, 16)
            sp.dma_start(djump_b, jump_dram).then_inc(s_djld, 16)

        @block.gpsimd
        def _(pool):
            pool.memset(m.power, -0.5).then_inc(s_pw, 1)
            pool.memset(m.power1, -1.0).then_inc(s_pw, 1)
            pool.memset(m.ident, 0.0).then_inc(s_id0, 1)
            pool.memset(ones, 1.0).then_inc(s_const, 1)
            pool.wait_ge(s_id0, 1)
            pool.affine_select(out=m.ident, in_=m.ident, compare_op=ALU.not_equal, fill=1.0, base=0,
                               pattern=[[-1, P]], channel_multiplier=1).then_inc(s_const, 1)
            pool.iota(m.iota, [[1, TQ]], base=0, channel_multiplier=0,
                      allow_small_or_imprecise_dtypes=True).then_inc(s_const, 1)
            pool.wait_ge(s_const, 3)
            pool.tensor_copy(m.identb, m.ident).then_inc(s_const, 1)
            pool.memset(big, BIG).then_inc(s_init, 1)
            pool.wait_ge(s_pw, 2)
            pool.wait_ge(s_cmv, B)
            pool.tensor_scalar(crstd, cmv[:, :, 1], LN_EPS, None, ALU.add).then_inc(s_v2, 1)
            pool.wait_ge(s_v2, 1)
            pool.tensor_tensor(crstd, crstd, m.power[0:S, 0:B], ALU.pow).then_inc(s_cr, 1)
            for q in range(4):
                t = slice(4 * q, 4 * q + 4)
                pool.wait_ge(s_mv, 4 * q + 4)
                pool.tensor_scalar(rstd[:, t], mv[:, t, 1], LN_EPS, None, ALU.add).then_inc(s_v1, 1)
                pool.wait_ge(s_v1, q + 1)
                pool.tensor_tensor(rstd[:, t], rstd[:, t], m.power[:, 0:4], ALU.pow).then_inc(s_r, 1)
            pool.memset(ring, BIG).then_inc(s_init, 1)
            pool.memset(first, BIG).then_inc(s_init, 1)
            pool.memset(floor, 0.0).then_inc(s_init, 1)
            pool.wait_ge(s_init, 4)
            pool.memset(first[0:B], 0.0).then_inc(s_init, 1)
            pool.memset(floor[0:B], BIG).then_inc(s_init, 1)
            pool.memset(path, float(TQ - 1)).then_inc(s_path, 1)
            pool.memset(near_path, float(TQ - 1)).then_inc(s_path, 1)
            pool.wait_ge(s_path, 2)
            pool.memset(path[:, 0:1], 0.0).then_inc(s_hop, 1)
            pool.memset(m.v, 1.0).then_inc(s_one, 1)
            pool.wait_ge(s_kvn, B)
            pool.wait_ge(s_kvg, 64)
            for b in range(B):
                pool.tensor_tensor(kvn[:, b, :], kvn[:, b, :], m.vg[0:S, :], ALU.mult).then_inc(s_kg, 1)
                pool.wait_ge(s_kg, b + 1)
                pool.tensor_tensor(kvn[:, b, :], kvn[:, b, :], m.vb[0:S, :], ALU.add).then_inc(s_kvb, 1)
            pool.wait_ge(s_tot, 1)
            pool.tensor_scalar(m.wscale[:, 0:2], wsum, 1.0 / (HID * D), 1e-5, ALU.mult, ALU.max).then_inc(s_ws, 1)
            pool.wait_ge(s_ws, 1)
            pool.tensor_tensor(m.wscale[:, 2:4], m.wscale[:, 0:2], m.power1, ALU.pow).then_inc(s_ws, 1)
            pool.wait_ge(s_ws, 2)
            for n, w in enumerate((w1s.rearrange("p k d -> p (k d)"), w2s.rearrange("p k h -> p (k h)"))):
                pool.tensor_scalar(w, w, m.wscale[:, 2 + n:3 + n], MAGIC, ALU.mult, ALU.add).then_inc(s_wq, 1)
                pool.wait_ge(s_wq, 2 * n + 1)
                pool.tensor_scalar(w, w, MAGIC, 1.0, ALU.subtract, ALU.min).then_inc(s_wq, 1)
                pool.wait_ge(s_wq, 2 * n + 2)
                if n:
                    pool.wait_ge(s_wT, 3)
                pool.tensor_scalar(wq, w, -1.0, None, ALU.max).then_inc(s_wqb, 1)
            for b in range(B):
                tot, mean, ssq, rs, bias = (ksum[:, n, b:b + 1] for n in range(5))
                pool.wait_ge(s_ksum, b + 1)
                pool.tensor_scalar(mean, tot, -1.0 / INNER, None, ALU.mult).then_inc(s_knm, 1)
                pool.wait_ge(s_kssq, b + 1)
                pool.tensor_scalar(rs, ssq, 1.0 / INNER, LN_EPS, ALU.mult, ALU.add).then_inc(s_kvar, 1)
                pool.wait_ge(s_kvar, b + 1)
                pool.tensor_tensor(rs, rs, m.power[0:S, 0:1], ALU.pow).then_inc(s_krs, 1)
                pool.wait_ge(s_krs, b + 1)
                pool.tensor_tensor(bias, rs, mean, ALU.mult).then_inc(s_kbias, 1)
                pool.wait_ge(s_kn, b + 1)
                k = kn[b % 2]
                pool.tensor_tensor(k, k, m.qg[0:S, :], ALU.mult).then_inc(s_kga, 1)
                pool.wait_ge(s_kga, b + 1)
                pool.tensor_tensor(k, k, m.qb[0:S, :], ALU.add).then_inc(s_kb, 1)

        @block.scalar
        def _(act):
            act.dma_start(junk[:, 0:2], bcast(a["g_xattn"], P)).then_inc(s_gate, 16)
            act.dma_start(junk[:, 2:4], bcast(a["g_ffn"], P)).then_inc(s_gate, 16)
            act.dma_start(w1s, a["L0_ffn_w1"].rearrange("(k p) d -> p k d", p=P)).then_inc(s_w12, 16)
            act.dma_start(w2s, a["L0_ffn_w2"].rearrange("(k p) h -> p k h", p=P)).then_inc(s_w12, 16)
            act.dma_start(m.vg, bcast(a["L1_xattn_tab_g"], P)).then_inc(s_kvg, 16)
            act.dma_start(m.vb, bcast(a["L1_xattn_tab_b"], P)).then_inc(s_kvg, 16)
            act.dma_start(m.qg, bcast(a["L1_xattn_k_g"], P)).then_inc(s_kvg, 16)
            act.dma_start(m.qb, bcast(a["L1_xattn_k_b"], P)).then_inc(s_kvg, 16)
            act.dma_start(wk, a["L1_xattn_Wk"].rearrange("(k p) n -> p k n", p=P)).then_inc(s_kv, 16)
            act.dma_start(wv, a["L1_xattn_Wv"].rearrange("(k p) n -> p k n", p=P)).then_inc(s_kv, 16)
            act.wait_ge(s_gate, 32)
            act.activation(m.tanh, junk, ACT.Tanh).then_inc(s_th, 1)
            act.wait_ge(s_ctx, 16)
            for b in range(B):
                if b:
                    act.wait_ge(s_aa, b)
                act.activation(sqjunk, m.ctx[:, b, :], ACT.Square, accum_out=norm2[:, b:b + 1]).then_inc(s_aa, 1)
            def roots(b):
                act.wait_ge(s_a, b + 1)
                if b:
                    act.wait_ge(s_dr, b)
                act.activation(sq[:, 1, :], sq[:, 0, :], ACT.Sqrt).then_inc(s_sq, 1)
            for b in range(B):
                act.wait_ge(s_xT, b + 1)
                if b >= 2:
                    act.wait_ge(s_D, b - 1)
                bank = m.bank(b % 2)[:, 0, :].rearrange("p (k j) -> p k j", k=KD)
                act.activation(xnT[:, b % 2], bank, ACT.Copy).then_inc(s_xTc, 1)
                act.activation(xsq[:, b % 2], bank, ACT.Square).then_inc(s_xsq, 1)
                if b:
                    roots(b - 1)
            roots(B - 1)
            act.wait_ge(s_w12, 32)
            act.activation(wq[:, 0:HT * D], w1s.rearrange("p k d -> p (k d)"), ACT.Abs,
                           accum_out=wsum[:, 0:1]).then_inc(s_ab, 1)
            act.wait_ge(s_ab, 1)
            act.activation(wq[:, 0:HT * D], w2s.rearrange("p k h -> p (k h)"), ACT.Abs,
                           accum_out=wsum[:, 1:2]).then_inc(s_ab, 1)
            act.wait_ge(s_wT, 1)
            act.activation(wsum, m.bank(7)[:, 0, 0:2], ACT.Copy).then_inc(s_tot, 1)
            for n in range(2):
                for half in range(2):
                    act.wait_ge(s_wT, 2 + 2 * n + half)
                    dst = (m.w1T[:, half, :] if n == 0 else
                           m.w2T[:, 4 * half:4 * half + 4, :].rearrange("p k d -> p (k d)"))
                    act.activation(dst, m.bank(6 + half)[:, 0, :].bitcast(BF16), ACT.Copy).then_inc(s_wTc, 1)
            act.wait_ge(s_wTc, 4)
            for dst, src in zip(ffn_vectors(m), (a["L0_ffn_b1"], a["L0_ffn_ln2_g"], a["L0_ffn_ln2_b"],
                                                 a["L0_ffn_ln1_g"], a["L0_ffn_ln1_b"], a["L0_ffn_b2"])):
                act.dma_start(dst, bcast(src, P)).then_inc(m.ld_ffn, 16)
            def keep_keys(b):
                act.wait_ge(s_kTp, b + 1)
                act.activation(m.kT[:, :, b, :], m.bank(4)[:, 0, 0:PAIRS * S].rearrange("p (i s) -> p i s", i=PAIRS),
                               ACT.Copy).then_inc(s_kTc, 1)

            for b in range(B):
                act.wait_ge(s_kvTp, b + 1)
                if b:
                    act.wait_ge(s_v, b)
                act.activation(kvT, m.bank(5)[:, 0, 0:KD * S].rearrange("p (k s) -> p k s", k=KD),
                               ACT.Copy).then_inc(s_kvTc, 1)
                act.wait_ge(s_k, b + 1)
                if b >= 2:
                    act.wait_ge(s_kn, b - 1)
                kp = m.bank(0, 2)[0:S, :, 0:INNER // 2]
                kr = kraw[b % 2].rearrange("p (n j) -> p n j", n=2)
                act.activation(kr, kp, ACT.Identity, accum_out=ksum[:, 0, b:b + 1]).then_inc(s_ksum, 1)
                act.wait_ge(s_v, b + 1)
                if b == 0:
                    act.wait_ge(s_one, 1)
                for n in range(2):
                    act.activation(m.v[:, b, 6 * n:6 * n + 6, 0:DH],
                                   m.bank(2 + n)[0:S, 0, 0:INNER // 2].rearrange("p (h e) -> p h e", e=DH),
                                   ACT.Copy).then_inc(s_vc, 1)
                act.wait_ge(s_knm, b + 1)
                act.wait_ge(s_ksum, b + 1)
                if b >= 2:
                    act.wait_ge(s_kTp, b - 1)
                act.activation(kn[b % 2], kraw[b % 2], ACT.Square, bias=ksum[:, 1, b:b + 1],
                               accum_out=ksum[:, 2, b:b + 1]).then_inc(s_kssq, 1)
                act.wait_ge(s_kbias, b + 1)
                act.wait_ge(s_kssq, b + 1)
                act.activation(kn[b % 2], kraw[b % 2], ACT.Identity, bias=ksum[:, 4, b:b + 1],
                               scale=ksum[:, 3, b:b + 1]).then_inc(s_kn, 1)
                if b:
                    keep_keys(b - 1)
            keep_keys(B - 1)
            act.wait_ge(s_vT, 1)
            act.activation(m.vT, m.bank(7)[0:S, 0, 0:2 * B].rearrange("p (k b) -> p k b", k=2),
                           ACT.Copy).then_inc(s_vTc, 1)

        @block.tensor
        def _(pe):
            pe.wait_ge(s_const, 4)
            pe.wait_ge(s_ctx, 16)
            def turn_inputs(b):
                if b >= 2:
                    pe.wait_ge(s_cTc, b - 1)
                for k in range(KD):
                    mm = pe.transpose(m.bank(2 + b % 2)[:, 0, k * S:(k + 1) * S],
                                      m.ctx[:, b, k * P:(k + 1) * P], m.ident[0:S, 0:S])
                mm.then_inc(s_cT, 1)
                pe.wait_ge(s_xn, 2 * b + 2)
                if b >= 2:
                    pe.wait_ge(s_xsq, b - 1)
                for h in range(2):
                    for k in range(KD):
                        mm = pe.transpose(m.bank(b % 2)[:, 0, k * TQ + h * P:k * TQ + (h + 1) * P],
                                          xn[:, 2 * b + h, k * P:(k + 1) * P], m.ident)
                mm.then_inc(s_xT, 1)

            turn_inputs(0)
            for b in range(B):
                if b + 1 < B:
                    turn_inputs(b + 1)
                pe.wait_ge(s_cTc, b + 1)
                pe.wait_ge(s_xTc, b + 1)
                if b >= 2:
                    pe.wait_ge(s_a, b - 1)
                out = m.bank(4 + b % 2)[0:S, 0, 0:TQ]
                for k in range(KD):
                    pe.matmul(out, ctxT[b % 2][:, k, :], xnT[:, b % 2, k, :], start=(k == 0), stop=False)
                pe.wait_ge(s_xsq, b + 1)
                for k in range(KD):
                    mm = pe.matmul(out, ones[:, 0:S], xsq[:, b % 2, k, :], start=False, stop=(k == KD - 1))
                mm.then_inc(s_D, 1)
            pe.wait_ge(s_ab, 2)
            pe.matmul(m.bank(7)[:, 0, 0:2], ones, wsum, start=True, stop=True).then_inc(s_wT, 1)
            for n in range(2):
                pe.wait_ge(s_wqb, n + 1)
                src = wq.rearrange("p (k d) -> p k d", k=HT) if n == 0 else wq.rearrange("p (k h) -> p k h", k=KD)
                for half in range(2):
                    if n == 0 and half:
                        pe.wait_ge(s_tot, 1)
                    if n:
                        pe.wait_ge(s_wTc, half + 1)
                    bank = m.bank(6 + half)[:, 0, :].bitcast(BF16)
                    for k in range(8):
                        if n == 0:
                            out, in_ = bank[:, k * P:(k + 1) * P], src[:, k, half * P:(half + 1) * P]
                        else:
                            tile = 4 * half + k // 2
                            out = bank[:, k * P:(k + 1) * P]
                            in_ = src[:, k % 2, tile * P:(tile + 1) * P]
                        mm = pe.transpose(out, in_, m.identb)
                    mm.then_inc(s_wT, 1)
            def turn_keys(b):
                pe.wait_ge(s_kb, b + 1)
                if b:
                    pe.wait_ge(s_kTc, b)
                for i in range(PAIRS):
                    mm = pe.transpose(m.bank(4)[:, 0, i * S:(i + 1) * S], kn[b % 2][:, i * P:(i + 1) * P],
                                      m.ident[0:S, 0:S])
                mm.then_inc(s_kTp, 1)

            pe.wait_ge(s_kv, 32)
            for b in range(B):
                pe.wait_ge(s_kvb, b + 1)
                if b:
                    pe.wait_ge(s_kvTc, b)
                for k in range(KD):
                    mm = pe.transpose(m.bank(5)[:, 0, k * S:(k + 1) * S], kvn[:, b, k * P:(k + 1) * P],
                                      m.ident[0:S, 0:S])
                mm.then_inc(s_kvTp, 1)
                pe.wait_ge(s_kvTc, b + 1)
                for w, bank, done, read in ((wk, 0, s_k, s_ksum), (wv, 2, s_v, s_vc)):
                    if b:
                        pe.wait_ge(read, b if read is s_ksum else 2 * b)
                    for n in range(2):
                        for k in range(KD):
                            mm = pe.matmul(m.bank(bank + n)[0:S, 0, 0:INNER // 2], kvT[:, k, :],
                                           w[:, k, n * INNER // 2:(n + 1) * INNER // 2],
                                           start=(k == 0), stop=(k == KD - 1))
                    mm.then_inc(done, 1)
                if b:
                    turn_keys(b - 1)
            turn_keys(B - 1)
            pe.wait_ge(s_hop, 1 + (S - 1) // HOPS * (HOPS + 2))
            pe.wait_ge(s_wTc, 4)
            for k in range(2):
                mm = pe.transpose(m.bank(7)[0:S, 0, k * B:(k + 1) * B], path[:, k:k + S], m.ident[0:B, 0:B])
            mm.then_inc(s_vT, 1)

        @block.vector
        def _(dve):
            dve.wait_ge(s_ctx, 16)
            for b in range(B):
                dve.bn_stats(cstats[:, b, :], m.ctx[:, b, :]).then_inc(s_cst, 1)
            for b in range(B):
                dve.wait_ge(s_cst, b + 1)
                dve.bn_aggr(cmv[:, b, :], cstats[:, b, :]).then_inc(s_cmv, 1)
            def statistics(q):
                dve.wait_ge(s_x[q], 16)
                for t in range(4 * q, 4 * q + 4):
                    dve.bn_stats(stats[:, t, :], m.x[:, t, :]).then_inc(s_st, 1)
                for t in range(4 * q, 4 * q + 4):
                    dve.wait_ge(s_st, t + 1)
                    dve.bn_aggr(mv[:, t, :], stats[:, t, :]).then_inc(s_mv, 1)

            def norms(q):
                dve.wait_ge(s_r, q + 1)
                for t in range(4 * q, 4 * q + 4):
                    dve.tensor_scalar(xn[:, t, :], m.x[:, t, :], mv[:, t, 0:1], rstd[:, t:t + 1],
                                      ALU.subtract, ALU.mult).then_inc(s_xn, 1)

            def transposed_context(b):
                dve.wait_ge(s_cT, b + 1)
                if b >= 2:
                    dve.wait_ge(s_D, b - 1)
                dve.tensor_scalar(ctxT[b % 2], m.bank(2 + b % 2)[:, 0, 0:KD * S].rearrange("p (k s) -> p k s", k=KD),
                                  -2.0, None, ALU.mult).then_inc(s_cTc, 1)

            def distances(b):
                if b + 1 < B:
                    transposed_context(b + 1)
                dve.tensor_scalar(kvn[:, b, :], m.ctx[:, b, :], cmv[:, b, 0:1], crstd[:, b:b + 1],
                                  ALU.subtract, ALU.mult).then_inc(s_kvn, 1)
                dve.wait_ge(s_D, b + 1)
                if b:
                    dve.wait_ge(s_dr, b)
                dve.tensor_scalar(sq[:, 0, :], m.bank(4 + b % 2)[0:S, 0, 0:TQ], norm2[:, b:b + 1], 1e-30,
                                  ALU.add, ALU.max).then_inc(s_a, 1)
                dve.wait_ge(s_sq, b + 1)
                dve.reciprocal(sq[:, 2, :], sq[:, 1, :]).then_inc(s_rc, 1)
                dve.wait_ge(s_rc, b + 1)
                dve.wait_ge(s_a, b + 1)
                dve.tensor_tensor(sq[:, 0, :], sq[:, 0, :], sq[:, 2, :], ALU.mult).then_inc(s_ar, 1)
                dve.wait_ge(s_ar, b + 1)
                dve.tensor_tensor(drow[:, b, :], sq[:, 0, :], sq[:, 1, :], ALU.add).then_inc(s_dr, 1)

            statistics(0)
            statistics(1)
            dve.wait_ge(s_const, 4)
            norms(0)
            dve.wait_ge(s_cr, 1)
            dve.wait_ge(s_aa, B)
            transposed_context(0)
            statistics(2)
            norms(1)
            distances(0)
            statistics(3)
            norms(2)
            distances(1)
            norms(3)
            for b in range(2, B):
                distances(b)

            dve.wait_ge(s_init, 6)
            dve.wait_ge(s_dist, 16 * CH)
            to_right = [(p - B) % (CH * B) for p in range(CH * B)]

            def step(base, u, turn_no, near):
                t = base + u
                start = isinstance(base, int) and u == 0
                prev, row = ring[:, (u - 1) % RING, :], ring[:, u, :]
                if not start:
                    dve.wait_ge(s_scan, t)
                    if not (isinstance(base, int) and u < 3):
                        dve.wait_ge(s_bnd, t - 2)
                dve.tensor_tensor(diag, prev[:, 1:CW + 1], prev[:, 0:CW], ALU.min).then_inc(s_min, 1)
                if not start:
                    dve.stream_shuffle(shifted[:, u % 2:u % 2 + 1], prev[:, CW:CW + 1], to_right).then_inc(s_shf, 1)
                dve.wait_ge(s_min, t + 1)
                if not (isinstance(base, int) and u < 2):
                    dve.wait_ge(s_bnd, t - 1)
                if u % GROUP == 0 and not isinstance(base, int):
                    dve.wait_ge(s_cost[u // GROUP], 16 * turn_no)
                dve.tensor_tensor_scan(row[:, 1:CW + 1], diag, near[:, u, :],
                                       first if start else row[:, 0:1], ALU.min, ALU.add).then_inc(s_scan, 1)
                if not start:
                    dve.wait_ge(s_shf, t)
                    dve.tensor_tensor(ring[:, (u + 1) % RING, 0:1], shifted[:, u % 2:u % 2 + 1], floor, ALU.max)\
                       .then_inc(s_bnd, 1)

            for u in range(RING):
                step(0, u, 0, dist)
            with dve.Fori(1, STEPS // RING) as turn_no:
                near = dist[:, bass.ds(turn_no * RING, RING), :]
                for u in range(RING):
                    step(turn_no * RING, u, turn_no, near)

            for g in range(RING // GROUP):
                dve.wait_ge(s_cost[g], 16 * STEPS // RING)
            for buf in (cost, above):
                dve.memset(buf[:, :, 0:1], BIG).then_inc(s_cm, 1)
            dve.memset(above[0:1, :, 1:W1], BIG).then_inc(s_cm, 1)
            dve.wait_ge(s_cm, 3)
            dve.wait_ge(s_cl0, 32 * CH)
            dve.wait_ge(s_cl, 32 * CH)
            up, corner, left = above[:, :, 1:W1], above[:, :, 0:TQ], cost[:, :, 0:TQ]
            iota_b = m.iota[0:S, :].unsqueeze(1).to_broadcast([S, B, TQ])
            dve.tensor_tensor(best, up, corner, ALU.min).then_inc(s_F, 1)
            dve.tensor_tensor(turn, corner, up, ALU.is_le).then_inc(s_F, 1)
            dve.wait_ge(s_F, 1)
            dve.tensor_tensor(stay, left, best, ALU.is_ge).then_inc(s_F, 1)
            dve.wait_ge(s_F, 2)
            dve.scalar_tensor_tensor(turn, turn, -0.75, iota_b, ALU.mult, ALU.add).then_inc(s_F, 1)
            dve.wait_ge(s_F, 4)
            dve.tensor_tensor(turn, turn, stay, ALU.mult).then_inc(s_F, 1)
            dve.wait_ge(s_F, 5)
            for b in range(B):
                scan = dve.tensor_tensor_scan(jump[:, b, :], turn[:, b, :], turn[:, b, :], 0.0, ALU.max, ALU.max)
            scan.then_inc(s_F, 1)
            dve.wait_ge(s_F, 6)
            dve.tensor_copy(djump[:, :, 0:1], jump[:, :, 0:1]).then_inc(s_cm, 1)
            dve.tensor_tensor(djump[:, :, 1:TQ], jump[:, :, 1:TQ], jump[:, :, 0:TQ - 1], ALU.subtract)\
               .then_inc(s_F, 1)
            dve.wait_ge(s_djld, 16)
            dve.wait_ge(s_hop, 1)
            with dve.Fori(0, (S - 1) // HOPS) as n:
                low = n * -HOPS + (S - HOPS)
                jumps = djump_b[:, bass.ds(low, HOPS), :]
                for u in reversed(range(HOPS)):
                    dve.wait_ge(s_hop, n * (HOPS + 2) + (HOPS - u))
                    dve.scalar_tensor_tensor(hopjunk, m.iota[0:B, :], near_path[:, u + 1:u + 2], jumps[:, u, :],
                                             ALU.is_le, ALU.mult, accum_out=near_path[:, u:u + 1]).then_inc(s_hop, 1)
                dve.wait_ge(s_hop, n * (HOPS + 2) + (HOPS + 1))
                dve.tensor_copy(near_path[:, HOPS:HOPS + 1], near_path[:, 0:1]).then_inc(s_hop, 1)
                dve.tensor_copy(path[:, bass.ds(low, HOPS)], near_path[:, 0:HOPS]).then_inc(s_hop, 1)


def pipeline(eng, stages, count, head):
    assert head % 2 == 0
    depth = max(lag for _, lag in stages)

    def turn(k):
        for stage, lag in stages:
            if 0 <= k - lag < count:
                stage(k - lag, (k - lag) % 2)

    for k in range(head):
        turn(k)
    tail = max(head, (count - 2) // 2 * 2)
    if head < tail:
        with eng.Fori(head // 2, tail // 2) as i:
            for u in range(2):
                for stage, lag in stages:
                    stage(i * 2 + (u - lag), (u - lag) % 2)
    for k in range(tail, count + depth):
        turn(k)


class Waits:

    def __init__(self, eng, tick):
        self.eng, self.tick = eng, tick

    def __call__(self, sem, n, alone=False):
        if isinstance(n, int):
            if n > 0:
                self.eng.wait_ge(sem, n)
        else:
            self.eng.wait_ge(sem, n)
            if alone:
                self.eng.sem_inc(self.tick, 1)


def ffn(nc, ctx, m, a):
    def sem(name):
        return nc.alloc_semaphore("f_" + name)

    arena = m.arena
    b1, g2, c2, g1, c1, b2 = ffn_vectors(m)
    def pair(cols, dtype=F32, parts=P):
        return [arena.take(parts, cols, dtype) for _ in range(2)]
    h, hq, hqT = pair(D), pair(D, BF16), arena.take(P, D, BF16)
    z, w, zq, zqT = pair(HID), pair(HID), pair(HID, BF16), arena.take(P, HID, BF16)
    out1 = arena.take(P, D)
    mask = m.late.take(S, TQ)
    half_mask = m.late.take(S, TQ)
    junk = m.late.take(P, HID, BF16)
    st1, mv1, r1, am1, inv1, sc1, f1 = pair(6), pair(2), pair(1), pair(1), pair(1), pair(1), pair(1)
    sum2, neg2, sq2, r2, am2, inv2, sc2, f2 = (pair(1) for _ in range(8))
    magic, unmagic = arena.take(P, 1), arena.take(P, 1)

    HEAD = 8

    names = ("start mhalf mask E x1 st1 mv1 v1 r1 t1 h am1 inv1 sc1 f1 hr hq T1 hqT Z z g neg2 sq2 v2 r2 "
             "t2 n2 h2 am2 inv2 sc2 f2 zr zq T2 zqT Y y x2").split()
    q = {n: sem(n) for n in names}

    def work(t):
        return m.x[:, bass.ds(t, 1), :].rearrange("p t d -> p (t d)")

    with nc.Block() as block:
        @block.sync
        def _(sp):
            sp.dma_start(m.wa.rearrange("p (k n) -> p k n", k=KD),
                         a["L1_xattn_Wq"].rearrange("(k p) n -> p k n", p=P)).then_inc(m.ld_attn, 16)
            sp.dma_start(m.wb.rearrange("p (k n) -> p k n", k=PAIRS),
                         a["L1_xattn_Wo"].rearrange("(k p) n -> p k n", p=P)).then_inc(m.ld_attn, 16)
            for dst, src in ((m.qg, a["L1_xattn_q_g"]), (m.qb, a["L1_xattn_q_b"]), (m.vg, a["L1_xattn_vid_g"]),
                             (m.vb, a["L1_xattn_vid_b"]), (m.bo, a["L1_xattn_bo"])):
                sp.dma_start(dst, bcast(src, P)).then_inc(m.ld_attn, 16)
            sp.dma_start(m.early.tensor[:, :].rearrange("p (e k h) -> p e k h", e=NE, k=KD),
                         a["L1_ffn_W1"].rearrange("e (k p) h -> p e k h", p=P)).then_inc(m.ld_w1, 16)

        @block.gpsimd
        def _(pool):
            wait = Waits(pool, sem("tick_pool"))
            pool.memset(magic, MAGIC).then_inc(q["start"], 1)
            pool.memset(unmagic, -MAGIC).then_inc(q["start"], 1)

            def rstd1(t, p):
                wait(q["mv1"], t + 1, alone=True)
                wait(q["h"], t - 1, alone=True)
                pool.tensor_scalar(r1[p], mv1[p][:, 1:2], 1.0 + LN_EPS, LN_EPS * LN_EPS, ALU.mult,
                                   ALU.add).then_inc(q["v1"], 1)
                wait(q["v1"], t + 1)
                pool.tensor_tensor(r1[p], r1[p], m.power[:, 0:1], ALU.pow).then_inc(q["r1"], 1)

            def mean2(t, p):
                wait(q["g"], t + 1, alone=True)
                wait(q["t2"], t - 1, alone=True)
                pool.tensor_scalar(neg2[p], sum2[p], -1.0 / HID, None, ALU.mult).then_inc(q["neg2"], 1)

            def rstd2(t, p):
                wait(q["sq2"], t + 1, alone=True)
                wait(q["t2"], t - 1, alone=True)
                pool.tensor_scalar(r2[p], sq2[p], 1.0 / HID, LN_EPS, ALU.mult, ALU.add).then_inc(q["v2"], 1)
                wait(q["v2"], t + 1)
                pool.tensor_tensor(r2[p], r2[p], m.power[:, 0:1], ALU.pow).then_inc(q["r2"], 1)

            def affine2(t, p):
                wait(q["t2"], t + 1)
                pool.tensor_tensor(w[p], w[p], g2, ALU.mult).then_inc(q["n2"], 1)
                wait(q["n2"], t + 1)
                pool.tensor_tensor(w[p], w[p], c2, ALU.add).then_inc(q["h2"], 1)

            pipeline(pool, [(rstd1, 0), (mean2, 3), (rstd2, 3), (affine2, 4)], TILES, HEAD)

        @block.scalar
        def _(act):
            wait = Waits(act, sem("tick_act"))

            act.wait_ge(q["start"], 2)

            def scale1(t, p):
                wait(q["sc1"], t + 1)
                act.activation(h[p], h[p], ACT.Identity, bias=magic, scale=sc1[p]).then_inc(q["hr"], 1)

            def round1(t, p):
                wait(q["hr"], t + 1)
                wait(q["T1"], t - 1)
                act.activation(hq[p], h[p], ACT.Identity, bias=unmagic).then_inc(q["hq"], 1)

            def copy1(t, p):
                wait(q["T1"], t + 1)
                wait(q["Z"], t)
                act.activation(hqT, m.bank(1)[:, 0, 0:P].bitcast(BF16), ACT.Copy)\
                   .then_inc(q["hqT"], 1)

            def gelu(t, p):
                wait(q["z"], t + 1)
                wait(q["neg2"], t - 1)
                act.activation(z[p], z[p], ACT.Gelu, accum_out=sum2[p]).then_inc(q["g"], 1)

            def square(t, p):
                wait(q["neg2"], t + 1)
                wait(q["v2"], t - 1)
                wait(q["sq2"], t)
                act.activation(junk, z[p], ACT.Square, bias=neg2[p], accum_out=sq2[p]).then_inc(q["sq2"], 1)

            def scale2(t, p):
                wait(q["sc2"], t + 1)
                act.activation(w[p], w[p], ACT.Identity, bias=magic, scale=sc2[p]).then_inc(q["zr"], 1)

            def round2(t, p):
                wait(q["zr"], t + 1)
                wait(q["T2"], t - 1)
                act.activation(zq[p], w[p], ACT.Identity, bias=unmagic).then_inc(q["zq"], 1)

            def copy2(t, p):
                wait(q["T2"], t + 1)
                wait(q["Y"], t)
                act.activation(zqT, m.bank(6)[:, 0, :].bitcast(BF16), ACT.Copy).then_inc(q["zqT"], 1)

            pipeline(act, [(copy1, 2), (gelu, 3), (copy2, 6), (square, 3), (scale1, 1), (round1, 1), (scale2, 5),
                           (round2, 5)], TILES, HEAD)

        @block.tensor
        def _(pe):
            wait = Waits(pe, sem("tick_pe"))

            def aligned(t, p):
                b = t // 2 if isinstance(t, int) else (t - p) // 2
                wait(q["mask"], (t // 2 if isinstance(t, int) else b) + 1)
                wait(q["x1"], t)
                pe.matmul(m.bank(0)[:, 0, 0:D], mask[:, p * P:(p + 1) * P],
                          m.ctx[:, bass.ds(b, 1), :].rearrange("s b d -> s (b d)"), start=True, stop=True)\
                  .then_inc(q["E"], 1)

            def turn1(t, p):
                wait(q["hq"], t + 1)
                wait(q["hqT"], t)
                for k in range(KD):
                    mm = pe.transpose(m.bank(1)[:, 0, k * 64:(k + 1) * 64].bitcast(BF16),
                                      hq[p][:, k * P:(k + 1) * P], m.identb)
                mm.then_inc(q["T1"], 1)

            def up(t, p):
                wait(q["hqT"], t + 1)
                wait(q["z"], t - 1)
                for n in range(2):
                    for k in range(KD):
                        mm = pe.matmul(m.bank(2 + 2 * p + n)[:, 0, :], hqT[:, k * P:(k + 1) * P],
                                       m.w1T[:, k, n * 512:(n + 1) * 512], start=(k == 0), stop=(k == KD - 1))
                mm.then_inc(q["Z"], 1)

            def turn2(t, p):
                wait(q["zq"], t + 1)
                wait(q["zqT"], t)
                for k in range(HT):
                    mm = pe.transpose(m.bank(6)[:, 0, k * 64:(k + 1) * 64].bitcast(BF16),
                                      zq[p][:, k * P:(k + 1) * P], m.identb)
                mm.then_inc(q["T2"], 1)

            def down(t, p):
                wait(q["zqT"], t + 1)
                wait(q["y"], t)
                for k in range(HT):
                    mm = pe.matmul(m.bank(7)[:, 0, 0:D], zqT[:, k * P:(k + 1) * P],
                                   m.w2T[:, k, :], start=(k == 0), stop=(k == HT - 1))
                mm.then_inc(q["Y"], 1)

            pipeline(pe, [(aligned, 0), (turn1, 2), (turn2, 6), (up, 2), (down, 6)], TILES, HEAD)

        @block.vector
        def _(dve):
            wait = Waits(dve, sem("tick_dve"))
            dve.wait_ge(m.ld_ffn, 96)

            def path_mask(b):
                v0, v1 = (m.vT[:, k, bass.ds(b, 1)] for k in range(2))
                wait(q["mask"], b)
                dve.tensor_scalar(half_mask, m.iota[0:S, :], v0, None, ALU.is_ge).then_inc(q["mhalf"], 1)
                wait(q["mhalf"], b + 1)
                dve.scalar_tensor_tensor(mask, m.iota[0:S, :], v1, half_mask, ALU.is_le, ALU.mult)\
                   .then_inc(q["mask"], 1)

            def next_mask(t, p):
                if p and not (isinstance(t, int) and t == TILES - 1):
                    wait(q["E"], t + 1)
                    path_mask((t + 1) // 2)

            def add_aligned(t, p):
                wait(q["E"], t + 1)
                dve.scalar_tensor_tensor(work(t), m.bank(0)[:, 0, 0:D], m.tanh[:, 0:1], work(t),
                                         ALU.mult, ALU.add).then_inc(q["x1"], 1)

            def stats1(t, p):
                wait(q["x1"], t + 1, alone=True)
                wait(q["mv1"], t - 1, alone=True)
                dve.bn_stats(st1[p], work(t)).then_inc(q["st1"], 1)

            def gather1(t, p):
                wait(q["st1"], t + 1, alone=True)
                wait(q["r1"], t - 1, alone=True)
                dve.bn_aggr(mv1[p], st1[p]).then_inc(q["mv1"], 1)

            def largest(t, p, k, am, src):
                dve.tensor_reduce(am[p], src, AX.X, ALU.max, apply_absolute_value=True).then_inc(q["am" + k], 1)

            def unit(t, p, k, am, inv):
                wait(q["am" + k], t + 1)
                dve.tensor_scalar(inv[p], am[p], 1e-5, 1.0 / 127.0, ALU.max, ALU.mult).then_inc(q["inv" + k], 1)

            def factors(t, p, k, inv, sc, f, wscale):
                wait(q["inv" + k], t + 1)
                dve.reciprocal(sc[p], inv[p]).then_inc(q["sc" + k], 1)
                dve.tensor_tensor(f[p], inv[p], wscale, ALU.mult).then_inc(q["f" + k], 1)

            def center1(t, p):
                wait(q["r1"], t + 1)
                wait(q["hq"], t - 1)
                wait(q["z"], t - 1)
                dve.scalar_tensor_tensor(h[p], work(t), mv1[p][:, 0:1], g1, ALU.subtract, ALU.mult)\
                   .then_inc(q["t1"], 1)

            def affine1(t, p):
                wait(q["t1"], t + 1)
                dve.scalar_tensor_tensor(h[p], h[p], r1[p], c1, ALU.mult, ALU.add).then_inc(q["h"], 1)

            def largest1(t, p):
                wait(q["h"], t + 1)
                wait(q["inv1"], t - 1)
                largest(t, p, "1", am1, h[p])

            def unit1(t, p):
                wait(q["f1"], t - 1)
                unit(t, p, "1", am1, inv1)

            def factors1(t, p):
                factors(t, p, "1", inv1, sc1, f1, m.wscale[:, 0:1])

            def hidden(t, p):
                wait(q["Z"], t + 1)
                wait(q["f1"], t + 1)
                wait(q["t2"], t - 1)
                dve.scalar_tensor_tensor(z[p], m.bank(2 + 2 * p, 2).rearrange("p n j -> p (n j)"), f1[p], b1,
                                         ALU.mult, ALU.add).then_inc(q["z"], 1)

            def center2(t, p):
                wait(q["neg2"], t + 1)
                wait(q["sq2"], t + 1)
                wait(q["zq"], t - 1)
                wait(q["r2"], t + 1)
                dve.tensor_scalar(w[p], z[p], neg2[p], r2[p], ALU.add, ALU.mult).then_inc(q["t2"], 1)

            def largest2(t, p):
                wait(q["h2"], t + 1)
                wait(q["inv2"], t - 1)
                largest(t, p, "2", am2, w[p])

            def unit2(t, p):
                wait(q["f2"], t - 1)
                unit(t, p, "2", am2, inv2)

            def factors2(t, p):
                factors(t, p, "2", inv2, sc2, f2, m.wscale[:, 1:2])

            def add_out(t, p):
                wait(q["Y"], t + 1)
                wait(q["f2"], t + 1)
                wait(q["x2"], t)
                dve.scalar_tensor_tensor(out1, m.bank(7)[:, 0, 0:D], f2[p], b2,
                                         ALU.mult, ALU.add).then_inc(q["y"], 1)

            def add_x2(t, p):
                wait(q["y"], t + 1)
                dve.scalar_tensor_tensor(work(t), out1, m.tanh[:, 2:3], work(t), ALU.mult, ALU.add)\
                   .then_inc(q["x2"], 1)

            path_mask(0)
            pipeline(dve, [(hidden, 3), (add_aligned, 0), (center1, 1), (stats1, 0), (affine1, 1),
                           (gather1, 0), (largest1, 1), (unit1, 1), (factors1, 1), (center2, 4), (next_mask, 0),
                           (largest2, 5), (unit2, 5), (factors2, 5), (add_out, 6), (add_x2, 6)], TILES, HEAD)


def cap(n):
    return min(n, TILES) if isinstance(n, int) else n


def attention(nc, ctx, m, a):
    def sem(name):
        return ctx.enter_context(nc.semaphore("a_" + name))

    arena = m.arena
    arena.at = 0
    def pair(cols):
        return [arena.take(P, cols) for _ in range(2)]
    h, hT = arena.take(P, D), arena.take(P, D)
    qn, qT, prob, o, oT = pair(INNER), pair(INNER), pair(HEADS * S), pair(INNER), pair(INNER)
    pT = arena.take(S, HEADS * P).rearrange("s (h j) -> s h j", h=HEADS)
    kb = arena.take(P, PAIRS * 2 * S).rearrange("p (i n s) -> p i n s", i=PAIRS, n=2)
    out1 = m.spare.take(P, D)
    st, mv, r = pair(6), pair(2), pair(1)
    spare = m.spare
    m.b2 = spare.take(P, NE * D).rearrange("p (e d) -> p e d", e=NE)
    m.logit = spare.take(P, TILES * NE).rearrange("p (t e) -> p t e", t=TILES)
    m.b1 = spare.take(NE * HT, P)
    wg = spare.take(P, KD * NE).rearrange("p (k e) -> p k e", k=KD)
    bg = spare.take(P, NE)
    y, yT = ([spare.take(P, D) for _ in range(2)] for _ in range(2))
    sty, mvy, ry = ([spare.take(P, n) for _ in range(2)] for n in (6, 2, 1))
    m.sum_dram = nc.dram_tensor("sum_dram", [(TILES + 1) * P, D], F32, kind="Internal").ap()
    m.y_dram = nc.dram_tensor("y_dram", [TILES * P, D], F32, kind="Internal").ap()
    stq, mvq, rq, top, rden = pair(12), pair(2), pair(1), arena.take(P, HEADS), arena.take(P, HEADS)
    wq = m.wa.rearrange("p (k n) -> p k n", k=KD)
    wo = m.wb.rearrange("p (i n) -> p i n", i=PAIRS)
    HALF = INNER // 2
    HEAD = 10

    names = ("st mv v r t1 h xT hT k0 q stq mvq vq rq qg qn qT qTc kb S top sub exp PT PTc PV rden o oT oTc out o1 x3 "
             "qscale ldg sty mvy vy ry y yp yT G lg st_x").split()
    q = {n: sem(n) for n in names}
    st_y = [sem(f"st_y{p}") for p in range(2)]

    s_ps = m.bank(0, 2)[:, :, 0:HEADS // 2 * S]
    q_ps = m.bank(2, 2)[:, :, 0:HALF]
    t_ps = m.bank(4, 2)[:, :, 0:HALF]
    p_ps = m.bank(6, 2)[:, :, 0:HALF]
    PVW = DH + 1
    pv_ps = [m.bank(3)[:, 0, 0:6 * PVW].rearrange("p (h e) -> p h e", h=6),
             m.bank(2)[:, 0, 0:6 * PVW].rearrange("p (h e) -> p h e", h=6)]

    def work(t):
        return m.x[:, bass.ds(t, 1), :].rearrange("p t d -> p (t d)")

    def halves(x):
        return x.rearrange("p (n c) -> p n c", n=2)

    def tile(x, t):
        return x[:, bass.ds(t, 1), :].rearrange("p t d -> p (t d)")

    with nc.Block() as block:
        @block.sync
        def _(sp):
            wait = Waits(sp, sem("tick_sp"))
            for dst, src in ((wg, a["L1_ffn_Wg"].rearrange("(k p) e -> p k e", p=P)), (bg, bcast(a["L1_ffn_bg"], P)),
                             (m.b1, a["L1_ffn_b1"].rearrange("e (k p) -> (e k) p", p=P)),
                             (m.b2.rearrange("p e d -> p (e d)"), bcast(a["L1_ffn_b2"].rearrange("e d -> (e d)"), P))):
                sp.dma_start(dst, src).then_inc(q["ldg"], 16)

            def store(t, p):
                wait(q["y"], t + 1)
                sp.dma_start(m.y_dram[bass.ds(t * P, P), :], y[p]).then_inc(st_y[p], 16)

            def store_x(t, p):
                wait(q["x3"], t + 1)
                sp.dma_start(m.sum_dram[bass.ds(t * P, P), :], work(t)).then_inc(q["st_x"], 16)

            pipeline(sp, [(store_x, 0), (store, 0)], TILES, 6)
            sp.dma_start(m.sum_dram[TILES * P:(TILES + 1) * P, :], m.x[:, 0, :]).then_inc(q["st_x"], 16)
            sp.wait_ge(q["st_x"], 16 * (TILES + 1))
            for p in range(2):
                sp.wait_ge(st_y[p], 16 * TILES // 2)

        @block.gpsimd
        def _(pool):
            wait = Waits(pool, sem("tick_pool"))

            def keys(b):
                for n in range(2):
                    rows = slice(n * DH, (n + 1) * DH)
                    pool.tensor_copy(kb[rows, :, n, :],
                                     m.kT[rows, :, bass.ds(b, 1), :].rearrange("p i b s -> p i (b s)"))\
                        .then_inc(q["kb"], 1)
                    wait(q["kb"], b * 2 + n + 1, alone=True)

            def rstd(t, p):
                wait(q["mv"], t + 1, alone=True)
                wait(q["h"], t - 1, alone=True)
                pool.tensor_scalar(r[p], mv[p][:, 1:2], 1.0 + LN_EPS, LN_EPS * LN_EPS, ALU.mult, ALU.add)\
                    .then_inc(q["v"], 1)
                wait(q["v"], t + 1)
                pool.tensor_tensor(r[p], r[p], m.power[:, 0:1], ALU.pow).then_inc(q["r"], 1)

            def rstd_q(t, p):
                wait(q["mvq"], t + 1, alone=True)
                wait(q["qn"], t - 1, alone=True)
                pool.tensor_scalar(rq[p], mvq[p][:, 1:2], LN_EPS, None, ALU.add).then_inc(q["vq"], 1)
                wait(q["vq"], t + 1)
                pool.tensor_tensor(rq[p], rq[p], m.power[:, 0:1], ALU.pow).then_inc(q["rq"], 1)

            def next_keys(t, p):
                if p and not (isinstance(t, int) and t == TILES - 1):
                    wait(q["S"], t + 1, alone=True)
                    keys((t + 1) // 2)

            def rstd_y(t, p):
                wait(q["mvy"], t + 1, alone=True)
                wait(q["y"], t - 1, alone=True)
                pool.tensor_scalar(ry[p], mvy[p][:, 1:2], LN_EPS, None, ALU.add).then_inc(q["vy"], 1)
                wait(q["vy"], t + 1)
                pool.tensor_tensor(ry[p], ry[p], m.power[:, 0:1], ALU.pow).then_inc(q["ry"], 1)

            pool.memset(kb, 0.0).then_inc(q["k0"], 1)
            pool.wait_ge(q["k0"], 1)
            keys(0)
            pipeline(pool, [(rstd, 0), (rstd_q, 2), (next_keys, 3), (rstd_y, 5)], TILES, HEAD)

        @block.scalar
        def _(act):
            wait = Waits(act, sem("tick_act"))

            def copy_x(t, p):
                wait(q["xT"], t + 1)
                wait(q["q"], t)
                act.activation(hT, m.bank(6)[:, 0, 0:D], ACT.Copy).then_inc(q["hT"], 1)

            def copy_q(t, p):
                wait(q["qT"], t + 1)
                wait(q["S"], t - 1)
                act.activation(halves(qT[p]), t_ps, ACT.Copy).then_inc(q["qTc"], 1)

            def exponent(t, p):
                wait(q["sub"], t + 1)
                act.activation(prob[p], prob[p], ACT.Exp).then_inc(q["exp"], 1)

            def copy_p(n):
                def stage(t, p):
                    wait(q["PT"], t * 2 + n + 1)
                    wait(q["PV"], t * 2 - 1 + n)
                    act.activation(halves(pT[:, 6 * n:6 * n + 6, :].rearrange("s h j -> s (h j)")), p_ps[0:S],
                                   ACT.Copy).then_inc(q["PTc"], 1)
                return stage

            def copy_o(t, p):
                wait(q["oT"], t + 1)
                wait(q["out"], t - 1)
                act.activation(halves(oT[p]), t_ps, ACT.Copy).then_inc(q["oTc"], 1)

            def copy_y(t, p):
                wait(q["yp"], t + 1)
                wait(q["xT"], cap(t + 6))
                wait(q["G"], t - 1)
                act.activation(yT[p], m.bank(6)[:, 0, D:2 * D], ACT.Copy).then_inc(q["yT"], 1)

            pipeline(act, [(copy_x, 2), (copy_q, 3), (copy_y, 7), (copy_p(0), 4), (copy_o, 5), (copy_p(1), 4),
                           (exponent, 3)], TILES, HEAD)

        @block.tensor
        def _(pe):
            wait = Waits(pe, sem("tick_pe"))
            pe.wait_ge(m.ld_attn, 112)

            def turn_x(t, p):
                wait(q["h"], t + 1)
                if isinstance(t, int):
                    wait(q["hT"], t)
                wait(q["PTc"], t * 2 - 4)
                for k in range(KD):
                    mm = pe.transpose(m.bank(6)[:, 0, k * P:(k + 1) * P], h[:, k * P:(k + 1) * P], m.ident)
                mm.then_inc(q["xT"], 1)

            def turn_y(t, p):
                wait(q["y"], t + 1)
                wait(q["yT"], t)
                wait(q["PTc"], cap(t + 3) * 2)
                for k in range(KD):
                    mm = pe.transpose(m.bank(6)[:, 0, D + k * P:D + (k + 1) * P], y[p][:, k * P:(k + 1) * P],
                                      m.ident)
                mm.then_inc(q["yp"], 1)

            def logits(t, p):
                if isinstance(t, int) and t == 0:
                    wait(q["ldg"], 64)
                wait(q["yT"], t + 1)
                wait(q["qg"], cap(t + 6))
                wait(q["o"], cap(t + 3) * 2)
                wait(q["lg"], t)
                for k in range(KD):
                    mm = pe.matmul(m.bank(2)[:, 0, D:D + NE], yT[p][:, k * P:(k + 1) * P], wg[:, k, :],
                                   start=(k == 0), stop=(k == KD - 1))
                mm.then_inc(q["G"], 1)

            def query(t, p):
                wait(q["hT"], t + 1)
                if isinstance(t, int):
                    wait(q["qg"], t)
                wait(q["o"], t * 2 - 4)
                for n in range(2):
                    for k in range(KD):
                        mm = pe.matmul(q_ps[:, n, :], hT[:, k * P:(k + 1) * P], wq[:, k, n * HALF:(n + 1) * HALF],
                                       start=(k == 0), stop=(k == KD - 1))
                mm.then_inc(q["q"], 1)

            def turn_q(t, p):
                wait(q["qn"], t + 1)
                if isinstance(t, int):
                    wait(q["qTc"], t)
                wait(q["oTc"], t - 2)
                for i in range(PAIRS):
                    mm = pe.transpose(t_ps[:, i // 3, i % 3 * P:(i % 3 + 1) * P], qn[p][:, i * P:(i + 1) * P],
                                      m.ident)
                mm.then_inc(q["qT"], 1)

            def scores(t, p):
                b = (t - p) // 2
                wait(q["qTc"], t + 1)
                wait(q["kb"], b * 2 + 2)
                wait(q["sub"], t)
                for i in range(PAIRS):
                    mm = pe.matmul(s_ps[:, i // 3, i % 3 * 2 * S:(i % 3 + 1) * 2 * S],
                                   qT[p][:, i * P:(i + 1) * P], kb[:, i, :, :].rearrange("p n s -> p (n s)"),
                                   start=True, stop=True)
                mm.then_inc(q["S"], 1)

            def turn_p(n):
                def stage(t, p):
                    wait(q["exp"], t + 1)
                    if not n:
                        wait(q["hT"], cap(t + 3))
                        wait(q["yT"], t - 2)
                    wait(q["PTc"], t * 2 + n)
                    for i in range(6):
                        j = 6 * n + i
                        mm = pe.transpose(p_ps[0:S, i // 3, i % 3 * P:(i % 3 + 1) * P],
                                          prob[p][:, j * S:(j + 1) * S], m.ident)
                    mm.then_inc(q["PT"], 1)
                return stage

            def turn_o(t, p):
                wait(q["o"], t * 2 + 2)
                wait(q["qTc"], cap(t + 3))
                for i in range(PAIRS):
                    mm = pe.transpose(t_ps[:, i // 3, i % 3 * P:(i % 3 + 1) * P], o[p][:, i * P:(i + 1) * P],
                                      m.ident)
                mm.then_inc(q["oT"], 1)

            def output(t, p):
                wait(q["oTc"], t + 1)
                wait(q["qg"], cap(t + 4))
                for i in range(PAIRS):
                    mm = pe.matmul(m.bank(2)[:, 0, 0:D], oT[p][:, i * P:(i + 1) * P], wo[:, i, :],
                                   start=(i == 0), stop=(i == PAIRS - 1))
                mm.then_inc(q["out"], 1)

            def values(n):
                def stage(t, p):
                    b = (t - p) // 2
                    wait(q["PTc"], t * 2 + n + 1)
                    wait(q["qg"], cap(t + 3))
                    if n:
                        wait(q["o1"], t)
                        wait(q["lg"], t - 2)
                    for i in range(6):
                        mm = pe.matmul(pv_ps[n][:, i, :], pT[:, 6 * n + i, :],
                                       m.v[:, bass.ds(b, 1), 6 * n + i, :].rearrange("s b e -> s (b e)"),
                                       start=True, stop=True)
                    mm.then_inc(q["PV"], 1)
                return stage

            pipeline(pe, [(turn_y, 7), (turn_x, 2), (turn_q, 3), (query, 2), (turn_p(0), 4), (turn_o, 5), (scores, 3),
                          (turn_p(1), 4), (logits, 7), (output, 5), (values(0), 4), (values(1), 4)],
                     TILES, HEAD)

        @block.vector
        def _(dve):
            wait = Waits(dve, sem("tick_dve"))
            dve.wait_ge(m.ld_attn, 112)
            dve.tensor_scalar(m.qg, m.qg, DH ** -0.5, None, ALU.mult).then_inc(q["qscale"], 1)
            dve.tensor_scalar(m.qb, m.qb, DH ** -0.5, None, ALU.mult).then_inc(q["qscale"], 1)
            dve.wait_ge(q["qscale"], 2)

            def stats(t, p):
                wait(q["mv"], t - 1, alone=True)
                dve.bn_stats(st[p], work(t)).then_inc(q["st"], 1)
                wait(q["st"], t + 1, alone=True)
                wait(q["r"], t - 1, alone=True)
                dve.bn_aggr(mv[p], st[p]).then_inc(q["mv"], 1)

            def norm(t, p):
                wait(q["r"], t + 1)
                wait(q["xT"], t)
                dve.scalar_tensor_tensor(h, work(t), mv[p][:, 0:1], m.vg, ALU.subtract, ALU.mult)\
                   .then_inc(q["t1"], 1)
                wait(q["t1"], t + 1)
                dve.scalar_tensor_tensor(h, h, r[p], m.vb, ALU.mult, ALU.add).then_inc(q["h"], 1)

            def query_stats(t, p):
                wait(q["q"], t + 1)
                wait(q["mvq"], t - 1)
                for n in range(2):
                    dve.bn_stats(stq[p][:, 6 * n:6 * n + 6], q_ps[:, n, :]).then_inc(q["stq"], 1)
                wait(q["stq"], t * 2 + 2, alone=True)
                wait(q["rq"], t - 1, alone=True)
                dve.bn_aggr(mvq[p], stq[p]).then_inc(q["mvq"], 1)
                wait(q["mvq"], t + 1)
                wait(q["qT"], t - 1)
                dve.scalar_tensor_tensor(halves(qn[p]), q_ps, mvq[p][:, 0:1], halves(m.qg), ALU.subtract,
                                         ALU.mult).then_inc(q["qg"], 1)

            def query_norm(t, p):
                wait(q["rq"], t + 1)
                wait(q["qg"], t + 1)
                dve.scalar_tensor_tensor(qn[p], qn[p], rq[p], m.qb, ALU.mult, ALU.add).then_inc(q["qn"], 1)

            def shift(t, p):
                s4 = s_ps.rearrange("p n (h s) -> p n h s", s=S)
                wait(q["S"], t + 1)
                wait(q["sub"], t)
                dve.tensor_reduce(top.rearrange("p (n h) -> p n h", n=2), s4, AX.X, ALU.max).then_inc(q["top"], 1)
                wait(q["top"], t + 1)
                wait(q["PT"], t * 2 - 2)
                dve.tensor_tensor(prob[p].rearrange("p (n h s) -> p n h s", n=2, s=S), s4,
                                  top.rearrange("p (n h) -> p n h", n=2).unsqueeze(3)
                                  .to_broadcast([P, 2, 6, S]), ALU.subtract).then_inc(q["sub"], 1)

            def average(t, p):
                for n in range(2):
                    wait(q["PV"], t * 2 + n + 1)
                    wait(q["o"], t * 2 + n - 1)
                    dve.reciprocal(rden[:, 6 * n:6 * n + 6], pv_ps[n][:, :, DH]).then_inc(q["rden"], 1)
                    wait(q["rden"], t * 2 + n + 1)
                    wait(q["oT"], t - 1)
                    dve.tensor_tensor(o[p].rearrange("p (n h e) -> p n h e", n=2, e=DH)[:, n],
                                      pv_ps[n][:, :, 0:DH],
                                      rden[:, 6 * n:6 * n + 6].unsqueeze(2).to_broadcast([P, 6, DH]),
                                      ALU.mult).then_inc(q["o"], 1)

            def add_out(t, p):
                wait(q["out"], t + 1)
                wait(q["x3"], t)
                dve.tensor_tensor(out1, m.bank(2)[:, 0, 0:D], m.bo, ALU.add).then_inc(q["o1"], 1)

            def add_x(t, p):
                wait(q["o1"], t + 1)
                dve.scalar_tensor_tensor(work(t), out1, m.tanh[:, 1:2], work(t), ALU.mult, ALU.add)\
                   .then_inc(q["x3"], 1)

            def stats_y(t, p):
                wait(q["x3"], t + 1, alone=True)
                wait(q["mvy"], t - 1, alone=True)
                dve.bn_stats(sty[p], work(t)).then_inc(q["sty"], 1)
                wait(q["sty"], t + 1, alone=True)
                wait(q["ry"], t - 1, alone=True)
                dve.bn_aggr(mvy[p], sty[p]).then_inc(q["mvy"], 1)

            def norm_y(t, p):
                wait(q["ry"], t + 1)
                wait(q["yp"], t - 1)
                wait(st_y[p], t * 8 - p * 8)
                dve.tensor_scalar(y[p], work(t), mvy[p][:, 0:1], ry[p], ALU.subtract, ALU.mult)\
                   .then_inc(q["y"], 1)

            def keep_logits(t, p):
                if isinstance(t, int) and t == 0:
                    wait(q["ldg"], 64)
                wait(q["G"], t + 1)
                wait(q["out"], cap(t + 3))
                dve.tensor_tensor(tile(m.logit, t), m.bank(2)[:, 0, D:D + NE], bg, ALU.add).then_inc(q["lg"], 1)

            pipeline(dve, [(stats, 0), (norm_y, 6), (norm, 1), (query_stats, 2), (shift, 3), (query_norm, 2),
                           (add_out, 5), (keep_logits, 7), (average, 4), (add_x, 5), (stats_y, 5)], TILES, HEAD)



def route(nc, ctx, m, a):
    def sem(name):
        return ctx.enter_context(nc.semaphore("r_" + name))

    TE, COPIES = TILES * NE, 2 * TILES
    arena = m.arena
    m.token = arena.take(P, SLOTS + 1, U32, at=0)
    m.dest = arena.take(P, SLOTS + 1, U32)
    m.gain = arena.take(P, SLOTS + 1)
    m.expert = arena.take(P, SLOTS + 1, I32)
    m.b1T = arena.take(P, NE * HT).rearrange("p (e k) -> p e k", e=NE)
    m.routed_end = arena.at

    def te():
        return arena.take(P, TE).rearrange("p (t e) -> p t e", t=TILES)
    logit, prob, cand, place, picked = m.logit, te(), te(), te(), te()
    both = arena.take(P, TE, BF16).rearrange("p (t e) -> p t e", t=TILES)
    hot = [te(), te()]
    def per_tile():
        return arena.take(P, TILES)
    top, total, inv, p1, i1, p2, i2, gap, den = (per_tile() for _ in range(9))
    ones, upper, one = arena.take(P, P, BF16), arena.take(P, P, BF16), arena.take(P, P)
    used, slots, last, start = (arena.take(P, NE) for _ in range(4))
    tokens = arena.take(P, TILES)
    where, slot, lane = (arena.take(P, COPIES).rearrange("p (c t) -> p c t", c=2) for _ in range(3))
    onlane = arena.take(P, COPIES * P, F16).rearrange("p (n j) -> p n j", n=COPIES)
    PARTS = 5
    row = arena.take(P, COPIES * (PARTS - 1), F16).rearrange("p (n v) -> p n v", v=PARTS - 1)
    table = arena.take(P, COPIES * PARTS * SLOTS, F16).rearrange("p (n v s) -> p n v s", n=COPIES, v=PARTS)
    weight, rest = (arena.take(P, COPIES).rearrange("p (c t) -> p c t", c=2) for _ in range(2))
    pad, unpad, offset = arena.take(P, 1), arena.take(P, 1), arena.take(P, SLOTS)
    past = arena.take(P, SLOTS * (NE - 1)).rearrange("p (s e) -> p s e", s=SLOTS)
    expert, gain = arena.take(P, SLOTS), arena.take(P, SLOTS)

    q = {n: sem(n) for n in "const b1T e pe soft split route half onehot idx".split()}

    def over_e(x):
        return x.unsqueeze(2).to_broadcast([P, TILES, NE])

    iota_e = m.iota[:, 0:NE].unsqueeze(1).to_broadcast([P, TILES, NE])

    with nc.Block() as block:
        @block.sync
        def _(sp):
            for e in range(NE):
                sp.dma_start(m.late.tensor[:, e * HT * D:(e + 1) * HT * D].rearrange("p (k d) -> p k d", k=HT),
                             a["L1_ffn_W2"][e].rearrange("(k p) d -> p k d", p=P)).then_inc(m.ld_w2[e], 16)

        @block.gpsimd
        def _(pool):
            pool.memset(ones, 1.0).then_inc(q["const"], 1)
            pool.memset(one, 1.0).then_inc(q["const"], 1)
            pool.wait_ge(q["const"], 2)
            pool.affine_select(out=upper, in_=ones, compare_op=ALU.is_ge, fill=0.0, base=-1,
                               pattern=[[1, P]], channel_multiplier=-1).then_inc(q["const"], 1)
            pool.iota(tokens, [[P, TILES]], base=0, channel_multiplier=1,
                      allow_small_or_imprecise_dtypes=True).then_inc(q["const"], 1)
            pool.iota(pad, [[0, 1]], base=TILES * P, channel_multiplier=1,
                      allow_small_or_imprecise_dtypes=True).then_inc(q["const"], 1)
            pool.iota(unpad, [[0, 1]], base=-TILES * P, channel_multiplier=-1,
                      allow_small_or_imprecise_dtypes=True).then_inc(q["const"], 1)
            pool.wait_ge(q["split"], 6)
            pool.wait_ge(q["onehot"], 1)
            pool.tensor_tensor(table[:, TILES:, 1:PARTS, :],
                               table[:, TILES:, 0:1, :].to_broadcast([P, TILES, PARTS - 1, SLOTS]),
                               row[:, TILES:].unsqueeze(3).to_broadcast([P, TILES, PARTS - 1, SLOTS]), ALU.mult)\
                .then_inc(q["half"], 1)

        @block.scalar
        def _(act):
            act.wait_ge(q["b1T"], 1)
            act.activation(m.b1T.rearrange("p e k -> p (e k)"), m.bank(4)[:, 0, 0:NE * HT], ACT.Copy)\
               .then_inc(q["b1T"], 1)
            act.wait_ge(q["soft"], 2)
            act.activation(prob, prob, ACT.Exp).then_inc(q["e"], 1)
            act.wait_ge(q["soft"], 17)
            act.activation(gap, gap, ACT.Exp).then_inc(q["e"], 1)

        @block.tensor
        def _(pe):
            pe.transpose(m.bank(4)[:, 0, 0:NE * HT], m.b1, m.ident[0:NE * HT, 0:NE * HT]).then_inc(q["b1T"], 1)

            pe.wait_ge(q["const"], 6)
            pe.wait_ge(q["route"], 2)
            pe.matmul(m.bank(5)[:, 0, 0:TE], upper, both.rearrange("p t e -> p (t e)"), start=True, stop=False)
            for t in range(TILES - 1):
                n = TILES - 1 - t
                mm = pe.matmul(m.bank(5)[:, 0, (t + 1) * NE:TE].rearrange("p (t e) -> p t e", e=NE), ones,
                               both[:, t:t + 1, :].to_broadcast([P, n, NE]), start=False, stop=(t == TILES - 2))
            mm.then_inc(q["pe"], 1)
            pe.matmul(m.bank(6)[:, 0, 0:NE], one, used, start=True, stop=True).then_inc(q["pe"], 1)
            pe.wait_ge(q["onehot"], 3)
            for n in range(COPIES):
                if n == TILES:
                    pe.wait_ge(q["half"], 1)
                mm = pe.matmul(m.bank(7)[:, 0, 0:PARTS * SLOTS], onlane[:, n, :],
                               table[:, n, :, :].rearrange("p v s -> p (v s)"),
                               start=(n == 0), stop=(n == COPIES - 1))
            mm.then_inc(q["pe"], 1)

        @block.vector
        def _(dve):
            dve.tensor_reduce(top, logit, AX.X, ALU.max).then_inc(q["soft"], 1)
            dve.wait_ge(q["soft"], 1)
            dve.tensor_tensor(prob, logit, over_e(top), ALU.subtract).then_inc(q["soft"], 1)
            dve.wait_ge(q["e"], 1)
            dve.tensor_reduce(total, prob, AX.X, ALU.add).then_inc(q["soft"], 1)
            dve.wait_ge(q["soft"], 3)
            dve.reciprocal(inv, total).then_inc(q["soft"], 1)
            dve.wait_ge(q["soft"], 4)
            dve.tensor_tensor(prob, prob, over_e(inv), ALU.mult).then_inc(q["soft"], 1)
            dve.wait_ge(q["soft"], 5)
            dve.tensor_reduce(p1, prob, AX.X, ALU.max).then_inc(q["soft"], 1)
            dve.wait_ge(q["soft"], 6)
            dve.tensor_tensor(cand, prob, over_e(p1), ALU.is_lt).then_inc(q["soft"], 1)
            dve.wait_ge(q["soft"], 7)
            dve.scalar_tensor_tensor(cand, cand, 1000.0, iota_e, ALU.mult, ALU.add).then_inc(q["soft"], 1)
            dve.wait_ge(q["soft"], 8)
            dve.tensor_reduce(i1, cand, AX.X, ALU.min).then_inc(q["soft"], 1)
            dve.wait_ge(q["soft"], 9)
            dve.tensor_tensor(hot[0], iota_e, over_e(i1), ALU.is_equal).then_inc(q["soft"], 1)
            dve.wait_ge(q["soft"], 10)
            dve.scalar_tensor_tensor(prob, hot[0], -2.0, prob, ALU.mult, ALU.add).then_inc(q["soft"], 1)
            dve.wait_ge(q["soft"], 11)
            dve.tensor_reduce(p2, prob, AX.X, ALU.max).then_inc(q["soft"], 1)
            dve.wait_ge(q["soft"], 12)
            dve.tensor_tensor(cand, prob, over_e(p2), ALU.is_lt).then_inc(q["soft"], 1)
            dve.wait_ge(q["soft"], 13)
            dve.scalar_tensor_tensor(cand, cand, 1000.0, iota_e, ALU.mult, ALU.add).then_inc(q["soft"], 1)
            dve.wait_ge(q["soft"], 14)
            dve.tensor_reduce(i2, cand, AX.X, ALU.min).then_inc(q["soft"], 1)
            dve.wait_ge(q["soft"], 15)
            dve.tensor_tensor(hot[1], iota_e, over_e(i2), ALU.is_equal).then_inc(q["soft"], 1)
            dve.tensor_tensor(gap, p2, p1, ALU.subtract).then_inc(q["soft"], 1)
            dve.wait_ge(q["soft"], 16)
            dve.tensor_tensor(both, hot[0], hot[1], ALU.add).then_inc(q["route"], 1)
            dve.wait_ge(q["route"], 1)
            dve.tensor_reduce(used, both.rearrange("p t e -> p e t"), AX.X, ALU.add).then_inc(q["route"], 1)
            dve.wait_ge(q["e"], 2)
            dve.tensor_scalar(den, gap, 1.0, None, ALU.add).then_inc(q["soft"], 1)
            dve.wait_ge(q["soft"], 18)
            dve.reciprocal(weight[:, 0, :], den).then_inc(q["soft"], 1)
            dve.wait_ge(q["soft"], 19)
            dve.tensor_tensor(weight[:, 1, :], gap, weight[:, 0, :], ALU.mult).then_inc(q["soft"], 1)
            dve.wait_ge(q["soft"], 20)
            dve.tensor_scalar(weight, weight, m.tanh[:, 3:4], None, ALU.mult).then_inc(q["soft"], 1)
            parts = row.rearrange("p (c t) v -> p v c t", c=2)
            dve.wait_ge(q["soft"], 21)
            dve.tensor_copy(parts[:, 1], weight).then_inc(q["split"], 1)
            dve.wait_ge(q["split"], 1)
            dve.tensor_tensor(rest, weight, parts[:, 1], ALU.subtract).then_inc(q["split"], 1)
            dve.wait_ge(q["split"], 2)
            dve.tensor_scalar(parts[:, 2], rest, 2048.0, None, ALU.mult).then_inc(q["split"], 1)
            dve.wait_ge(q["split"], 3)
            dve.scalar_tensor_tensor(rest, rest, 2048.0, parts[:, 2], ALU.mult, ALU.subtract).then_inc(q["split"], 1)
            dve.wait_ge(q["split"], 4)
            dve.tensor_scalar(parts[:, 3], rest, 2048.0, None, ALU.mult).then_inc(q["split"], 1)
            dve.wait_ge(q["const"], 6)
            dve.tensor_copy(parts[:, 0], tokens.unsqueeze(1).to_broadcast([P, 2, TILES])).then_inc(q["split"], 1)
            dve.wait_ge(q["pe"], 2)
            dve.tensor_scalar(slots, m.bank(6)[:, 0, 0:NE], 1.0 / P, (P - 1.0) / P - 0.5 + 0.5 / P, ALU.mult,
                              ALU.add).then_inc(q["route"], 1)
            dve.wait_ge(q["route"], 3)
            dve.tensor_scalar(slots, slots, MAGIC, None, ALU.add).then_inc(q["route"], 1)
            dve.wait_ge(q["route"], 4)
            dve.tensor_scalar(slots, slots, MAGIC, 1.0, ALU.subtract, ALU.max).then_inc(q["route"], 1)
            dve.wait_ge(q["route"], 5)
            dve.wait_ge(q["const"], 2)
            dve.tensor_tensor_scan(last, one[:, 0:NE], slots, 0.0, ALU.mult, ALU.add).then_inc(q["route"], 1)
            dve.wait_ge(q["route"], 6)
            dve.tensor_tensor(start, last, slots, ALU.subtract).then_inc(q["route"], 1)
            dve.wait_ge(q["route"], 7)
            dve.scalar_tensor_tensor(place, start.unsqueeze(1).to_broadcast([P, TILES, NE]), float(P),
                                     m.bank(5)[:, 0, 0:TE].rearrange("p (t e) -> p t e", t=TILES),
                                     ALU.mult, ALU.add).then_inc(q["route"], 1)
            dve.wait_ge(q["route"], 8)
            for c in range(2):
                dve.tensor_tensor(picked, place, hot[c], ALU.mult).then_inc(q["route"], 1)
                dve.wait_ge(q["route"], 9 + 2 * c)
                dve.tensor_reduce(where[:, c, :], picked, AX.X, ALU.add).then_inc(q["route"], 1)
                dve.wait_ge(q["route"], 10 + 2 * c)
            dve.tensor_scalar(slot, where, 1.0 / P, -0.5 + 0.5 / P, ALU.mult, ALU.add).then_inc(q["route"], 1)
            dve.wait_ge(q["route"], 13)
            dve.tensor_scalar(slot, slot, MAGIC, None, ALU.add).then_inc(q["route"], 1)
            dve.wait_ge(q["route"], 14)
            dve.tensor_scalar(slot, slot, MAGIC, None, ALU.subtract).then_inc(q["route"], 1)
            dve.wait_ge(q["route"], 15)
            dve.scalar_tensor_tensor(lane, slot, -float(P), where, ALU.mult, ALU.add).then_inc(q["route"], 1)
            dve.wait_ge(q["route"], 16)
            dve.tensor_tensor(table[:, :, 0, :], m.iota[:, 0:SLOTS].unsqueeze(1).to_broadcast([P, COPIES, SLOTS]),
                              slot.rearrange("p c t -> p (c t)").unsqueeze(2).to_broadcast([P, COPIES, SLOTS]),
                              ALU.is_equal).then_inc(q["onehot"], 1)
            dve.wait_ge(q["split"], 6)
            dve.wait_ge(q["onehot"], 1)
            dve.tensor_tensor(table[:, 0:TILES, 1:PARTS, :],
                              table[:, 0:TILES, 0:1, :].to_broadcast([P, TILES, PARTS - 1, SLOTS]),
                              row[:, 0:TILES].unsqueeze(3).to_broadcast([P, TILES, PARTS - 1, SLOTS]), ALU.mult)\
               .then_inc(q["onehot"], 1)
            dve.tensor_tensor(onlane, m.iota[:, 0:P].unsqueeze(1).to_broadcast([P, COPIES, P]),
                              lane.rearrange("p c t -> p (c t)").unsqueeze(2).to_broadcast([P, COPIES, P]),
                              ALU.is_equal).then_inc(q["onehot"], 1)
            dve.tensor_tensor(past, m.iota[:, 0:SLOTS].unsqueeze(2).to_broadcast([P, SLOTS, NE - 1]),
                              last[:, 0:NE - 1].unsqueeze(1).to_broadcast([P, SLOTS, NE - 1]), ALU.is_ge)\
               .then_inc(q["route"], 1)
            dve.wait_ge(q["route"], 17)
            dve.tensor_reduce(expert, past, AX.X, ALU.add).then_inc(q["route"], 1)
            dve.wait_ge(q["route"], 18)
            dve.tensor_copy(m.expert[:, 0:SLOTS], expert).then_inc(q["idx"], 1)
            dve.wait_ge(q["pe"], 3)
            cell = m.bank(7)[:, 0, 0:PARTS * SLOTS].rearrange("p (v s) -> p v s", v=PARTS)
            dve.tensor_copy(m.token[:, 0:SLOTS], cell[:, 1]).then_inc(q["idx"], 1)
            dve.tensor_scalar(offset, cell[:, 0], unpad, pad, ALU.mult, ALU.add).then_inc(q["idx"], 1)
            dve.tensor_copy(gain, cell[:, 4]).then_inc(q["idx"], 1)
            dve.wait_ge(q["idx"], 4)
            dve.tensor_tensor(m.dest[:, 0:SLOTS], cell[:, 1], offset, ALU.add).then_inc(q["idx"], 1)
            dve.scalar_tensor_tensor(gain, gain, 2.0 ** -11, cell[:, 3], ALU.mult, ALU.add).then_inc(q["idx"], 1)
            dve.wait_ge(q["idx"], 6)
            dve.scalar_tensor_tensor(m.gain[:, 0:SLOTS], gain, 2.0 ** -11, cell[:, 2], ALU.mult, ALU.add)\
               .then_inc(q["idx"], 1)
            dve.wait_ge(q["idx"], 7)


def experts(nc, ctx, m, a):
    def sem(name):
        return ctx.enter_context(nc.semaphore("e_" + name))

    arena = m.arena
    arena.at = m.routed_end
    def pair(cols, dtype=F32):
        return [arena.take(P, cols, dtype) for _ in range(2)]
    col, dest, xs, result = pair(1, U32), pair(1, U32), pair(D), pair(D)
    xT, h, hT = arena.take(P, D), arena.take(P, HID), arena.take(P, HT * P)
    w1 = m.early.tensor[:, :].rearrange("p (e k h) -> p e k h", e=NE, k=KD)
    w2 = m.late.tensor[:, :].rearrange("p (e k d) -> p e k d", e=NE, k=HT)

    q = {n: sem(n) for n in "col dest xT xTc H h T b hT Y biased res".split()}
    ld = [sem(f"ld_rows{p}") for p in range(2)]
    added = [sem(f"added{p}") for p in range(2)]
    s_out = sem("st_out")

    h_ps = m.bank(1, 2)
    t_ps = m.bank(3, 2).rearrange("p n (k j) -> p (n k) j", j=P)

    def expert_of(eng, s):
        return eng.value_load(m.expert[0:1, bass.ds(s, 1)], min_val=0, max_val=NE - 1)

    with nc.Block() as block:
        @block.sync
        def _(sp):
            sp.wait_ge(added[0], 16 * ((SLOTS + 1) // 2))
            sp.wait_ge(added[1], 16 * (SLOTS // 2))
            out = a["out"].rearrange("b j d -> (b j) d")
            for n in range(4):
                rows = slice(n * B * TQ // 4, (n + 1) * B * TQ // 4)
                sp.dma_start(out[rows, :], m.sum_dram[rows, :]).then_inc(s_out, 16)
            sp.wait_ge(s_out, 16 * 4)

        @block.gpsimd
        def _(pool):
            wait = Waits(pool, sem("tick_pool"))

            def fetch(s, p):
                wait(q["xT"], s - 1, alone=True)
                pool.tensor_copy(col[p], m.token[:, bass.ds(s, 1)]).then_inc(q["col"], 1)
                wait(q["col"], s + 1, alone=True)
                pool.indirect_dma_start(xs[p], None, m.y_dram, bass.IndirectOffsetOnAxis(ap=col[p], axis=0))\
                    .then_inc(ld[p], 16)

            def add(s, p):
                wait(q["res"], s + 1, alone=True)
                wait(added[1 - p], s * 8 + p * 8, alone=True)
                pool.tensor_copy(dest[p], m.dest[:, bass.ds(s, 1)]).then_inc(q["dest"], 1)
                wait(q["dest"], s + 1, alone=True)
                pool.indirect_dma_start(m.sum_dram, bass.IndirectOffsetOnAxis(ap=dest[p], axis=0), result[p], None,
                                        compute_op=ALU.add).then_inc(added[p], 16)

            pipeline(pool, [(fetch, 0), (add, 4)], SLOTS, 6)

        @block.scalar
        def _(act):
            wait = Waits(act, sem("tick_act"))

            def copy_x(s, p):
                wait(q["xT"], s + 1)
                wait(q["H"], s)
                act.activation(xT, m.bank(0)[:, 0, 0:D], ACT.Copy).then_inc(q["xTc"], 1)

            def copy_h(s, p):
                wait(q["H"], s + 1)
                wait(q["T"], s)
                act.activation(h.rearrange("p (n j) -> p n j", n=2), h_ps, ACT.Copy).then_inc(q["h"], 1)

            pipeline(act, [(copy_h, 3), (copy_x, 2)], SLOTS, 6)

        @block.tensor
        def _(pe):
            wait = Waits(pe, sem("tick_pe"))
            pe.wait_ge(m.ld_w1, 16)
            of = {}

            def load(s, p):
                of[1] = expert_of(pe, s)

            def load2(s, p):
                of[2] = expert_of(pe, s)

            def turn_x(s, p):
                wait(ld[p], s * 8 - p * 8 + 16)
                wait(q["xTc"], s)
                for k in range(KD):
                    mm = pe.transpose(m.bank(0)[:, 0, k * P:(k + 1) * P], xs[p][:, k * P:(k + 1) * P], m.ident)
                mm.then_inc(q["xT"], 1)

            def turn_h(s, p):
                wait(q["h"], s + 1)
                wait(q["b"], s)
                for k in range(HT):
                    mm = pe.transpose(t_ps[:, k, :], h[:, k * P:(k + 1) * P], m.ident)
                mm.then_inc(q["T"], 1)

            def layer1(s, p):
                wait(q["xTc"], s + 1)
                wait(q["h"], s)
                for n in range(2):
                    for k in range(KD):
                        mm = pe.matmul(h_ps[:, n, :], xT[:, k * P:(k + 1) * P],
                                       w1[:, bass.ds(of[1], 1), k, n * 512:(n + 1) * 512]
                                       .rearrange("p e h -> p (e h)"), start=(k == 0), stop=(k == KD - 1))
                mm.then_inc(q["H"], 1)

            def layer2(s, p):
                if isinstance(s, int) and s < NE:
                    wait(m.ld_w2[s], 16)
                wait(q["hT"], s + 1)
                wait(q["biased"], s)
                for k in range(HT):
                    mm = pe.matmul(m.bank(5)[:, 0, 0:D], hT[:, k * P:(k + 1) * P],
                                   w2[:, bass.ds(of[2], 1), k, :].rearrange("p e d -> p (e d)"),
                                   start=(k == 0), stop=(k == HT - 1))
                mm.then_inc(q["Y"], 1)

            pipeline(pe, [(load, 2), (load2, 3), (turn_x, 2), (turn_h, 3), (layer1, 2), (layer2, 3)],
                     SLOTS, NE + 4)

        @block.vector
        def _(dve):
            wait = Waits(dve, sem("tick_dve"))
            of = {}

            def load(s, p):
                of[0] = expert_of(dve, s)

            def bias(s, p):
                wait(q["T"], s + 1)
                wait(q["Y"], s)
                b1 = m.b1T[:, bass.ds(of[0], 1), :].rearrange("p e k -> p (e k)").unsqueeze(2)
                dve.tensor_tensor(hT.rearrange("p (k j) -> p k j", k=HT), t_ps, b1.to_broadcast([P, HT, P]),
                                  ALU.add).then_inc(q["b"], 1)
                wait(q["b"], s + 1)
                dve.tensor_scalar(hT, hT, 0.0, None, ALU.max).then_inc(q["hT"], 1)

            def keep(s, p):
                wait(q["Y"], s + 1)
                wait(added[p], s * 8 - p * 8)
                dve.tensor_tensor(result[p], m.bank(5)[:, 0, 0:D],
                                  m.b2[:, bass.ds(of[0], 1), :].rearrange("p e d -> p (e d)"), ALU.add)\
                   .then_inc(q["biased"], 1)
                wait(q["biased"], s + 1)
                dve.tensor_scalar(result[p], result[p], m.gain[:, bass.ds(s, 1)], None, ALU.mult)\
                   .then_inc(q["res"], 1)

            pipeline(dve, [(load, 3), (bias, 3), (keep, 3)], SLOTS, 6)


def build(nc, a):
    with ExitStack() as ctx:
        m = Memory()
        allocate(nc, ctx, m)
        m.ld_attn = ctx.enter_context(nc.semaphore("ld_attn"))
        m.ld_w1 = ctx.enter_context(nc.semaphore("ld_w1"))
        m.ld_w2 = [ctx.enter_context(nc.semaphore(f"ld_w2_{e}")) for e in range(NE)]
        before = nc.snapshot_sems()
        align(nc, ctx, m, a)
        ffn(nc, ctx, m, a)
        nc.clear_and_free_semaphores(nc.allocated_since(before))
        nc.all_engine_barrier()
        attention(nc, ctx, m, a)
        route(nc, ctx, m, a)
        experts(nc, ctx, m, a)


_INS = ["x", "ctx_1024", "g_xattn", "g_ffn", "L0_ffn_ln1_g", "L0_ffn_ln1_b", "L0_ffn_w1", "L0_ffn_b1",
        "L0_ffn_ln2_g", "L0_ffn_ln2_b", "L0_ffn_w2", "L0_ffn_b2", "L1_xattn_tab_g", "L1_xattn_tab_b",
        "L1_xattn_vid_g", "L1_xattn_vid_b", "L1_xattn_Wq", "L1_xattn_Wk", "L1_xattn_Wv", "L1_xattn_q_g",
        "L1_xattn_q_b", "L1_xattn_k_g", "L1_xattn_k_b", "L1_xattn_Wo", "L1_xattn_bo", "L1_ffn_W1", "L1_ffn_b1",
        "L1_ffn_W2", "L1_ffn_b2", "L1_ffn_Wg", "L1_ffn_bg"]


def kernel(**inputs):
    import numpy as np
    import concourse.bacc as bacc
    from concourse.bass_utils import run_bass_kernel_spmd

    nc = bacc.Bacc("TRN2", target_bir_lowering=False, num_devices=1)
    arrays, a = {}, {}
    for name in _INS:
        array = np.ascontiguousarray(inputs[name])
        arrays[f"in_{name}_dram"] = array
        a[name] = nc.dram_tensor(f"in_{name}_dram", array.shape, mybir.dt.from_np(array.dtype),
                                 kind="ExternalInput").ap()
    a["out"] = nc.dram_tensor("out_dram", [B, TQ, D], F32, kind="ExternalOutput").ap()
    build(nc, a)
    r = run_bass_kernel_spmd(nc, [arrays], core_ids=[0])
    return r.results[0]["out_dram"]
```
